# Optimizing a Trainium2 kernel written in Bass

```python
import numpy as np
import jax
import jax.numpy as jnp

def _softmax(x, axis=-1):
    return jax.nn.softmax(x, axis=axis)

def _gelu(x):
    return jax.nn.gelu(x, approximate=True)

def _silu(x):
    return jax.nn.silu(x)

def _sigmoid(x):
    return jax.nn.sigmoid(x)

def _layernorm(x, axis=-1, eps=1e-05):
    m = jnp.mean(x, axis=axis, keepdims=True)
    v = jnp.var(x, axis=axis, keepdims=True)
    return (x - m) / jnp.sqrt(v + eps)

def _scatter_add(tgt, idx, src, axis=0):
    return tgt.at[idx].add(src)

def _segment_sum(src, seg, n):
    return jax.ops.segment_sum(src, seg, n)
kernel_name = 'mk_cond_resid_d4_seqx_r4_7e6555'

def setup_inputs(seed: int=0):
    np.random.seed(seed)
    _w = jnp.asarray

    def _rec_inputs():
        import jax
        import jax.numpy as jnp
        _rk = jax.random.key(seed)
        x = -0.0003929 + 0.9999 * jax.random.normal(jax.random.fold_in(_rk, 1), (64, 64, 256), jnp.float32)
        _lenS = 64 - jax.random.randint(jax.random.fold_in(_rk, 7), (64,), 0, max(1, 64 // 4) + 1, jnp.int32)
        _lenS2 = 64 - jax.random.randint(jax.random.fold_in(_rk, 8), (64,), 0, max(1, 64 // 4) + 1, jnp.int32)
        cond_1024 = 0.00061147 + 0.102565 * jax.random.normal(jax.random.fold_in(_rk, 11), (64, 256), jnp.float32)
        return (x, cond_1024)
    x, cond_1024 = _rec_inputs()

    def _L0_cond_setup():
        import jax, jax.numpy as jnp
        import numpy as np
        key = jax.random.key(seed)
        ks = jax.random.split(key, 8)
        B, L, D, N, K = (4, 1024, 256, 64, 4)
        return {'x': jax.random.normal(ks[0], (B, L, D), dtype=jnp.float32), 'conv_w': jax.random.normal(ks[1], (K, 1, D), dtype=jnp.float32) * 0.1, 'conv_b': jnp.zeros((D,), dtype=jnp.float32), 'Wp': jax.random.normal(ks[2], (D, 2 * N), dtype=jnp.float32) * (1.0 / np.sqrt(D)), 'bp': jnp.zeros((2 * N,), dtype=jnp.float32), 'Ws': jax.random.normal(ks[3], (D, N), dtype=jnp.float32) * (1.0 / np.sqrt(D)), 'bs': jnp.zeros((N,), dtype=jnp.float32), 'A_log': jax.random.normal(ks[4], (N,), dtype=jnp.float32) * 0.02, 'dt_log': jax.random.normal(ks[5], (N,), dtype=jnp.float32) * 0.02, 'Wo': jax.random.normal(ks[6], (N, D), dtype=jnp.float32) * (1.0 / np.sqrt(N)), 'bo': jnp.zeros((D,), dtype=jnp.float32)}
    _L0_cond_all = _L0_cond_setup()
    _L0_cond_in = {k: v for k, v in _L0_cond_all.items() if k in ('conv_b', 'Wp', 'bp', 'Ws', 'bs', 'A_log', 'dt_log', 'Wo', 'bo')}
    del _L0_cond_all

    def _L1_cond_setup():
        import jax, jax.numpy as jnp
        import numpy as np
        EPS = 1e-08
        key = jax.random.key(seed)
        ks = jax.random.split(key, 8)
        B, S, D, H = (8, 512, 256, 256)
        scale = 1.0 / np.sqrt(D)
        return {'input_seq': jax.random.normal(ks[0], (B, S, D), dtype=jnp.float32), 'initial_hidden': jax.random.normal(ks[1], (B, H), dtype=jnp.float32), 'W_f': jax.random.normal(ks[2], (H, D), dtype=jnp.float32) * scale, 'b_f': jnp.zeros((H,), dtype=jnp.float32), 'W_i': jax.random.normal(ks[3], (H, D), dtype=jnp.float32) * scale, 'b_i': jnp.zeros((H,), dtype=jnp.float32), 'W_h': jax.random.normal(ks[4], (H, D), dtype=jnp.float32) * scale, 'b_h': jnp.zeros((H,), dtype=jnp.float32)}
    _L1_cond_all = _L1_cond_setup()
    _L1_cond_in = {k: v for k, v in _L1_cond_all.items() if k in ('W_f', 'b_f', 'W_i', 'b_i', 'W_h', 'b_h')}
    del _L1_cond_all

    def _L2_cond_setup():
        import jax, jax.numpy as jnp
        import numpy as np
        D_MODEL = 256
        D_FF = 1024
        N_EXPERTS = 8
        TOP_K = 2
        N_SHARED = 2
        B, T = (4, 512)
        key = jax.random.key(seed)
        ks = jax.random.split(key, 9)
        Hs = D_FF // 2
        Hr = D_FF // 4
        inp = {'x': jax.random.normal(ks[0], (B, T, D_MODEL), dtype=jnp.float32), 't_emb': jax.random.normal(ks[1], (B, D_MODEL), dtype=jnp.float32), 'W_router': 0.01 * jax.random.normal(ks[2], (N_EXPERTS, 2 * D_MODEL), dtype=jnp.float32), 'router_bias': jnp.zeros((N_EXPERTS,), dtype=jnp.float32), 's_w1': 0.02 * jax.random.normal(ks[3], (N_SHARED, Hs, D_MODEL), dtype=jnp.float32), 's_w3': 0.02 * jax.random.normal(ks[4], (N_SHARED, Hs, D_MODEL), dtype=jnp.float32), 's_w2': 0.02 * jax.random.normal(ks[5], (N_SHARED, D_MODEL, Hs), dtype=jnp.float32), 'r_w1': 0.02 * jax.random.normal(ks[6], (N_EXPERTS, Hr, D_MODEL), dtype=jnp.float32), 'r_w2': 0.02 * jax.random.normal(ks[7], (N_EXPERTS, D_MODEL, Hr), dtype=jnp.float32)}
        return inp
    _L2_cond_all = _L2_cond_setup()
    _L2_cond_in = {k: v for k, v in _L2_cond_all.items() if k in ('W_router', 'router_bias', 's_w1', 's_w3', 's_w2', 'r_w1', 'r_w2')}
    del _L2_cond_all

    def _L3_cond_setup():
        import jax, jax.numpy as jnp
        import numpy as np
        LATENT = 256
        key = jax.random.key(seed)
        k1, k2, k3, k4 = jax.random.split(key, 4)
        B, T, D = (64, 128, LATENT)
        h_t = jax.random.normal(k1, (B, D), dtype=jnp.float32)
        z = jax.random.normal(k2, (B, T, D), dtype=jnp.float32)
        bound = 1.0 / np.sqrt(2 * D)
        W = jax.random.uniform(k3, (D, 2 * D), minval=-bound, maxval=bound, dtype=jnp.float32)
        b = jax.random.uniform(k4, (D,), minval=-bound, maxval=bound, dtype=jnp.float32)
        alpha = jnp.full((D,), 0.1, dtype=jnp.float32)
        return {'h_t': h_t, 'z': z, 'W': W, 'b': b, 'alpha': alpha}
    _L3_cond_all = _L3_cond_setup()
    _L3_cond_in = {k: v for k, v in _L3_cond_all.items() if k in ('W', 'b', 'alpha')}
    del _L3_cond_all
    return {'x': x, 'cond_1024': cond_1024, 'L0_cond_conv_b': _L0_cond_in['conv_b'], 'L0_cond_Wp': _L0_cond_in['Wp'], 'L0_cond_bp': _L0_cond_in['bp'], 'L0_cond_Ws': _L0_cond_in['Ws'], 'L0_cond_bs': _L0_cond_in['bs'], 'L0_cond_A_log': _L0_cond_in['A_log'], 'L0_cond_dt_log': _L0_cond_in['dt_log'], 'L0_cond_Wo': _L0_cond_in['Wo'], 'L0_cond_bo': _L0_cond_in['bo'], 'L1_cond_W_f': _L1_cond_in['W_f'], 'L1_cond_b_f': _L1_cond_in['b_f'], 'L1_cond_W_i': _L1_cond_in['W_i'], 'L1_cond_b_i': _L1_cond_in['b_i'], 'L1_cond_W_h': _L1_cond_in['W_h'], 'L1_cond_b_h': _L1_cond_in['b_h'], 'L2_cond_W_router': _L2_cond_in['W_router'], 'L2_cond_router_bias': _L2_cond_in['router_bias'], 'L2_cond_s_w1': _L2_cond_in['s_w1'], 'L2_cond_s_w3': _L2_cond_in['s_w3'], 'L2_cond_s_w2': _L2_cond_in['s_w2'], 'L2_cond_r_w1': _L2_cond_in['r_w1'], 'L2_cond_r_w2': _L2_cond_in['r_w2'], 'L3_cond_W': _L3_cond_in['W'], 'L3_cond_b': _L3_cond_in['b'], 'L3_cond_alpha': _L3_cond_in['alpha']}

def reference(x, cond_1024, L0_cond_conv_b, L0_cond_Wp, L0_cond_bp, L0_cond_Ws, L0_cond_bs, L0_cond_A_log, L0_cond_dt_log, L0_cond_Wo, L0_cond_bo, L1_cond_W_f, L1_cond_b_f, L1_cond_W_i, L1_cond_b_i, L1_cond_W_h, L1_cond_b_h, L2_cond_W_router, L2_cond_router_bias, L2_cond_s_w1, L2_cond_s_w3, L2_cond_s_w2, L2_cond_r_w1, L2_cond_r_w2, L3_cond_W, L3_cond_b, L3_cond_alpha):
    import jax
    import jax.numpy as jnp

    def _L0_cond_ref(x, conv_w, conv_b, Wp, bp, Ws, bs, A_log, dt_log, Wo, bo):
        import jax, jax.numpy as jnp
        import numpy as np
        B, L, D = x.shape
        K = conv_w.shape[0]
        N = Ws.shape[1]
        x_pad = jnp.pad(x, ((0, 0), (K - 1, 0), (0, 0)))
        conv = conv_b + sum((x_pad[:, k:k + L, :] * conv_w[k, 0] for k in range(K)))
        proj = conv @ Wp + bp
        B_t = jax.nn.softplus(proj[..., :N])
        C_t = jnp.tanh(proj[..., N:])
        u = x @ Ws + bs
        A = -jax.nn.softplus(A_log)
        dt = jax.nn.softplus(dt_log)
        decay = 1.0 + dt * A

        def step(state, inputs):
            u_t, b_t, c_t = inputs
            state = decay * state + dt * b_t * u_t
            return (state, c_t * state)
        init = jnp.zeros((B, N), dtype=x.dtype)
        xs = tuple((jnp.swapaxes(a, 0, 1) for a in (u, B_t, C_t)))
        _, ys = jax.lax.scan(step, init, xs, unroll=4)
        y = jnp.swapaxes(ys, 0, 1)
        return y @ Wo + bo

    def _L1_cond_ref(input_seq, initial_hidden, W_f, b_f, W_i, b_i, W_h, b_h):
        import jax, jax.numpy as jnp
        import numpy as np
        EPS = 1e-08
        forget_gate = jax.nn.sigmoid(jnp.einsum('bsd,hd->bsh', input_seq, W_f) + b_f)
        input_gate = jax.nn.sigmoid(jnp.einsum('bsd,hd->bsh', input_seq, W_i) + b_i)
        gate_sum = forget_gate + input_gate + EPS
        forget_norm = forget_gate / gate_sum
        input_norm = input_gate / gate_sum
        candidate = jnp.einsum('bsd,hd->bsh', input_seq, W_h) + b_h
        new_info = input_norm * candidate
        log_ret = jnp.log(forget_norm + EPS)
        log_cumprod = jnp.cumsum(log_ret, axis=1)
        B, _, H = log_cumprod.shape
        padded = jnp.concatenate([jnp.zeros((B, 1, H), dtype=log_cumprod.dtype), log_cumprod], axis=1)
        scaling = jnp.exp(log_cumprod[:, -1:, :] - padded[:, :-1, :])
        hidden = jnp.cumsum(scaling * new_info, axis=1)
        hidden = hidden + jnp.exp(log_cumprod) * initial_hidden[:, None, :]
        return hidden

    def _L2_cond_ref(x, t_emb, W_router, router_bias, s_w1, s_w3, s_w2, r_w1, r_w2):
        import jax, jax.numpy as jnp
        import numpy as np
        D_MODEL = 256
        D_FF = 1024
        N_EXPERTS = 8
        TOP_K = 2
        N_SHARED = 2
        B, T = (4, 512)
        Bn, Tn, C = x.shape
        N = Bn * Tn
        x_flat = x.reshape(N, C)
        t_flat = jnp.broadcast_to(t_emb[:, None, :], (Bn, Tn, C)).reshape(N, C)
        shared_out = jnp.zeros_like(x_flat)
        for e in range(N_SHARED):
            h = jax.nn.silu(x_flat @ s_w1[e].T) * (x_flat @ s_w3[e].T)
            shared_out = shared_out + h @ s_w2[e].T
        shared_out = shared_out / N_SHARED
        router_in = jnp.concatenate([x_flat, t_flat], axis=-1)
        s = jax.nn.sigmoid((router_in @ W_router.T).astype(jnp.float32))
        sel_scores = s + router_bias
        _, topk_idx = jax.lax.top_k(sel_scores, TOP_K)
        s_sel = jnp.take_along_axis(s, topk_idx, axis=1)
        denom = jnp.sum(s_sel, axis=1, keepdims=True)
        gates = jnp.where(denom > 1e-09, s_sel / (denom + 1e-09), 1.0 / TOP_K).astype(x.dtype)
        gates_full = jnp.sum(jax.nn.one_hot(topk_idx, N_EXPERTS, dtype=x.dtype) * gates[..., None], axis=1)
        routed_out = jnp.zeros_like(x_flat)
        for e in range(N_EXPERTS):
            h = jax.nn.gelu(x_flat @ r_w1[e].T, approximate=False)
            routed_out = routed_out + h @ r_w2[e].T * gates_full[:, e:e + 1]
        out = (shared_out + routed_out) / (N_SHARED + TOP_K)
        return out.reshape(Bn, Tn, C)

    def _L3_cond_ref(h_t, z, W, b, alpha):
        import jax, jax.numpy as jnp
        import numpy as np
        LATENT = 256
        D = h_t.shape[-1]
        Wh = W[:, :D]
        Wz = W[:, D:]
        leak = 1.0 - alpha

        def step(h, z_t):
            gate = jax.nn.sigmoid(h @ Wh.T + z_t @ Wz.T + b)
            h_new = jnp.tanh(h * leak + gate * z_t)
            return (h_new, h_new)
        _, hs = jax.lax.scan(step, h_t, jnp.swapaxes(z, 0, 1))
        return jnp.swapaxes(hs, 0, 1)
    x = x + _L0_cond_ref(x, cond_1024[:, None, :], L0_cond_conv_b, L0_cond_Wp, L0_cond_bp, L0_cond_Ws, L0_cond_bs, L0_cond_A_log, L0_cond_dt_log, L0_cond_Wo, L0_cond_bo)
    x = x + _L1_cond_ref(x, cond_1024, L1_cond_W_f, L1_cond_b_f, L1_cond_W_i, L1_cond_b_i, L1_cond_W_h, L1_cond_b_h)
    x = x + _L2_cond_ref(x, cond_1024, L2_cond_W_router, L2_cond_router_bias, L2_cond_s_w1, L2_cond_s_w3, L2_cond_s_w2, L2_cond_r_w1, L2_cond_r_w2)
    x = x + _L3_cond_ref(cond_1024, x, L3_cond_W, L3_cond_b, L3_cond_alpha)
    return x

_drawn_inputs = setup_inputs


def setup_inputs(seed=0):
    import zlib

    import numpy as np

    out = dict(_drawn_inputs(seed))
    spreads = {'L0_cond_conv_b': (0.0, 0.1),
     'L0_cond_bp': (0.0, 0.1),
     'L0_cond_bs': (0.0, 0.1),
     'L0_cond_bo': (0.0, 0.1),
     'L1_cond_b_f': (0.0, 2.0),
     'L1_cond_b_i': (0.0, 2.0),
     'L1_cond_b_h': (0.0, 0.8),
     'L2_cond_router_bias': (0.0, 0.733),
     'L3_cond_alpha': (0.10000000149011612, 0.6)}
    factors = {'L0_cond_A_log': 8.0,
     'L0_cond_dt_log': 8.0,
     'L1_cond_W_f': 5.006,
     'L1_cond_W_i': 4.931,
     'L2_cond_W_router': 8.0,
     'L2_cond_s_w1': 8.0,
     'L2_cond_s_w3': 8.0,
     'L2_cond_s_w2': 8.0,
     'L2_cond_r_w1': 5.792,
     'L2_cond_r_w2': 5.452,
     'L3_cond_b': 44.252}
    for name, (base, spread) in spreads.items():
        noise = np.random.default_rng([zlib.crc32(name.encode()), seed]).standard_normal(out[name].shape)
        drawn = base * np.exp(spread * noise) if base else spread * noise
        out[name] = jnp.asarray(drawn.astype(out[name].dtype))
    for name, factor in factors.items():
        out[name] = (out[name] * factor).astype(out[name].dtype)
    return out
```

```python
import concourse.bass as bass
from concourse import mybir
from contextlib import ExitStack

B, L, D, N = 64, 64, 256, 64
TOK = B * L
P = 128
DH = D // P
HALF = B // 2
TILE = 512
NT = TOK // TILE
TB = TILE // L
NE = 8
HS, HR = 512, 256
NSH = 2
SHC = NSH * HS // P
RC = NE * HR // P
CH = SHC + RC
GRP = 2 * SHC + RC
FT = 256
FB = FT // L
NF = TOK // FT
LAG = 2
EPS = 1e-8
NQ = 4


def layered_blocks_kernel(nc, x, cond, conv_b, Wp, bp, Ws, bs, A_log, dt_log, Wo, bo,
                          W_f, b_f, W_i, b_i, W_h, b_h, W_router, router_bias,
                          s_w1, s_w3, s_w2, r_w1, r_w2, W3, b3, alpha, out):
    f32, f32r, bf16 = mybir.dt.float32, mybir.dt.float32r, mybir.dt.bfloat16
    ALU, ACT, AX = mybir.AluOpType, mybir.ActivationFunctionType, mybir.AxisListType

    padded = nc.dram_tensor("cond_padded", (2 * L, D), f32, kind="Internal").ap()

    ctx = ExitStack()
    with ctx:
        def sb(name, shape, dt=f32, where=ctx):
            return where.enter_context(nc.sbuf_tensor(name, shape, dt))

        def sem(name):
            return ctx.enter_context(nc.semaphore(name))

        xT = sb("xT", [P, DH, TOK])
        with ExitStack() as o:
            Xs = sb("Xs", [P, B, P], where=o)
        with ExitStack() as o:
            convT = sb("convT", [P, DH, TOK], where=o)
        u_ctx = ExitStack()
        with u_ctx as o:
            with ExitStack() as o1:
                x1h = sb("x1h", [P, DH, FT], f32r, o1)
                x1l = sb("x1l", [P, DH, FT], f32r, o1)
                fgt = sb("fgt", [P, DH, FT], f32, o1)
                inp = sb("inp", [P, DH, FT], f32, o1)
                cnd = sb("cnd", [P, DH, FT], f32, o1)
                gsum = sb("gsum", [P, DH, FT], f32, o1)
                rcp = sb("rcp", [P, DH, FT], f32, o1)
            with ExitStack() as o2:
                z4 = sb("z4", [P, DH, NQ, B], f32, o2)
                z4h = sb("z4h", [P, DH, NQ, B], f32r, o2)
                z4l = sb("z4l", [P, DH, NQ, B], f32r, o2)
                o4 = sb("o4", [P, DH, NQ, B], f32, o2)
                ost = sb("ost", [P, 2, D], f32, o2)
                th = sb("th", [P, DH, B], f32, o2)
                uz = sb("uz", [P, DH, B], f32, o2)
                hl = sb("hl", [P, DH, B], f32, o2)
                hid = sb("hid", [P, DH, B], f32, o2)
            keep = sb("u_l1_place", [P, 7 * DH * FT], f32, o)
            act_g = sb("act_g", [P, 2, TILE], f32, o)
            hbuf = sb("hbuf", [P, 2, TILE], f32, o)
            hh = sb("hh", [P, LAG, TILE], f32r, o)
            hlo = sb("hlo", [P, LAG, TILE], f32r, o)
        place = sb("u_place", [P, B * P])
        with ExitStack() as o:
            Tz = sb("Tz", [P, L, P], f32, o)
            convS = sb("convS", [P, P, B], f32, o)
        with ExitStack() as o:
            o.enter_context(nc.sbuf_tensor("tz_place", [P, L * P], f32))
            sel = sb("sel", [B, (NT // 2 + 1) * TILE], f32, o)
            rows = sb("rows", [19, P], f32, o)
            condN = sb("condN", [B, D], f32, o)
            wrN = sb("wrN", [NE, 2 * D], f32, o)
            zrow = sb("zrow", [L, D], f32, o)
        w13h = sb("w13h", [P, DH, 2 * NSH * HS], f32r)
        w13l = sb("w13l", [P, DH, 2 * NSH * HS], f32r)
        rw1h = sb("rw1h", [P, DH, NE * HR], f32r)
        rw1l = sb("rw1l", [P, DH, NE * HR], f32r)
        w2h = sb("w2h", [P, SHC + RC, D], f32r)
        w2l = sb("w2l", [P, SHC + RC, D], f32r)
        with ExitStack() as o:
            stage = sb("stage", [P, 2, 4 * D], f32, o)
        with ExitStack() as o:
            rt = sb("rt", [P, 6, 4 * NE], f32, o)
            pair = sb("pair", [P, 2, 4, NE * NE], f32, o)
            r4 = sb("r4", [P, 4, 4], f32, o)
            gg = sb("gg", [P, 4, 2 * NE], f32r, o)
            gT = sb("gT", [2 * NE, TILE], f32r, o)
        stage_place = sb("stage_place", [P, 8 * D])
        with ExitStack() as o:
            pb = sb("pb", [P, 2, FT], f32, o)
            ct = sb("ct", [P, 2, FT], f32, o)
            ys = sb("ys", [P, 2, FT], f32, o)
            ab = sb("ab", [P, FT], f32, o)
            bu = sb("bu", [P, FT], f32, o)
        xh = sb("xh", [P, DH, TILE], f32r)
        xl = sb("xl", [P, DH, TILE], f32r)
        w1h = sb("w1h", [P, DH, 3 * D], f32r)
        w1l = sb("w1l", [P, DH, 3 * D], f32r)
        wzh = sb("wzh", [P, DH, D], f32r)
        wzl = sb("wzl", [P, DH, D], f32r)
        whT = sb("whT", [P, DH, D])
        with ExitStack() as o:
            esel = sb("esel", [2 * NE, NE, P], f32r, o)
        wq = sb("wq", [P, DH, 3, 3 * N])
        wo2 = sb("wo2", [P, 2, D])
        starts = sb("starts", [P, DH * FT], bf16)
        carry = sb("carry", [P, DH * FT], bf16)
        dec = sb("dec", [P, FT])
        ident = sb("ident", [P, P])
        cols = sb("cols", [P, 19])
        sc = sb("sc", [P, 12])
        condT = sb("condT", [P, DH, B])
        wrh = sb("wrh", [P, DH, NE], f32r)
        wrl = sb("wrl", [P, DH, NE], f32r)
        wrt = sb("wrt", [P, DH, NE])
        cl = sb("cl", [B, NE])
        teA = sb("teA", [P, NT // 2, 4 * NE])
        teB = sb("teB", [P, 4 * NE])
        rb = sb("rb", [P, 4, NE])
        lm = sb("lm", [P, NE, NE])
        PS = ctx.enter_context(nc.psum_tensor("PS", [P, 8, 512], f32))
        del keep, place, stage_place

        O = [0, 1]
        ROT = [2, 3, 4, 5]
        G = 6
        FL = 7

        xv = xT[:, :, :].rearrange("p h (b t) -> p h b t", t=L)

        def weight_stages():
            r = lambda w: w.rearrange("(r p) n -> p r n", p=P)
            st = []
            for e in range(NE // 2):
                st.append(("rw2", e, [r(r_w2[2 * e + i]) for i in range(2)]))
            for e in range(NSH):
                st.append(("w2", e, [r(s_w2[e])]))
            st.append(("l1a", 0, [r(W_f), r(W_i)]))
            st.append(("l1b", 0, [r(W_h), r(W3[:, D:2 * D])]))
            st.append(("l3h", 0, [r(W3[:, 0:D])]))
            for w, nm in ((s_w1, "w1"), (s_w3, "w3")):
                for e in range(NSH):
                    st.append((nm, e, [r(w[e])]))
            for e in range(NE // 2):
                st.append(("rw1", e, [r(r_w1[2 * e + i]) for i in range(2)]))
            return st

        STAGES = weight_stages()
        NSTG = len(STAGES)

        def stage_dst(k, half):
            nm, e, _ = STAGES[k]
            if nm == "rw2":
                c = SHC + 2 * (2 * e + half)
                return w2h[:, c:c + 2, :], w2l[:, c:c + 2, :], 2
            if nm == "w2":
                c = 4 * e + 2 * half
                return w2h[:, c:c + 2, :], w2l[:, c:c + 2, :], 2
            if nm == "l1a":
                return w1h[:, half, 0:512], w1l[:, half, 0:512], 1
            if nm == "w1":
                return w13h[:, half, e * HS:(e + 1) * HS], w13l[:, half, e * HS:(e + 1) * HS], 1
            if nm == "w3":
                q = NSH * HS + e * HS
                return w13h[:, half, q:q + HS], w13l[:, half, q:q + HS], 1
            return rw1h[:, half, e * 512:(e + 1) * 512], rw1l[:, half, e * 512:(e + 1) * 512], 1

        def stage_blocks(k, half):
            nm = STAGES[k][0]
            if nm == "rw2":
                return [(2 * half + r, kc) for kc in range(2) for r in range(2)]
            if nm == "w2":
                return [(r, 2 * half + kc) for kc in range(2) for r in range(2)]
            if nm == "l3h":
                return [(r, kc) for kc in range(2) for r in range(2)]
            return [(r, half) for r in range(4)]

        def stage_view(k):
            nm = STAGES[k][0]
            if nm == "w2":
                return stage[:, k % 2, :].rearrange("p (r n) -> p r n", r=2)
            return stage[:, k % 2, :].rearrange("p (r n) -> p r n", r=4)

        ORDER = [("rows", 0), ("cond", 0), ("rtr", 0), ("cl", 0), ("te", 0), ("bpe", 0)]
        ORDER += [("x", j) for j in range(16)]
        early = [("w", (k, h)) for k in range(9) for h in range(1 if STAGES[k][0] == "l3h" else 2)]
        late = [("w", (k, h)) for k in range(9, NSTG) for h in range(2)]
        for g in range(16):
            ORDER.append(("conv", g))
            if g >= 4:
                ORDER += early[:1]
                early = early[1:]
        ORDER += early
        for g in range(16):
            ORDER.append(("ct", g))
            if g % 2:
                ORDER += late[:1]
                late = late[1:]
        ORDER += late
        BANKED = [j for j in ORDER if j[0] != "conv"]

        def finisher(job):
            kind, j = job
            if kind in ("x", "ct", "conv") and j % 2 == 0:
                return "A"
            return "D"

        def signals(job):
            kind, j = job
            if kind == "w":
                return (0, 1) if STAGES[j[0]][0] == "l3h" else (1, 1)
            return (1, 0) if finisher(job) == "A" else (0, 1)

        A_AT, D_AT = {}, {}
        a = d = 0
        for job in ORDER:
            a += signals(job)[0]
            d += signals(job)[1]
            A_AT[job], D_AT[job] = a, d
        A_ALL, D_ALL = a, d

        s_in = {n: sem("s_in_" + n) for n in ("x", "t", "pad", "rows", "cond", "wr", "l0", "rb")}
        s_stg = [sem(f"s_stg{i}") for i in range(2)]
        s_cst = sem("s_cst")
        s_zero = sem("s_zero")
        s_tp = sem("s_tp")
        s_cv = sem("s_cv")
        s_av = sem("s_av")
        s_dv = sem("s_dv")
        s_par = sem("s_par")
        s_pa = sem("s_pa")
        l_pj = sem("l_pj")
        l_wo = sem("l_wo")
        l_a1 = sem("l_a1")
        l_ln = sem("l_ln")
        l_d = sem("l_d")
        l_x = sem("l_x")
        f_hi, f_lo, f_mm, f_ev = sem("f_hi"), sem("f_lo"), sem("f_mm"), sem("f_ev")
        f_s, f_r0, f_e, f_p = sem("f_s"), sem("f_r0"), sem("f_e"), sem("f_p")
        f_fn, f_S, f_P, f_w = sem("f_fn"), sem("f_S"), sem("f_P"), sem("f_w")
        f_qs, f_C, f_x2 = sem("f_qs"), sem("f_C"), sem("f_x2")
        m_xh, m_xl = sem("m_xh"), sem("m_xl")
        m_rt, m_gtr, m_bc = sem("m_rt"), sem("m_gtr"), sem("m_bc")
        m_l1, m_w2 = sem("m_l1"), sem("m_w2")
        m_act, m_hi, m_mul, m_lo, m_o = sem("m_act"), sem("m_hi"), sem("m_mul"), sem("m_lo"), sem("m_o")
        m_es = sem("m_es")
        m_lg, m_sig, m_rd, m_gsb = sem("m_lg"), sem("m_sig"), sem("m_rd"), sem("m_gsb")
        r_z, r_zh, r_zl, r_zw = sem("r_z"), sem("r_zh"), sem("r_zl"), sem("r_zw")
        r_mm, r_th, r_u, r_v, r_h = sem("r_mm"), sem("r_th"), sem("r_u"), sem("r_v"), sem("r_h")
        r_hl, r_o, r_tr, r_st, r_out = sem("r_hl"), sem("r_o"), sem("r_tr"), sem("r_st"), sem("r_out")

        block = ctx.enter_context(nc.Block())

        def wait(eng, s, v):
            if isinstance(v, int) and v <= 0:
                return
            eng.wait_ge(s, v)

        def flat(ap):
            return ap.rearrange("p h n -> p (h n)")

        NCST = 13

        def xsl(t0, n):
            return xT[:, :, t0:t0 + n] if isinstance(t0, int) else xT[:, :, bass.ds(t0, n)]

        ROUTER_AT = 2

        def front_ready(F):
            if isinstance(F, int):
                return 4 + 2 * (F // 2) + 2
            return 4 + F + 2 if False else 4 + 2 * NT

        def tile_x(T, kind):
            if kind == "A":
                return xsl(T * TILE, TILE)
            if isinstance(T, int):
                k = 16 * (T - NT // 2)
                return xv[:, :, HALF:B, k:k + 16]
            return xv[:, :, HALF:B, bass.ds(16 * (T - NT // 2), 16)]

        def tile_buf(buf, kind):
            v = buf[:, :, :]
            return v if kind == "A" else v.rearrange("p h (b t) -> p h b t", t=16)

        def transposed_src(job, bank):
            return PS[:, bank, :].rearrange("p (b h s) -> p h b s", b=4, h=2)

        def transposed_dst(job):
            kind, j = job
            if kind == "x":
                return xv[:, :, 4 * j:4 * j + 4, :]
            v = convT[:, :, :].rearrange("p h (b t) -> p h b t", t=L)
            return v[:, :, 4 * j:4 * j + 4, ::-1]

        def weight_parts(kh, bank, part):
            k, half = kh
            nm = STAGES[k][0]
            src = PS[:, bank, :]
            if nm == "l1b":
                return [((w1h, w1l)[part][:, half, 2 * D:3 * D], src[:, 0:D]),
                        ((wzh, wzl)[part][:, half, :], src[:, D:2 * D])]
            dst = stage_dst(k, half)
            if dst[2] == 2:
                src = src.rearrange("p (c n) -> p c n", c=2)
            return [(dst[part], src)]

        @block.sync
        def _(sp):
            sp.sem_inc(r_out, 32)
            sp.dma_start(padded[0:L, :], cond).then_inc(s_in["pad"], 16)
            sp.dma_start(condN[:, :], cond).then_inc(s_in["cond"], 16)
            sp.wait_ge(s_zero, 1)
            sp.dma_start(padded[L:2 * L, :], zrow[:, :]).then_inc(s_in["pad"], 16)
            for q in range(4):
                for h in range(DH):
                    sp.dma_start(Xs[h * L:(h + 1) * L, q * 16:(q + 1) * 16, :],
                                 x[q * 16:(q + 1) * 16, :, h * P:(h + 1) * P].rearrange("b s d -> s b d"))\
                      .then_inc(s_in["x"], 16)
            sp.wait_ge(s_in["pad"], 32)
            for h in range(DH):
                src = bass.AP(padded.tensor, h * P, [[D, L], [D, L], [1, P]])
                sp.dma_start(Tz[h * L:(h + 1) * L, :, :], src).then_inc(s_in["t"], 16)
            for k in range(NSTG):
                nm, _, srcs = STAGES[k]
                if k >= 2:
                    sp.wait_ge(s_tp, max(n + 1 for n, j in enumerate(BANKED)
                                         if j[0] == "w" and j[1][0] == k - 2))
                view = stage_view(k)
                r0 = 0
                for s in srcs:
                    sp.dma_start(view[:, r0:r0 + s.shape[1], :], s).then_inc(s_stg[k % 2], 16)
                    r0 += s.shape[1]

            def store(J):
                wait(sp, r_st, 1 + J + 1)
                for tp in range(2):
                    if isinstance(J, int):
                        dst = out[:, 4 * J + 2 * tp:4 * J + 2 * tp + 2, :]
                    else:
                        dst = out[:, bass.ds(4 * J + 2 * tp, 2), :]
                    sp.dma_start(dst.rearrange("b t d -> b (t d)"),
                                 ost[tp * B:(tp + 1) * B, :, :].rearrange("p t d -> p (t d)")).then_inc(r_out, 16)

            with sp.Fori(0, L // NQ) as J:
                store(J)
            sp.wait_ge(r_out, 32 + 32 * (L // NQ))

        @block.gpsimd
        def _(pool):
            n = [0]
            pool.sem_inc(r_o, NQ)

            def made(ins):
                n[0] += 1
                ins.then_inc(s_cst, 1)
                return n[0]

            def after(k):
                pool.wait_ge(s_cst, k)

            pool.memset(zrow[:, :], 0.0).then_inc(s_zero, 1)
            made(pool.memset(ident[:, :], 0.0))
            made(pool.memset(sel[:, :], 1.0))
            made(pool.memset(lm[:, :, :], 1.0))
            made(pool.memset(starts[:, :], 0.0))
            made(pool.memset(carry[:, :], 1.0))
            made(pool.memset(wq[:, :, :, :], 0.0))
            made(pool.memset(wo2[:, :, :], 0.0))
            after(7)
            made(pool.affine_select(out=ident[:, :], in_=ident[:, :], compare_op=ALU.not_equal, fill=1.0,
                                    base=0, pattern=[[-1, P]], channel_multiplier=1))
            sv = starts[:, :].rearrange("p (s t) -> p s t", t=L)
            made(pool.affine_select(out=sv, in_=sv, compare_op=ALU.not_equal, fill=1.0,
                                    base=0, pattern=[[0, DH * FB], [1, L]], channel_multiplier=0))
            cv = carry[:, :].rearrange("p (s t) -> p s t", t=L)
            made(pool.affine_select(out=cv, in_=cv, compare_op=ALU.not_equal, fill=0.0,
                                    base=0, pattern=[[0, DH * FB], [1, L]], channel_multiplier=0))
            made(pool.affine_select(out=lm[:, :, :], in_=lm[:, :, :], compare_op=ALU.is_ge, fill=0.0,
                                    base=-1, pattern=[[1, NE], [-1, NE]], channel_multiplier=0))
            after(11)
            nA = NT // 2 * TB
            sA = sel[:, 0:NT // 2 * TILE].rearrange("p (b t) -> p b t", t=L)
            sB = sel[:, NT // 2 * TILE:].rearrange("p (b t) -> p b t", t=16)
            made(pool.affine_select(out=sA, in_=sA, compare_op=ALU.is_equal, fill=0.0,
                                    base=0, pattern=[[-1, nA], [0, L]], channel_multiplier=1))
            made(pool.affine_select(out=sB, in_=sB, compare_op=ALU.is_equal, fill=0.0,
                                    base=-HALF, pattern=[[-1, HALF], [0, 16]], channel_multiplier=1))
            assert n[0] == NCST

            def front_pool(r, F):
                if r == 4:
                    wait(pool, f_e, 2 * F + 2)
                    pool.tensor_tensor(out=flat(fgt[:, :, :]), in0=flat(fgt[:, :, :]), in1=flat(rcp[:, :, :]),
                                       op=ALU.mult).then_inc(f_p, 1)
                    pool.tensor_tensor(out=flat(inp[:, :, :]), in0=flat(inp[:, :, :]), in1=flat(rcp[:, :, :]),
                                       op=ALU.mult).then_inc(f_p, 1)
                    wait(pool, f_p, 3 * F + 2)
                    wait(pool, f_ev, 3 * F + 3)
                    pool.tensor_tensor(out=flat(cnd[:, :, :]), in0=flat(cnd[:, :, :]), in1=flat(inp[:, :, :]),
                                       op=ALU.mult).then_inc(f_p, 1)
                if r == 5:
                    wait(pool, f_P, F + 1)
                    for h in range(DH):
                        v = rcp[:, h, :].rearrange("p (b t) -> p b t", t=L)
                        h0 = h0s[:, h, bass.ds(FB * F, FB)] if not isinstance(F, int) else h0s[:, h, FB * F:FB * F + FB]
                        last = pool.tensor_tensor(out=v, in0=v, in1=h0.unsqueeze(2).broadcast_to([P, FB, L]),
                                                  op=ALU.mult)
                    last.then_inc(f_w, 1)
                    wait(pool, f_w, 2 * F + 1)
                    pool.tensor_tensor(out=inp[:, :, :], in0=xsl(F * FT, FT), in1=rcp[:, :, :],
                                       op=ALU.add).then_inc(f_w, 1)

            h0s = condT
            pool.wait_ge(s_dv, D_ALL)
            for F in range(2):
                for r in range(6):
                    front_pool(r, F)
            with pool.Fori(0, NT // 2 - 1) as i:
                for c in range(CH):
                    front_pool(c % 6, 2 + 4 * i + c // 6)
            for c in range(12):
                front_pool(c % 6, NF - 2 + c // 6)

            def rec_pool(r, J, first=False):
                if r == 0:
                    wait(pool, r_zh, J + 1)
                    wait(pool, r_z, J + 1)
                    wait(pool, r_zw, 1 + J)
                    pool.tensor_tensor(out=z4l[:, :, :, :].rearrange("p h t b -> p (h t b)"),
                                       in0=z4[:, :, :, :].rearrange("p h t b -> p (h t b)"),
                                       in1=z4h[:, :, :, :].bitcast(f32).rearrange("p h t b -> p (h t b)"),
                                       op=ALU.subtract).then_inc(r_zl, 1)
                if 1 <= r <= 4:
                    t = r - 1
                    if not first or r > 1:
                        pass
                    wait(pool, r_h, 4 * J + t + 1)
                    wait(pool, r_v, 1 + 4 * J + t)
                    pool.tensor_tensor(out=hl[:, :, :], in0=hid[:, :, :], in1=leak(), op=ALU.mult).then_inc(r_hl, 1)
                    if t > 0:
                        out_row(J, t - 1)
                if r == 5:
                    wait(pool, r_h, 4 * J + NQ + 1)
                    out_row(J, NQ - 1)

            def leak():
                return cols_leak.unsqueeze(2).broadcast_to([P, DH, B])

            def out_row(J, t):
                if t == 0:
                    wait(pool, r_tr, 1 + J)
                q = 2 * (t % 2) + t // 2
                pool.tensor_tensor(out=o4[:, :, q, :], in0=z4[:, :, t, :], in1=hid[:, :, :], op=ALU.add)\
                    .then_inc(r_o, 1)

            cols_leak = sc[:, 6:8]
            with pool.Fori(0, L // NQ) as J:
                for r in range(6):
                    rec_pool(r, J)

        @block.scalar
        def _(act):
            act.sem_inc(l_a1, 4)
            act.sem_inc(m_act, CH)
            act.sem_inc(m_hi, CH)
            act.sem_inc(r_st, 1)
            vecs = [(0, bp[0:N], 1), (1, bp[N:2 * N], 1), (2, bs, 1), (3, A_log, 1), (4, dt_log, 1)]
            for r, v, _ in vecs:
                for q in range(2):
                    act.dma_start(rows[r:r + 1, q * N:(q + 1) * N], v.rearrange("(o n) -> o n", o=1))\
                       .then_inc(s_in["rows"], 16)
            for r, v in ((5, conv_b), (7, bo), (9, b_f), (11, b_i), (13, b_h), (15, b3), (17, alpha)):
                act.dma_start(rows[r:r + 2, :], v.rearrange("(h p) -> h p", h=2)).then_inc(s_in["rows"], 16)
            act.dma_start(wrN[:, :], W_router).then_inc(s_in["wr"], 16)
            act.wait_ge(s_cst, 7)
            for q, src in enumerate((Wp[:, 0:N], Wp[:, N:2 * N], Ws)):
                act.dma_start(wq[:, :, q, N:2 * N], src.rearrange("(k p) n -> p k n", p=P)).then_inc(s_in["l0"], 16)
            for q in range(2):
                act.dma_start(wo2[q * N:(q + 1) * N, q, :], Wo).then_inc(s_in["l0"], 16)
            act.dma_start(rb[:, :, :], bass.AP(router_bias.tensor, 0, [[0, P], [0, 4], [1, NE]]))\
               .then_inc(s_in["rb"], 16)

            def evacuate(job):
                kind, j = job
                if kind == "conv":
                    if finisher(job) == "A":
                        act.wait_ge(s_cv, j + 1)
                        act.activation(convS[:, 8 * j:8 * j + 8, :].rearrange("p c b -> p (c b)"),
                                       PS[:, j % 4, :], ACT.Copy).then_inc(s_av, 1)
                    return
                n = BANKED.index(job)
                bank = 4 + n % 4
                if kind in ("x", "ct") and finisher(job) == "A":
                    act.wait_ge(s_tp, n + 1)
                    act.activation(transposed_dst(job), transposed_src(job, bank), ACT.Copy).then_inc(s_av, 1)
                if kind == "w" and signals(job)[0]:
                    act.wait_ge(s_tp, n + 1)
                    for dst, src in weight_parts(j, bank, 0):
                        last = act.activation(dst, src, ACT.Copy)
                    last.then_inc(s_av, 1)

            for job in ORDER[:ORDER.index(("conv", 0))]:
                evacuate(job)
            act.wait_ge(s_par, 1)
            act.activation(sc[:, 0:2], sc[:, 0:2], ACT.Exp, scale=-1.0).then_inc(s_pa, 1)
            act.wait_ge(s_pa, 1)
            act.activation(sc[:, 0:2], sc[:, 0:2], ACT.Ln, bias=1.0).then_inc(s_pa, 1)
            for job in ORDER[ORDER.index(("conv", 0)):]:
                evacuate(job)

            def l0_act(t, p):
                wait(act, l_pj, 2 * t + 1)
                wait(act, l_d, 5 * t + 5)
                act.activation(pb[:, p, :], PS[:, 4 * p, 0:FT], ACT.Identity, bias=sc[:, 2:3]).then_inc(l_a1, 1)
                act.activation(ct[:, p, :], PS[:, 4 * p, FT:2 * FT], ACT.Tanh, bias=sc[:, 3:4]).then_inc(l_a1, 1)
                wait(act, l_d, 5 * t + 10 + 1)
                act.activation(ab[:, :], ab[:, :], ACT.Exp, scale=-1.0).then_inc(l_ln, 1)
                wait(act, l_ln, 2 * t + 1)
                act.activation(ab[:, :], ab[:, :], ACT.Ln, bias=1.0).then_inc(l_ln, 1)

            act.wait_ge(s_par, 5)
            l0_act(0, 0)
            with act.Fori(0, NT // 2 - 1) as i:
                l0_act(2 * i + 1, 1)
                l0_act(2 * i + 2, 0)
            l0_act(NT - 1, 1)

            def front_act(r, F):
                if r == 0:
                    wait(act, l_x, front_ready(F))
                    wait(act, f_mm, 3 * F)
                    act.activation(x1h[:, :, :], xsl(F * FT, FT), ACT.Copy).then_inc(f_hi, 1)
                if r in (1, 2, 3):
                    q = r - 1
                    wait(act, f_mm, 3 * F + q + 1)
                    if q == 0:
                        wait(act, f_P, F)
                    if q == 1:
                        wait(act, f_x2, F)
                    buf = (fgt, inp, cnd)[q]
                    fn = (ACT.Sigmoid, ACT.Sigmoid, ACT.Identity)[q]
                    for m in range(DH):
                        last = act.activation(buf[:, m, :], PS[:, FL, m * FT:(m + 1) * FT], fn,
                                              bias=cols[:, 9 + 2 * q + m:10 + 2 * q + m])
                    last.then_inc(f_ev, 1)
                if r == 3:
                    wait(act, f_s, F + 1)
                    wait(act, f_w, 2 * F)
                    act.activation(flat(rcp[:, :, :]), flat(gsum[:, :, :]), ACT.Ln).then_inc(f_r0, 1)
                    wait(act, f_r0, 2 * F + 1)
                    act.activation(flat(rcp[:, :, :]), flat(rcp[:, :, :]), ACT.Exp, scale=-1.0).then_inc(f_r0, 1)

            def split_act(T, kind):
                if kind == "A":
                    wait(act, f_x2, 2 * T + 2)
                else:
                    wait(act, f_x2, NF)
                wait(act, m_l1, GRP + GRP * T)
                wait(act, m_rt, 1 + T)
                src, dst = tile_x(T, kind), tile_buf(xh, kind)
                act.activation(dst, src, ACT.Copy).then_inc(m_xh, 1)

            def moe_act(c, T, kind):
                if c == 0:
                    split_act(T, kind)
                if c == ROUTER_AT:
                    wait(act, m_lg, T + 1)
                    act.activation(rt[:, 1, :], rt[:, 0, :], ACT.Sigmoid).then_inc(m_sig, 1)
                if c > 0:
                    hi(c - 1, T)
                wait(act, m_l1, GRP + GRP * T + (2 * c + 1 if c < SHC else c + SHC + 1))
                wait(act, m_mul, CH * T + CH + c - 1)
                bank = ROT[(2 * c if c < SHC else c + SHC) % 4]
                act.activation(act_g[:, c % 2, :], PS[:, bank, :], ACT.Silu if c < SHC else ACT.Gelu)\
                   .then_inc(m_act, 1)
                if c == CH - 1:
                    hi(c, T)

            def hi(c, T):
                wait(act, m_mul, CH * T + CH + c + 1)
                wait(act, m_w2, CH * T + CH + c - LAG + 1)
                act.activation(hh[:, c % LAG, :], hbuf[:, c % 2, :], ACT.Copy).then_inc(m_hi, 1)

            def rec_act(r, J, tiles):
                if r == 0:
                    wait(act, m_o, tiles)
                    wait(act, r_o, NQ + NQ * J)
                    wait(act, r_zw, 1 + J)
                    src = xv[:, :, :, 4 * J:4 * J + 4] if isinstance(J, int) else xv[:, :, :, bass.ds(4 * J, 4)]
                    src = src.rearrange("p h b t -> p h t b")
                    for h in range(DH):
                        last = act.activation(z4[:, h, :, :], src[:, h, :, :], ACT.Copy)
                    last.then_inc(r_z, 1)
                    wait(act, r_z, J + 1)
                    act.activation(z4h[:, :, :, :].rearrange("p h t b -> p (h t b)"),
                                   z4[:, :, :, :].rearrange("p h t b -> p (h t b)"), ACT.Copy).then_inc(r_zh, 1)
                if 1 <= r <= 4:
                    t = r - 1
                    wait(act, r_mm, 4 * J + t + 1)
                    for m in range(DH):
                        last = act.activation(th[:, m, :], PS[:, FL, m * FT + t * B:m * FT + (t + 1) * B], ACT.Tanh,
                                              bias=sc[:, 8 + m:9 + m], scale=0.5)
                    last.then_inc(r_th, 1)
                if r == 5:
                    wait(act, r_tr, 1 + J + 1)
                    wait(act, r_out, 32 + 32 * J)
                    act.activation(ost[:, :, :].rearrange("p t d -> p (t d)"), PS[:, FL, :], ACT.Copy)\
                       .then_inc(r_st, 1)

            def rec_act2(r, J):
                if 1 <= r <= 4:
                    t = r - 1
                    wait(act, r_v, 1 + 4 * J + t + 1)
                    wait(act, r_hl, 4 * J + t + 1)
                    wait(act, r_o, NQ + 4 * J + t)
                    act.activation(hid[:, :, :], uz[:, :, :], ACT.Tanh).then_inc(r_h, 1)

            for F in range(2):
                for r in range(6):
                    front_act(r, F)
            with act.Fori(0, NT // 2 - 1) as i:
                for c in range(CH):
                    front_act(c % 6, 2 + 4 * i + c // 6)
                    moe_act(c, i, "A")
            for c in range(CH):
                if c < 12:
                    front_act(c % 6, NF - 2 + c // 6)
                moe_act(c, NT // 2 - 1, "A")
            for c in range(CH):
                moe_act(c, NT // 2, "B")
            with act.Fori(0, NT // 2 - 1) as k:
                for c in range(CH):
                    J = 4 * k + c // 6
                    rec_act(c % 6, J, 2 * (NT // 2) + 2 + 2 * (1 + k) + 2 - 2)
                    moe_act(c, NT // 2 + 1 + k, "B")
                    rec_act2(c % 6, J)
            for J in range(L // NQ - 4, L // NQ):
                for r in range(6):
                    rec_act(r, J, 2 * NT + 2)
                    rec_act2(r, J)

        @block.vector
        def _(dve):
            dve.sem_inc(l_d, 10)
            dve.sem_inc(l_x, 4)
            dve.sem_inc(m_mul, CH)
            dve.sem_inc(m_lo, CH)
            dve.sem_inc(m_o, 2)
            dve.sem_inc(r_v, 1)

            def evacuate(job):
                kind, j = job
                if kind == "conv":
                    if finisher(job) == "D":
                        dve.wait_ge(s_cv, j + 1)
                        dve.tensor_copy(convS[:, 8 * j:8 * j + 8, :].rearrange("p c b -> p (c b)"),
                                        PS[:, j % 4, :]).then_inc(s_dv, 1)
                    return
                if finisher(job) != "D":
                    return
                n = BANKED.index(job)
                bank = 4 + n % 4
                dve.wait_ge(s_tp, n + 1)
                b = PS[:, bank, :]
                if kind in ("x", "ct"):
                    dve.tensor_copy(transposed_dst(job), transposed_src(job, bank)).then_inc(s_dv, 1)
                elif kind == "rows":
                    dve.tensor_copy(cols[:, :], b[:, 0:19]).then_inc(s_dv, 1)
                elif kind == "cond":
                    dve.tensor_copy(condT[:, :, :], b[:, 0:2 * B].rearrange("p (h b) -> p h b", h=2)).then_inc(s_dv, 1)
                elif kind == "rtr":
                    v = b[:, 0:4 * NE].rearrange("p (k e) -> p k e", k=4)
                    dve.tensor_copy(wrh[:, :, :], v[:, 0:2, :]).then_inc(s_par, 1)
                    dve.tensor_copy(wrt[:, :, :], v[:, 2:4, :])
                    dve.wait_ge(s_par, 2)
                    dve.tensor_tensor(out=wrl[:, :, :], in0=v[:, 0:2, :], in1=wrh[:, :, :].bitcast(f32),
                                      op=ALU.subtract).then_inc(s_dv, 1)
                elif kind == "cl":
                    dve.tensor_copy(cl[:, :], PS[0:B, bank, 0:NE]).then_inc(s_dv, 1)
                elif kind == "te":
                    dve.tensor_copy(teA[:, :, :].rearrange("p a b -> p (a b)"), b[:, 0:P])
                    dve.tensor_copy(teB[:, :], b[:, P:P + 4 * NE]).then_inc(s_dv, 1)
                elif kind == "bpe":
                    dve.tensor_tensor(out=sc[:, 2:4], in0=b[:, 0:2], in1=cols[:, 0:2], op=ALU.add).then_inc(s_dv, 1)
                elif kind == "w":
                    if STAGES[j[0]][0] == "l3h":
                        dve.tensor_copy(whT[:, :, :], b.rearrange("p (k n) -> p k n", k=2)).then_inc(s_dv, 1)
                        return
                    dve.wait_ge(s_av, A_AT[job])
                    for (hi_, src), (lo_, _) in zip(weight_parts(j, bank, 0), weight_parts(j, bank, 1)):
                        last = dve.tensor_tensor(out=lo_, in0=src, in1=hi_.bitcast(f32), op=ALU.subtract)
                    last.then_inc(s_dv, 1)

            evacuate(("rows", 0))
            dve.wait_ge(s_dv, 1)
            dve.scalar_tensor_tensor(out=sc[:, 0:2], in0=cols[:, 3:5], scalar=-1.0, in1=cols[:, 3:5],
                                     op0=ALU.mult, op1=ALU.max).then_inc(s_par, 1)
            for job in ORDER[1:ORDER.index(("conv", 0))]:
                evacuate(job)
            dve.tensor_scalar(sc[:, 6:8], cols[:, 17:19], -1.0, 1.0, ALU.mult, ALU.add)
            dve.tensor_scalar(sc[:, 8:10], cols[:, 15:17], 0.5, None, ALU.mult)
            dve.wait_ge(s_pa, 2)
            dve.scalar_tensor_tensor(out=sc[:, 4:6], in0=cols[:, 3:5], scalar=0.0, in1=sc[:, 0:2],
                                     op0=ALU.max, op1=ALU.add).then_inc(s_par, 1)
            dve.wait_ge(s_par, 3)
            dve.scalar_tensor_tensor(out=sc[:, 10:11], in0=sc[:, 4:5], scalar=-1.0, in1=sc[:, 5:6],
                                     op0=ALU.mult, op1=ALU.mult).then_inc(s_par, 1)
            dve.wait_ge(s_par, 4)
            dve.tensor_scalar(sc[:, 10:11], sc[:, 10:11], 1.0, None, ALU.add).then_inc(s_par, 1)
            dve.wait_ge(s_par, 5)
            dve.wait_ge(s_cst, NCST)
            dve.tensor_scalar(dec[:, :], carry[:, 0:FT], sc[:, 10:11], None, ALU.mult).then_inc(s_par, 1)
            for job in ORDER[ORDER.index(("conv", 0)):]:
                evacuate(job)

            def l0_x(t, p):
                for m in range(DH):
                    wait(dve, l_wo, 4 + 2 * t + m + 1)
                    xs = xT[:, m, t * TILE:(t + 1) * TILE] if isinstance(t, int) else xT[:, m, bass.ds(t * TILE, TILE)]
                    dve.scalar_tensor_tensor(out=xs, in0=PS[:, 4 * p + 2 + m, :], scalar=cols[:, 7 + m:8 + m],
                                             in1=xs, op0=ALU.add, op1=ALU.add).then_inc(l_x, 1)

            def l0_dve(t, p, first=False):
                wait(dve, l_a1, 4 + 2 * t + 1)
                dve.scalar_tensor_tensor(out=ab[:, :], in0=pb[:, p, :], scalar=-1.0, in1=pb[:, p, :],
                                         op0=ALU.mult, op1=ALU.max).then_inc(l_d, 1)
                if not first:
                    l0_x(t - 1, 1 - p)
                wait(dve, l_ln, 2 * t + 2)
                dve.scalar_tensor_tensor(out=bu[:, :], in0=pb[:, p, :], scalar=0.0, in1=ab[:, :],
                                         op0=ALU.max, op1=ALU.add).then_inc(l_d, 1)
                wait(dve, l_d, 10 + 5 * t + 2)
                wait(dve, l_pj, 2 * t + 2)
                dve.scalar_tensor_tensor(out=bu[:, :], in0=PS[:, 4 * p + 1, 0:FT], scalar=cols[:, 2:3],
                                         in1=bu[:, :], op0=ALU.add, op1=ALU.mult).then_inc(l_d, 1)
                wait(dve, l_d, 10 + 5 * t + 3)
                wait(dve, l_wo, 2 * t + 2 if isinstance(t, int) and t < 2 else 2 * t + 2)
                dve.tensor_tensor_scan(out=ys[:, p, :], data0=dec[:, :], data1=bu[:, :], initial=0.0,
                                       op0=ALU.mult, op1=ALU.add).then_inc(l_d, 1)
                wait(dve, l_d, 10 + 5 * t + 4)
                wait(dve, l_a1, 4 + 2 * t + 2)
                dve.scalar_tensor_tensor(out=ys[:, p, :], in0=ys[:, p, :], scalar=sc[:, 5:6], in1=ct[:, p, :],
                                         op0=ALU.mult, op1=ALU.mult).then_inc(l_d, 1)

            dve.wait_ge(s_in["rb"], 16)
            dve.wait_ge(s_par, 6)
            l0_dve(0, 0, True)
            with dve.Fori(0, NT // 2 - 1) as i:
                l0_dve(2 * i + 1, 1)
                l0_dve(2 * i + 2, 0)
            l0_dve(NT - 1, 1)
            l0_x(NT - 1, 1)

            dve.tensor_tensor(out=esel[:, :, :], in0=ident[0:2 * NE, 0:NE].unsqueeze(2).broadcast_to([2 * NE, NE, P]),
                              in1=ident[0:2 * NE, NE:2 * NE].unsqueeze(2).broadcast_to([2 * NE, NE, P]),
                              op=ALU.add).then_inc(m_es, 1)

            def front_dve(r, F):
                if r == 0:
                    wait(dve, f_hi, F + 1)
                    wait(dve, f_mm, 3 * F)
                    dve.tensor_tensor(out=x1l[:, :, :], in0=xsl(F * FT, FT), in1=x1h[:, :, :].bitcast(f32),
                                      op=ALU.subtract).then_inc(f_lo, 1)
                if r == 3:
                    wait(dve, f_ev, 3 * F + 2)
                    dve.scalar_tensor_tensor(out=flat(gsum[:, :, :]), in0=flat(fgt[:, :, :]), scalar=EPS,
                                             in1=flat(inp[:, :, :]), op0=ALU.add, op1=ALU.add).then_inc(f_s, 1)
                if r == 4:
                    wait(dve, f_r0, 2 * F + 2)
                    dve.tensor_tensor(out=flat(gsum[:, :, :]), in0=flat(gsum[:, :, :]), in1=flat(rcp[:, :, :]),
                                      op=ALU.mult).then_inc(f_e, 1)
                    wait(dve, f_e, 2 * F + 1)
                    dve.scalar_tensor_tensor(out=flat(rcp[:, :, :]), in0=flat(gsum[:, :, :]), scalar=2.0,
                                             in1=flat(rcp[:, :, :]), op0=ALU.subtract, op1=ALU.mult,
                                             reverse0=True).then_inc(f_e, 1)
                if r == 5:
                    wait(dve, f_p, 3 * F + 2)
                    dve.tensor_scalar(flat(fgt[:, :, :]), flat(fgt[:, :, :]), EPS, 1.0, ALU.add, ALU.min)\
                       .then_inc(f_fn, 1)
                    wait(dve, f_fn, F + 1)
                    dve.tensor_tensor_scan(out=flat(gsum[:, :, :])[:, ::-1], data0=starts[:, :],
                                           data1=flat(fgt[:, :, :])[:, ::-1], initial=0.0,
                                           op0=ALU.max, op1=ALU.mult).then_inc(f_S, 1)
                    dve.tensor_tensor_scan(out=flat(rcp[:, :, :]), data0=starts[:, :], data1=flat(fgt[:, :, :]),
                                           initial=0.0, op0=ALU.max, op1=ALU.mult).then_inc(f_P, 1)
                    wait(dve, f_S, F + 1)
                    wait(dve, f_p, 3 * F + 3)
                    dve.tensor_tensor(out=flat(cnd[:, :, :]), in0=flat(cnd[:, :, :]), in1=flat(gsum[:, :, :]),
                                      op=ALU.mult).then_inc(f_qs, 1)
                    wait(dve, f_qs, F + 1)
                    dve.tensor_tensor_scan(out=flat(gsum[:, :, :]), data0=carry[:, :], data1=flat(cnd[:, :, :]),
                                           initial=0.0, op0=ALU.mult, op1=ALU.add).then_inc(f_C, 1)
                    wait(dve, f_C, F + 1)
                    wait(dve, f_w, 2 * F + 2)
                    dve.tensor_tensor(out=xsl(F * FT, FT), in0=inp[:, :, :], in1=gsum[:, :, :],
                                      op=ALU.add).then_inc(f_x2, 1)

            K_RD = 14

            def router_dve(T, kind):
                base = K_RD * T
                k = [0]

                def step(ins):
                    k[0] += 1
                    ins.then_inc(m_rd, 1)

                def prev():
                    wait(dve, m_rd, base + k[0])

                lg, s, selv, rank, sm, mk = (rt[:, q, :] for q in range(6))
                v3 = lambda a: a.rearrange("p (g e) -> p g e", g=4)
                wait(dve, m_rt, 1 + T + 1)
                te = teB[:, :] if kind == "B" else (teA[:, T, :] if isinstance(T, int) else
                                                   teA[:, bass.ds(T, 1), :].rearrange("p a b -> p (a b)"))
                dve.tensor_tensor(out=lg, in0=PS[:, G, 0:4 * NE], in1=te, op=ALU.add).then_inc(m_lg, 1)
                wait(dve, m_sig, T + 1)
                step(dve.tensor_tensor(out=selv, in0=s, in1=rb[:, :, :].rearrange("p g e -> p (g e)"), op=ALU.add))
                prev()
                for g in range(4):
                    row = v3(selv)[:, g, :]
                    sj = row.unsqueeze(1).broadcast_to([P, NE, NE])
                    se = row.unsqueeze(2).broadcast_to([P, NE, NE])
                    pg = [pair[:, q, g, :].rearrange("p (e j) -> p e j", e=NE) for q in range(2)]
                    dve.tensor_tensor(out=pg[0], in0=sj, in1=se, op=ALU.is_gt)
                    last = dve.tensor_tensor(out=pg[1], in0=sj, in1=se, op=ALU.is_equal)
                step(last)
                prev()
                lmb = lm[:, :, :].rearrange("p e j -> p (e j)").unsqueeze(1).broadcast_to([P, 4, NE * NE])
                step(dve.tensor_tensor(out=pair[:, 1, :, :], in0=pair[:, 1, :, :], in1=lmb, op=ALU.mult))
                prev()
                step(dve.tensor_tensor(out=pair[:, 0, :, :], in0=pair[:, 0, :, :], in1=pair[:, 1, :, :], op=ALU.add))
                prev()
                step(dve.tensor_reduce(out=rank, in_=pair[:, 0, :, :].rearrange("p g (e j) -> p (g e) j", j=NE),
                                       op=ALU.add, axis=AX.X))
                prev()
                dve.tensor_scalar(mk, rank, 1.5, None, ALU.is_lt)
                step(dve.scalar_tensor_tensor(out=sm, in0=rank, scalar=1.5, in1=s, op0=ALU.is_lt, op1=ALU.mult))
                prev()
                den, rc, hc, one = (r4[:, q, :] for q in range(4))
                step(dve.tensor_reduce(out=den, in_=v3(sm), op=ALU.add, axis=AX.X))
                prev()
                dve.tensor_scalar(one, den, 1e-9, None, ALU.is_gt)
                step(dve.tensor_scalar(rc, den, 1e-9, None, ALU.add))
                prev()
                dve.tensor_scalar(hc, one, -0.5, 0.5, ALU.mult, ALU.add)
                step(dve.reciprocal(rc, rc))
                prev()
                step(dve.tensor_tensor(out=rc, in0=rc, in1=one, op=ALU.mult))
                prev()
                dve.tensor_tensor(out=v3(mk), in0=v3(mk), in1=hc.unsqueeze(2).broadcast_to([P, 4, NE]), op=ALU.mult)
                step(dve.tensor_tensor(out=v3(sm), in0=v3(sm), in1=rc.unsqueeze(2).broadcast_to([P, 4, NE]), op=ALU.mult))
                prev()
                step(dve.tensor_tensor(out=sm, in0=sm, in1=mk, op=ALU.add))
                prev()
                step(dve.tensor_copy(gg[:, :, 0:NE], v3(sm)))
                prev()
                step(dve.tensor_tensor(out=gg[:, :, NE:2 * NE], in0=v3(sm), in1=gg[:, :, 0:NE].bitcast(f32),
                                       op=ALU.subtract))
                assert k[0] == K_RD

            def lo(c, T):
                wait(dve, m_hi, CH * T + CH + c + 1)
                wait(dve, m_w2, CH * T + CH + c - LAG + 1)
                dve.tensor_tensor(out=hlo[:, c % LAG, :], in0=hbuf[:, c % 2, :], in1=hh[:, c % LAG, :].bitcast(f32),
                                  op=ALU.subtract).then_inc(m_lo, 1)

            def moe_dve(c, T, kind):
                if c == 0:
                    wait(dve, m_xh, T + 1)
                    dve_src, dst = tile_x(T, kind), tile_buf(xl, kind)
                    for h in range(DH):
                        last = dve.tensor_tensor(out=dst[:, h], in0=dve_src[:, h],
                                                 in1=tile_buf(xh, kind)[:, h].bitcast(f32), op=ALU.subtract)
                    last.then_inc(m_xl, 1)
                if c == ROUTER_AT:
                    router_dve(T, kind)
                if c == SHC - 1:
                    wait(dve, m_gtr, T + 1)
                    dve.tensor_copy(gT[:, :], PS[0:2 * NE, G, :]).then_inc(m_gsb, 1)
                if c > 0:
                    lo(c - 1, T)
                wait(dve, m_act, CH * T + CH + c + 1)
                if c < SHC:
                    wait(dve, m_l1, GRP + GRP * T + 2 * c + 2)
                    dve.scalar_tensor_tensor(out=hbuf[:, c % 2, :], in0=act_g[:, c % 2, :], scalar=1.0 / NSH,
                                             in1=PS[:, ROT[(2 * c + 1) % 4], :], op0=ALU.mult, op1=ALU.mult)\
                       .then_inc(m_mul, 1)
                else:
                    wait(dve, m_bc, NE * T + (c - SHC) // 2 + 1)
                    dve.tensor_tensor(out=hbuf[:, c % 2, :], in0=act_g[:, c % 2, :], in1=PS[:, G, :],
                                      op=ALU.mult).then_inc(m_mul, 1)
                if c == CH - 1:
                    lo(c, T)
                    wait(dve, m_w2, CH * T + CH + CH)
                    for m in range(DH):
                        xs = tile_x(T, kind)[:, m]
                        o = PS[:, O[m], :]
                        if kind == "B":
                            o = o.rearrange("p (b t) -> p b t", t=16)
                        dve.scalar_tensor_tensor(out=xs, in0=o, scalar=0.25, in1=xs,
                                                 op0=ALU.mult, op1=ALU.add).then_inc(m_o, 1)

            def rec_dve(r, J):
                if 1 <= r <= 4:
                    t = r - 1
                    wait(dve, r_th, 4 * J + t + 1)
                    dve.scalar_tensor_tensor(out=uz[:, :, :], in0=th[:, :, :], scalar=1.0, in1=z4[:, :, t, :],
                                             op0=ALU.add, op1=ALU.mult).then_inc(r_u, 1)
                    wait(dve, r_u, 4 * J + t + 1)
                    wait(dve, r_hl, 4 * J + t + 1)
                    dve.scalar_tensor_tensor(out=uz[:, :, :], in0=uz[:, :, :], scalar=0.5, in1=hl[:, :, :],
                                             op0=ALU.mult, op1=ALU.add).then_inc(r_v, 1)

            for F in range(2):
                for r in range(6):
                    front_dve(r, F)
            with dve.Fori(0, NT // 2 - 1) as i:
                for c in range(CH):
                    front_dve(c % 6, 2 + 4 * i + c // 6)
                    moe_dve(c, i, "A")
            for c in range(CH):
                if c < 12:
                    front_dve(c % 6, NF - 2 + c // 6)
                moe_dve(c, NT // 2 - 1, "A")
            for c in range(CH):
                if c == 1:
                    dve.tensor_copy(hid[:, :, :], condT[:, :, :]).then_inc(r_h, 1)
                moe_dve(c, NT // 2, "B")
            with dve.Fori(0, NT // 2 - 1) as k:
                for c in range(CH):
                    rec_dve(c % 6, 4 * k + c // 6)
                    moe_dve(c, NT // 2 + 1 + k, "B")
            for J in range(L // NQ - 4, L // NQ):
                for r in range(6):
                    rec_dve(r, J)

        @block.tensor
        def _(pe):
            pe.sem_inc(l_wo, 4)
            pe.sem_inc(m_w2, CH)
            pe.sem_inc(m_l1, GRP)
            pe.sem_inc(m_rt, 1)
            pe.sem_inc(r_zw, 1)
            pe.sem_inc(r_tr, 1)

            def free_bank(job):
                kind, j = job
                if kind == "conv":
                    same = [("conv", j - 4)] if j >= 4 else []
                else:
                    n = BANKED.index(job)
                    same = [BANKED[n - 4]] if n >= 4 else []
                for old in same:
                    if finisher(old) == "A":
                        pe.wait_ge(s_av, A_AT[old])
                    else:
                        pe.wait_ge(s_dv, D_AT[old])

            def split3(o, wh, wl, bh, bl, first, last, **kw):
                pe.matmul(o, wh, bh, start=first, stop=False, **kw)
                pe.matmul(o, wh, bl, start=False, stop=False, **kw)
                return pe.matmul(o, wl, bh, start=False, stop=last, **kw)

            waited = set()

            def once(s, name, v):
                if name not in waited:
                    waited.add(name)
                    pe.wait_ge(s, v)

            for job in ORDER:
                kind, j = job
                free_bank(job)
                if kind == "conv":
                    once(s_in["t"], "t", 32)
                    for c in range(8):
                        ch = 8 * j + c
                        for h in range(DH):
                            q = slice(h * L, (h + 1) * L)
                            last = pe.matmul(PS[q, j % 4, c * B:(c + 1) * B], Tz[q, :, ch], Xs[q, :, ch],
                                             start=True, stop=True)
                    last.then_inc(s_cv, 1)
                    continue
                n = BANKED.index(job)
                b = PS[:, 4 + n % 4, :]
                if kind == "rows":
                    pe.wait_ge(s_cst, NCST)
                    once(s_in["rows"], "rows", 16 * 17)
                    last = pe.transpose(b[:, 0:19], rows[:, :], ident[0:19, 0:19])
                elif kind == "cond":
                    once(s_in["cond"], "cond", 16)
                    for h in range(DH):
                        last = pe.transpose(b[:, h * B:(h + 1) * B], condN[:, h * P:(h + 1) * P], ident[0:B, 0:B])
                elif kind == "rtr":
                    once(s_in["wr"], "wr", 16)
                    for k in range(4):
                        last = pe.transpose(b[:, k * NE:(k + 1) * NE], wrN[:, k * P:(k + 1) * P], ident[0:NE, 0:NE])
                elif kind == "cl":
                    pe.wait_ge(s_dv, D_AT[("rtr", 0)])
                    for k in range(DH):
                        last = pe.matmul(PS[0:B, 4 + n % 4, 0:NE], condT[:, k, :], wrt[:, k, :],
                                         start=k == 0, stop=k == DH - 1)
                elif kind == "te":
                    pe.wait_ge(s_dv, D_AT[("cl", 0)])
                    for g in range(4 * (NT // 2 + 1)):
                        last = pe.matmul(b[:, g * NE:(g + 1) * NE], sel[:, g * P:(g + 1) * P], cl[:, :],
                                         start=True, stop=True)
                elif kind == "bpe":
                    once(s_in["l0"], "l0", 16 * 5)
                    for q in range(2):
                        for th_ in range(2):
                            for k in range(DH):
                                last = pe.matmul(b[:, q:q + 1], wq[:, k, q, (1 - th_) * N:(1 - th_) * N + P],
                                                 cols[:, 5 + k:6 + k], start=th_ == 0 and k == 0,
                                                 stop=th_ == 1 and k == DH - 1)
                elif kind in ("x", "ct"):
                    if kind == "x":
                        once(s_in["x"], "x", 16 * 8)
                    else:
                        once(s_av, "cvA", A_AT[("conv", 14)])
                        once(s_dv, "cvD", D_AT[("conv", 15)])
                    for i in range(4):
                        bt = 4 * j + i
                        src = Xs[:, bt, :] if kind == "x" else convS[:, :, bt]
                        last = pe.transpose(b[:, i * P:(i + 1) * P], src, ident[:, :])
                elif kind == "w":
                    k, half = j
                    if half == 0:
                        cnt = 16 * sum(len(STAGES[q][2]) for q in range(k % 2, k + 1, 2))
                        pe.wait_ge(s_stg[k % 2], cnt)
                    v = stage_view(k)
                    for i, (r, kc) in enumerate(stage_blocks(k, half)):
                        last = pe.transpose(b[:, i * P:(i + 1) * P], v[:, r, kc * P:(kc + 1) * P], ident[:, :])
                last.then_inc(s_tp, 1)

            def l0_proj(t, p):
                def rhs(src, k, th_):
                    o = t * TILE + th_ * FT
                    return src[:, k, o:o + FT] if isinstance(o, int) else src[:, k, bass.ds(o, FT)]

                wait(pe, l_a1, 2 * t + 2)
                for q in range(3):
                    if q == 2:
                        wait(pe, l_d, 5 * t + 3)
                    o = PS[:, 4 * p + q // 2, (q % 2) * FT:(q % 2) * FT + FT]
                    n = 0
                    for k in range(DH):
                        for th_ in range(2):
                            n += 1
                            last = pe.matmul(o, wq[:, k, q, (1 - th_) * N:(1 - th_) * N + P],
                                             rhs(convT if q < 2 else xT, k, th_), start=n == 1, stop=n == 4)
                    if q:
                        last.then_inc(l_pj, 1)

            def l0_out(t, p):
                wait(pe, l_d, 10 + 5 * t + 5)
                wait(pe, l_x, 2 * t + 2)
                for m in range(DH):
                    for th_ in range(2):
                        last = pe.matmul(PS[:, 4 * p + 2 + m, th_ * FT:(th_ + 1) * FT],
                                         wo2[:, th_, m * P:(m + 1) * P], ys[:, p, :], start=True, stop=True)
                    last.then_inc(l_wo, 1)

            pe.wait_ge(s_av, A_ALL)
            pe.wait_ge(s_dv, D_ALL)
            l0_proj(0, 0)
            with pe.Fori(0, NT // 2 - 1) as i:
                l0_proj(2 * i + 1, 1)
                l0_out(2 * i, 0)
                l0_proj(2 * i + 2, 0)
                l0_out(2 * i + 1, 1)
            l0_proj(NT - 1, 1)
            l0_out(NT - 2, 0)
            l0_out(NT - 1, 1)

            def front_pe(r, F):
                if r in (1, 2, 3):
                    q = r - 1
                    if q == 0:
                        wait(pe, f_hi, F + 1)
                        wait(pe, f_lo, F + 1)
                    wait(pe, f_ev, 3 * F + q)
                    for m in range(DH):
                        w = slice(q * D + m * P, q * D + (m + 1) * P)
                        for k in range(DH):
                            last = split3(PS[:, FL, m * FT:(m + 1) * FT], w1h[:, k, w], w1l[:, k, w],
                                          x1h[:, k, :], x1l[:, k, :], k == 0, k == DH - 1)
                    last.then_inc(f_mm, 1)

            def router_pe(T):
                wait(pe, m_mul, CH * T + CH)
                for g in range(4):
                    o = PS[:, G, g * NE:(g + 1) * NE]
                    q = slice(g * P, (g + 1) * P)
                    for k in range(DH):
                        pe.matmul(o, xh[:, k, q], wrh[:, k, :], start=k == 0, stop=False)
                        pe.matmul(o, xl[:, k, q], wrh[:, k, :], start=False, stop=False)
                        last = pe.matmul(o, xh[:, k, q], wrl[:, k, :], start=False, stop=k == DH - 1)
                last.then_inc(m_rt, 1)

            def layer1(o, wh, wl, w):
                for k in range(DH):
                    last = split3(o, wh[:, k, w], wl[:, k, w], xh[:, k, :], xl[:, k, :], k == 0, k == DH - 1)
                last.then_inc(m_l1, 1)

            def w2(c, T):
                wait(pe, m_lo, CH * T + CH + c + 1)
                if c == 0:
                    wait(pe, m_o, 2 * T + 2)
                for m in range(DH):
                    w = slice(m * P, (m + 1) * P)
                    last = split3(PS[:, O[m], :], w2h[:, c, w], w2l[:, c, w], hh[:, c % LAG, :], hlo[:, c % LAG, :],
                                  c == 0, c == CH - 1, skip_group_check=True)
                last.then_inc(m_w2, 1)

            def moe_pe(c, T):
                if c == 0:
                    wait(pe, m_xh, T + 1)
                    wait(pe, m_xl, T + 1)
                    router_pe(T)
                if c < SHC:
                    wait(pe, m_act, CH * T + CH + c - 1)
                    layer1(PS[:, ROT[(2 * c) % 4], :], w13h, w13l, slice(c * P, (c + 1) * P))
                    wait(pe, m_mul, CH * T + CH + c - 1)
                    layer1(PS[:, ROT[(2 * c + 1) % 4], :], w13h, w13l,
                           slice((SHC + c) * P, (SHC + c + 1) * P))
                else:
                    g = c - SHC
                    if g < 4:
                        wait(pe, m_mul, CH * T + CH + SHC - 2 + g // 2 + 1)
                    else:
                        wait(pe, m_act, CH * T + CH + c - 3)
                    layer1(PS[:, ROT[g % 4], :], rw1h, rw1l, slice(g * P, (g + 1) * P))
                if c == SHC - 1:
                    wait(pe, m_rd, 14 * T + 14)
                    for g in range(4):
                        last = pe.transpose(PS[0:2 * NE, G, g * P:(g + 1) * P], gg[:, g, :].bitcast(f32), ident[:, :])
                    last.then_inc(m_gtr, 1)
                if c >= LAG:
                    w2(c - LAG, T)
                if c >= SHC and (c - SHC) % 2 == 0:
                    e = (c - SHC) // 2
                    if e == 0:
                        if isinstance(T, int) or True:
                            wait(pe, m_es, 1)
                        wait(pe, m_gsb, T + 1)
                    wait(pe, m_mul, CH * T + CH + c)
                    pe.matmul(PS[:, G, :], esel[:, e, :], gT[:, :], start=True, stop=True).then_inc(m_bc, 1)
                if c == CH - 1:
                    for q in range(CH - LAG, CH):
                        w2(q, T)

            def rec_pe(r, J):
                if r == 0:
                    wait(pe, r_zl, J + 1)
                    wait(pe, r_zh, J + 1)
                    wait(pe, r_st, 1 + J)
                    for m in range(DH):
                        w = slice(m * P, (m + 1) * P)
                        for k in range(DH):
                            z_h = z4h[:, k, :, :].rearrange("p t b -> p (t b)")
                            z_l = z4l[:, k, :, :].rearrange("p t b -> p (t b)")
                            last = split3(PS[:, FL, m * FT:(m + 1) * FT], wzh[:, k, w], wzl[:, k, w], z_h, z_l,
                                          m == 0 and k == 0, False, skip_group_check=True)
                    last.then_inc(r_zw, 1)
                if 1 <= r <= 4:
                    t = r - 1
                    wait(pe, r_h, 4 * J + t + 1)
                    for m in range(DH):
                        for k in range(DH):
                            last = pe.matmul(PS[:, FL, m * FT + t * B:m * FT + (t + 1) * B],
                                             whT[:, k, m * P:(m + 1) * P], hid[:, k, :], start=False,
                                             stop=t == NQ - 1, skip_group_check=True)
                    last.then_inc(r_mm, 1)
                if r == 5:
                    wait(pe, r_o, NQ + 4 * J + 4)
                    for j in range(2):
                        for m in range(DH):
                            src = o4[:, m, 2 * j:2 * j + 2, :].rearrange("p t b -> p (t b)")
                            last = pe.transpose(PS[:, FL, j * D + m * P:j * D + (m + 1) * P], src, ident[:, :])
                    last.then_inc(r_tr, 1)

            for F in range(2):
                for r in range(6):
                    front_pe(r, F)
            with pe.Fori(0, NT // 2 - 1) as i:
                for c in range(CH):
                    front_pe(c % 6, 2 + 4 * i + c // 6)
                    moe_pe(c, i)
            for c in range(CH):
                if c < 12:
                    front_pe(c % 6, NF - 2 + c // 6)
                moe_pe(c, NT // 2 - 1)
            for c in range(CH):
                moe_pe(c, NT // 2)
            with pe.Fori(0, NT // 2 - 1) as k:
                for c in range(CH):
                    rec_pe(c % 6, 4 * k + c // 6)
                    moe_pe(c, NT // 2 + 1 + k)
            for J in range(L // NQ - 4, L // NQ):
                for r in range(6):
                    rec_pe(r, J)


_INS = ['x', 'cond_1024', 'L0_cond_conv_b', 'L0_cond_Wp', 'L0_cond_bp', 'L0_cond_Ws', 'L0_cond_bs', 'L0_cond_A_log',
        'L0_cond_dt_log', 'L0_cond_Wo', 'L0_cond_bo', 'L1_cond_W_f', 'L1_cond_b_f', 'L1_cond_W_i', 'L1_cond_b_i',
        'L1_cond_W_h', 'L1_cond_b_h', 'L2_cond_W_router', 'L2_cond_router_bias', 'L2_cond_s_w1', 'L2_cond_s_w3',
        'L2_cond_s_w2', 'L2_cond_r_w1', 'L2_cond_r_w2', 'L3_cond_W', 'L3_cond_b', 'L3_cond_alpha']


def kernel(**inputs):
    import numpy as _np
    import concourse.bacc as _bacc
    from concourse import mybir as _mybir
    from concourse.bass_utils import run_bass_kernel_spmd as _run

    nc = _bacc.Bacc("TRN2", target_bir_lowering=False, num_devices=1, dynamic_dma_scratch_size=1024)
    arrays, args = {}, []
    for name in _INS:
        a = _np.ascontiguousarray(inputs[name])
        arrays[f"in_{name}_dram"] = a
        args.append(nc.dram_tensor(f"in_{name}_dram", a.shape, _mybir.dt.from_np(a.dtype), kind="ExternalInput").ap())
    args.append(nc.dram_tensor("out_0_dram", (B, L, D), _mybir.dt.float32, kind="ExternalOutput").ap())
    layered_blocks_kernel(nc, *args)
    r = _run(nc, [arrays], core_ids=[0])
    return r.results[0]["out_0_dram"]
```

```python
import concourse.bass as bass
from concourse import mybir
from contextlib import ExitStack

B, L, D, N = 64, 64, 256, 64
TOK = B * L
P = 128
DH = D // P
HALF = B // 2
TILE = 512
NT = TOK // TILE
TB = TILE // L
NE = 8
HS, HR = 512, 256
NSH = 2
SHC = NSH * HS // P
RC = NE * HR // P
CH = SHC + RC
GRP = 2 * SHC + RC
FT = 256
FB = FT // L
NF = TOK // FT
LAG = 3
EPS = 1e-8
NQ = 4
TH = TILE // (B // 2)
NP = NT + 1
KEPT = (NT // 2 - 2) * TH // NQ
NTAIL = TH // 2 // NQ


def layered_blocks_kernel(nc, x, cond, conv_b, Wp, bp, Ws, bs, A_log, dt_log, Wo, bo,
                          W_f, b_f, W_i, b_i, W_h, b_h, W_router, router_bias,
                          s_w1, s_w3, s_w2, r_w1, r_w2, W3, b3, alpha, out):
    f32, f32r, bf16 = mybir.dt.float32, mybir.dt.float32r, mybir.dt.bfloat16
    ALU, ACT, AX = mybir.AluOpType, mybir.ActivationFunctionType, mybir.AxisListType

    padded = nc.dram_tensor("cond_padded", (2 * L, D), f32, kind="Internal").ap()

    ctx = ExitStack()
    with ctx:
        def sb(name, shape, dt=f32, where=ctx):
            return where.enter_context(nc.sbuf_tensor(name, shape, dt))

        def sem(name):
            return ctx.enter_context(nc.semaphore(name))

        xT = sb("xT", [P, DH, TOK])
        with ExitStack() as o:
            Xs = sb("Xs", [P, B, P], where=o)
        with ExitStack() as o:
            convT = sb("convT", [P, NT, DH, TILE], where=o)
            dec = sb("dec", [P, FT], where=o)
            wrt = sb("wrt", [P, DH, NE], where=o)
            cl = sb("cl", [B, 2, NE], f32r, o)
        u_ctx = ExitStack()
        with u_ctx as o:
            with ExitStack() as o1:
                x1h = sb("x1h", [P, DH, FT], f32r, o1)
                x1l = sb("x1l", [P, DH, FT], f32r, o1)
                gates = sb("gates", [P, 2, DH, FT], f32, o1)
                fgt = gates[:, 0]
                inp = gates[:, 1]
                cnd = sb("cnd", [P, DH, FT], f32, o1)
                gsum = sb("gsum", [P, DH, FT], f32, o1)
                rcp = sb("rcp", [P, DH, FT], f32, o1)
            with ExitStack() as o2:
                z4s = sb("z4", [P, 2, DH, NQ, B], f32, o2)
                z4h = sb("z4h", [P, DH, NQ, B], f32r, o2)
                z4l = sb("z4l", [P, DH, NQ, B], f32r, o2)
                o4 = sb("o4", [P, DH, NQ, B], f32, o2)
                ost = sb("ost", [P, 2, D], f32, o2)
                th = sb("th", [P, DH, B], f32, o2)
                uz = sb("uz", [P, DH, B], f32, o2)
                hl = sb("hl", [P, DH, B], f32, o2)
                hid = sb("hid", [P, DH, B], f32, o2)
            keep = sb("u_l1_place", [P, 7 * DH * FT], f32, o)
            act_g = sb("act_g", [P, 2, TILE], f32, o)
            hbuf = sb("hbuf", [P, 2, TILE], f32, o)
            hh = sb("hh", [P, LAG, TILE], f32r, o)
            hlo = sb("hlo", [P, LAG, TILE], f32r, o)
        place = sb("u_place", [P, max(B * P, 7 * DH * FT + 4 * TILE + 2 * LAG * TILE)])
        with ExitStack() as o:
            Tz = sb("Tz", [P, L, P], f32, o)
            convS = sb("convS", [P, P, B], f32, o)
        with ExitStack() as o:
            o.enter_context(nc.sbuf_tensor("tz_place", [P, L * P], f32))
            sel = sb("sel", [B, (NT // 2 + 1) * TILE], f32r, o)
            rows = sb("rows", [19, P], f32, o)
            condN = sb("condN", [B, D], f32, o)
            wrN = sb("wrN", [NE, 2 * D], f32, o)
            zrow = sb("zrow", [L, D], f32, o)
        with ExitStack() as o:
            zth = sb("zth", [P, DH, NTAIL * NQ, B], f32r, o)
            ztl = sb("ztl", [P, DH, NTAIL * NQ, B], f32r, o)
            ot = sb("ot", [P, DH, NTAIL * NQ, B], f32, o)
            ostt = sb("ostt", [P, 2, 2, D], f32, o)
        w13h = sb("w13h", [P, DH, 2 * NSH * HS], f32r)
        w13l = sb("w13l", [P, DH, 2 * NSH * HS], f32r)
        rw1h = sb("rw1h", [P, DH, NE * HR], f32r)
        rw1l = sb("rw1l", [P, DH, NE * HR], f32r)
        w2h = sb("w2h", [P, SHC + RC, D], f32r)
        w2l = sb("w2l", [P, SHC + RC, D], f32r)
        with ExitStack() as o:
            stage = sb("stage", [P, 2, 4 * D], f32, o)
        with ExitStack() as o:
            rt = sb("rt", [P, 6, 4 * NE], f32, o)
            pair = sb("pair", [P, 2, 4, NE * NE], f32, o)
            r4 = sb("r4", [P, 4, 4], f32, o)
            gg = sb("gg", [P, 4, 2 * NE], f32r, o)
            gT = sb("gT", [2 * NE, TILE], f32r, o)
        stage_place = sb("stage_place", [P, 8 * D])
        with ExitStack() as o:
            pb = sb("pb", [P, 2, FT], f32, o)
            ct = sb("ct", [P, 2, FT], f32, o)
            ys = sb("ys", [P, 2, FT], f32, o)
            ab = sb("ab", [P, FT], f32, o)
            bu = sb("bu", [P, FT], f32, o)
        xh = sb("xh", [P, DH, TILE], f32r)
        xl = sb("xl", [P, DH, TILE], f32r)
        with ExitStack() as o:
            oh = sb("oh", [P, DH, (L // NQ - NTAIL - KEPT) * NQ, B], f32, o)
        w1h = sb("w1h", [P, DH, 3 * D], f32r)
        w1l = sb("w1l", [P, DH, 3 * D], f32r)
        wzh = sb("wzh", [P, DH, D], f32r)
        wzl = sb("wzl", [P, DH, D], f32r)
        whT = sb("whT", [P, DH, D])
        with ExitStack() as o:
            esel = sb("esel", [2 * NE, NE, P], f32r, o)
        wq = sb("wq", [P, DH, 3, 3 * N])
        wo2 = sb("wo2", [P, 2, D])
        starts = sb("starts", [P, DH * FT], bf16)
        carry = sb("carry", [P, DH * FT], bf16)
        ident = sb("ident", [P, P])
        cols = sb("cols", [P, 19])
        sc = sb("sc", [P, 12])
        condT = sb("condT", [P, DH, B])
        wr2 = sb("wr2", [P, DH, 2, NE], f32r)
        teA = sb("teA", [P, NT // 2, 4 * NE])
        teB = sb("teB", [P, 4 * NE])
        rb = sb("rb", [P, 4, NE])
        lm = sb("lm", [P, NE, NE])
        PS = ctx.enter_context(nc.psum_tensor("PS", [P, 8, 512], f32))
        del keep, place, stage_place

        LO = [4, 5]
        O = [0, 1]
        ROT = [2, 3, 4, 5]
        G = 6
        FL = 7
        GATE = [G, ROT[3]]

        xv = xT[:, :, :].rearrange("p h (b t) -> p h b t", t=L)

        def weight_stages():
            r = lambda w: w.rearrange("(r p) n -> p r n", p=P)
            st = []
            for e in range(NE // 2):
                st.append(("rw2", e, [r(r_w2[2 * e + i]) for i in range(2)]))
            for e in range(NSH):
                st.append(("w2", e, [r(s_w2[e])]))
            st.append(("l1a", 0, [r(W_f), r(W_i)]))
            st.append(("l1b", 0, [r(W_h), r(W3[:, D:2 * D])]))
            st.append(("l3h", 0, [r(W3[:, 0:D])]))
            for w, nm in ((s_w1, "w1"), (s_w3, "w3")):
                for e in range(NSH):
                    st.append((nm, e, [r(w[e])]))
            for e in range(NE // 2):
                st.append(("rw1", e, [r(r_w1[2 * e + i]) for i in range(2)]))
            return st

        STAGES = weight_stages()
        NSTG = len(STAGES)

        def stage_dst(k, half):
            nm, e, _ = STAGES[k]
            if nm == "rw2":
                c = SHC + 2 * (2 * e + half)
                return w2h[:, c:c + 2, :], w2l[:, c:c + 2, :], 2
            if nm == "w2":
                c = 4 * e + 2 * half
                return w2h[:, c:c + 2, :], w2l[:, c:c + 2, :], 2
            if nm == "l1a":
                return w1h[:, half, 0:512], w1l[:, half, 0:512], 1
            if nm == "w1":
                return w13h[:, half, e * HS:(e + 1) * HS], w13l[:, half, e * HS:(e + 1) * HS], 1
            if nm == "w3":
                q = NSH * HS + e * HS
                return w13h[:, half, q:q + HS], w13l[:, half, q:q + HS], 1
            return rw1h[:, half, e * 512:(e + 1) * 512], rw1l[:, half, e * 512:(e + 1) * 512], 1

        def stage_blocks(k, half):
            nm = STAGES[k][0]
            if nm == "rw2":
                return [(2 * half + r, kc) for kc in range(2) for r in range(2)]
            if nm == "w2":
                return [(r, 2 * half + kc) for kc in range(2) for r in range(2)]
            if nm == "l3h":
                return [(r, kc) for kc in range(2) for r in range(2)]
            return [(r, half) for r in range(4)]

        def stage_view(k):
            nm = STAGES[k][0]
            if nm == "w2":
                return stage[:, k % 2, :].rearrange("p (r n) -> p r n", r=2)
            return stage[:, k % 2, :].rearrange("p (r n) -> p r n", r=4)

        ORDER = [("x", j) for j in range(16)]
        ORDER += [("rows", 0), ("cond", 0), ("rtr", 0), ("cl", 0), ("te", 0)]
        early = [("w", (k, h)) for k in range(9) for h in range(1 if STAGES[k][0] == "l3h" else 2)]
        late = [("w", (k, h)) for k in range(9, NSTG) for h in range(2)]
        for g in range(16):
            ORDER.append(("conv", g))
            if g >= 4:
                ORDER += early[:1]
                early = early[1:]
        ORDER += early
        ORDER += [("ct", g) for g in range(16)] + [("bpe", 0)]
        N_EARLY = len(ORDER)
        ORDER += late
        BANKED = [j for j in ORDER if j[0] != "conv"]

        def bank_of(n):
            if BANKED[n] in late:
                i = late.index(BANKED[n])
                return FL if i < 12 and i % 2 else G
            return 4 + n % 4

        def finisher(job):
            kind, j = job
            if kind in ("x", "ct", "conv") and j % 2 == 0 and not (kind == "x" and j < 8):
                return "A"
            return "D"

        def signals(job):
            kind, j = job
            if kind == "w":
                return (0, 1) if STAGES[j[0]][0] == "l3h" else (1, 1)
            return (1, 0) if finisher(job) == "A" else (0, 1)

        A_AT, D_AT = {}, {}
        a = d = 0
        for job in ORDER:
            a += signals(job)[0]
            d += signals(job)[1]
            A_AT[job], D_AT[job] = a, d
        LAST_EARLY = ORDER[N_EARLY - 1]

        s_in = {n: sem("s_in_" + n) for n in ("t", "pad", "rows", "cond", "wr", "l0", "rb")}
        s_inx = [sem(f"s_in_x{q}") for q in range(4)]
        s_stg = [sem(f"s_stg{i}") for i in range(2)]
        s_tz = sem("s_tz")
        s_cl = sem("s_cl")
        s_cst = sem("s_cst")
        s_zero = sem("s_zero")
        s_tp = sem("s_tp")
        s_cv = sem("s_cv")
        s_av = sem("s_av")
        s_dv = sem("s_dv")
        s_par = sem("s_par")
        s_pa = sem("s_pa")
        l_pj = sem("l_pj")
        l_wo = sem("l_wo")
        l_a1 = sem("l_a1")
        l_ln = sem("l_ln")
        l_d = sem("l_d")
        l_x = sem("l_x")
        f_hi, f_lo, f_mm, f_ev = sem("f_hi"), sem("f_lo"), sem("f_mm"), sem("f_ev")
        f_sg, f_s, f_r, f_p = sem("f_sg"), sem("f_s"), sem("f_r"), sem("f_p")
        f_fn, f_S, f_P, f_w = sem("f_fn"), sem("f_S"), sem("f_P"), sem("f_w")
        f_qs, f_C, f_x2 = sem("f_qs"), sem("f_C"), sem("f_x2")
        m_xh, m_xl = sem("m_xh"), sem("m_xl")
        m_rt, m_gtr, m_bc = sem("m_rt"), sem("m_gtr"), sem("m_bc")
        m_l1, m_w2 = sem("m_l1"), sem("m_w2")
        m_act, m_hi, m_mul, m_lo, m_o = sem("m_act"), sem("m_hi"), sem("m_mul"), sem("m_lo"), sem("m_o")
        m_es, m_la = sem("m_es"), sem("m_la")
        m_lg, m_sig, m_rd, m_gsb = sem("m_lg"), sem("m_sig"), sem("m_rd"), sem("m_gsb")
        r_z, r_zh, r_zl, r_zw = sem("r_z"), sem("r_zh"), sem("r_zl"), sem("r_zw")
        r_mm, r_th, r_u, r_v, r_h = sem("r_mm"), sem("r_th"), sem("r_u"), sem("r_v"), sem("r_h")
        r_hl, r_o, r_tr, r_st, r_out = sem("r_hl"), sem("r_o"), sem("r_tr"), sem("r_st"), sem("r_out")

        t_zh, t_zl, t_mm, t_th = sem("t_zh"), sem("t_zl"), sem("t_mm"), sem("t_th")
        t_u, t_tr, t_st = sem("t_u"), sem("t_tr"), sem("t_st")
        t_out = [sem(f"t_out{i}") for i in range(2)]

        block = ctx.enter_context(nc.Block())

        def wait(eng, s, v):
            if isinstance(v, int) and v <= 0:
                return
            eng.wait_ge(s, v)

        def flat(ap):
            return ap.rearrange("p h n -> p (h n)")

        NCST = 13
        IDENT = 2
        ZEROED = 5

        def xsl(t0, n):
            return xT[:, :, t0:t0 + n] if isinstance(t0, int) else xT[:, :, bass.ds(t0, n)]

        ROUTER_AT = 2

        FRONT_AT = [0, 5, 11, 17]
        SPLIT_AT = [0, 4, 10, 16]

        def fronts_at(c, n=4):
            split = [(0, f) for f in range(n) if c == SPLIT_AT[f]]
            return [(c - FRONT_AT[f], f) for f in range(n) if 1 <= c - FRONT_AT[f] <= 6] + split

        def beside_l0(t):
            return late[3 * t:3 * t + 3] if t < 4 else late[8 + t:9 + t]

        def l0_slots(t):
            return {3: [0], 4: [1, 2, 3, 4], 5: [5, 6], 6: [7, 8, 9, 10], 7: [11]}.get(t, [])

        S_TAIL = L - NTAIL * NQ
        TR = [G, FL]
        ROWS_AT = {0: 0, 1: 1, 3: 2, 4: 3, 5: 4, 6: 5, 7: 6}
        N_OUT = L // NQ - KEPT

        def tail_z(b):
            t0 = S_TAIL + NQ * b
            return xv[:, :, :, t0:t0 + NQ].rearrange("p h b t -> p h t b")

        def front_ready(F):
            if isinstance(F, int):
                return 4 + 2 * (F // 2) + 2
            return 4 + 2 * NT

        def width(half):
            return TILE if half is None else FT

        def part(row, half):
            if half is None:
                return row
            return row.rearrange("p (b t) -> p b t", t=TH)[:, :, half * TH // 2:(half + 1) * TH // 2]

        def rec_at(c, k, half):
            if half is None:
                return [(c % 6, 4 * k + c // 6, c // 6 % 2)]
            J = 4 * k + 3 * half + c // 8
            at = {1: [(1, J)], 3: [(2, J)], 5: [(3, J), (0, J + 1)], 7: [(4, J)]}.get(c % 8, [])
            if c == 0 and half == 0:
                at = [(0, J)]
            return [(r, j, j % 2) for r, j in at if j < L // NQ - NTAIL]

        def tile_x(T, kind):
            if kind == "A":
                return xsl(T * TILE, TILE)
            if isinstance(T, int):
                k = 16 * (T - NT // 2)
                return xv[:, :, HALF:B, k:k + 16]
            return xv[:, :, HALF:B, bass.ds(16 * (T - NT // 2), 16)]

        def tile_buf(buf, kind):
            v = buf[:, :, :]
            return v if kind == "A" else v.rearrange("p h (b t) -> p h b t", t=16)

        def transposed_src(job, bank):
            return PS[:, bank, :].rearrange("p (b h s) -> p h b s", b=4, h=2)

        def transposed_dst(job):
            kind, j = job
            if kind == "x":
                return xv[:, :, 4 * j:4 * j + 4, :]
            v = convT[:, j // 2].rearrange("p h (b t) -> p h b t", t=L)
            j = j % 2
            return v[:, :, 4 * j:4 * j + 4, ::-1]

        def weight_parts(kh, bank, part):
            k, half = kh
            nm = STAGES[k][0]
            src = PS[:, bank, :]
            if nm == "l1b":
                return [((w1h, w1l)[part][:, half, 2 * D:3 * D], src[:, 0:D]),
                        ((wzh, wzl)[part][:, half, :], src[:, D:2 * D])]
            dst = stage_dst(k, half)
            if dst[2] == 2:
                src = src.rearrange("p (c n) -> p c n", c=2)
            return [(dst[part], src)]

        @block.sync
        def _(sp):
            sp.sem_inc(r_out, 32)
            def load_x(q):
                for h in range(DH):
                    sp.dma_start(Xs[h * L:(h + 1) * L, q * 16:(q + 1) * 16, :],
                                 x[q * 16:(q + 1) * 16, :, h * P:(h + 1) * P].rearrange("b s d -> s b d"))\
                      .then_inc(s_inx[q], 16)

            load_x(0)
            sp.dma_start(padded[0:L, :], cond).then_inc(s_in["pad"], 16)
            sp.wait_ge(s_zero, 1)
            sp.dma_start(padded[L:2 * L, :], zrow[:, :]).then_inc(s_in["pad"], 16)
            for q in range(1, 4):
                load_x(q)
            sp.wait_ge(s_in["pad"], 32)
            for h in range(DH):
                for s0, n in ((0, L), (L // 2, L // 2)):
                    src = bass.AP(padded.tensor, s0 * D + h * P, [[D, L // 2], [D, n], [1, P]])
                    sp.dma_start(Tz[h * L + s0:h * L + s0 + L // 2, 0:n, :], src).then_inc(s_in["t"], 16)
            sp.wait_ge(s_cst, ZEROED)
            for k in range(NSTG):
                if k == 2:
                    for q, src in enumerate((Wp[:, 0:N], Wp[:, N:2 * N], Ws)):
                        sp.dma_start(wq[:, :, q, N:2 * N], src.rearrange("(k p) n -> p k n", p=P))\
                          .then_inc(s_in["l0"], 16)
                    for q in range(2):
                        sp.dma_start(wo2[q * N:(q + 1) * N, q, :], Wo).then_inc(s_in["l0"], 16)
                    sp.dma_start(rb[:, :, :], bass.AP(router_bias.tensor, 0, [[0, P], [0, 4], [1, NE]]))\
                      .then_inc(s_in["rb"], 16)
                nm, _, srcs = STAGES[k]
                if k >= 2:
                    sp.wait_ge(s_tp, max(n + 1 for n, j in enumerate(BANKED)
                                         if j[0] == "w" and j[1][0] == k - 2))
                view = stage_view(k)
                r0 = 0
                for s in srcs:
                    sp.dma_start(view[:, r0:r0 + s.shape[1], :], s).then_inc(s_stg[k % 2], 16)
                    r0 += s.shape[1]

            def store(J):
                wait(sp, r_st, 1 + J + 1)
                for tp in range(2):
                    if isinstance(J, int):
                        dst = out[:, 4 * J + 2 * tp:4 * J + 2 * tp + 2, :]
                    else:
                        dst = out[:, bass.ds(4 * J + 2 * tp, 2), :]
                    sp.dma_start(dst.rearrange("b t d -> b (t d)"),
                                 ost[tp * B:(tp + 1) * B, :, :].rearrange("p t d -> p (t d)")).then_inc(r_out, 16)

            with sp.Fori(0, KEPT) as J:
                store(J)
            for b in range(N_OUT):
                sp.wait_ge(t_st, b + 1)
                for tp in range(2):
                    t = NQ * (KEPT + b) + 2 * tp
                    sp.dma_start(out[:, t:t + 2, :].rearrange("b t d -> b (t d)"),
                                 ostt[tp * B:(tp + 1) * B, b % 2, :, :].rearrange("p t d -> p (t d)"))\
                      .then_inc(t_out[b % 2], 16)
            sp.wait_ge(r_out, 32 + 32 * KEPT)
            for q in range(2):
                sp.wait_ge(t_out[q], 32 * (N_OUT // 2))

        @block.gpsimd
        def _(pool):
            n = [0]
            pool.sem_inc(r_o, 2 * NQ)

            def made(ins):
                n[0] += 1
                ins.then_inc(s_cst, 1)
                return n[0]

            def after(k):
                pool.wait_ge(s_cst, k)

            pool.memset(zrow[:, :], 0.0).then_inc(s_zero, 1)
            made(pool.memset(ident[:, :], 0.0))
            after(1)
            made(pool.affine_select(out=ident[:, :], in_=ident[:, :], compare_op=ALU.not_equal, fill=1.0,
                                    base=0, pattern=[[-1, P]], channel_multiplier=1))
            made(pool.memset(sel[:, :].bitcast(f32), 1.0))
            made(pool.memset(wq[:, :, :, :], 0.0))
            made(pool.memset(wo2[:, :, :], 0.0))
            made(pool.memset(lm[:, :, :], 1.0))
            made(pool.memset(starts[:, :], 0.0))
            made(pool.memset(carry[:, :], 1.0))
            after(8)
            sv = starts[:, :].rearrange("p (s t) -> p s t", t=L)
            made(pool.affine_select(out=sv, in_=sv, compare_op=ALU.not_equal, fill=1.0,
                                    base=0, pattern=[[0, DH * FB], [1, L]], channel_multiplier=0))
            cv = carry[:, :].rearrange("p (s t) -> p s t", t=L)
            made(pool.affine_select(out=cv, in_=cv, compare_op=ALU.not_equal, fill=0.0,
                                    base=0, pattern=[[0, DH * FB], [1, L]], channel_multiplier=0))
            made(pool.affine_select(out=lm[:, :, :], in_=lm[:, :, :], compare_op=ALU.is_ge, fill=0.0,
                                    base=-1, pattern=[[1, NE], [-1, NE]], channel_multiplier=0))
            after(11)
            nA = NT // 2 * TB
            sA = sel[:, 0:NT // 2 * TILE].rearrange("p (b t) -> p b t", t=L)
            sB = sel[:, NT // 2 * TILE:].rearrange("p (b t) -> p b t", t=16)
            made(pool.affine_select(out=sA, in_=sA.bitcast(f32), compare_op=ALU.is_equal, fill=0.0,
                                    base=0, pattern=[[-1, nA], [0, L]], channel_multiplier=1))
            made(pool.affine_select(out=sB, in_=sB.bitcast(f32), compare_op=ALU.is_equal, fill=0.0,
                                    base=-HALF, pattern=[[-1, HALF], [0, 16]], channel_multiplier=1))
            assert n[0] == NCST

            def front_pool(r, F):
                if r == 3:
                    wait(pool, f_ev, 3 * F + 3)
                    wait(pool, f_sg, F + 1)
                    pool.tensor_tensor(out=flat(cnd[:, :, :]), in0=flat(cnd[:, :, :]), in1=flat(inp[:, :, :]),
                                       op=ALU.mult).then_inc(f_p, 1)
                    wait(pool, f_r, 2 * F + 1)
                    pool.tensor_tensor(out=fgt[:, 0, :], in0=fgt[:, 0, :], in1=rcp[:, 0, :], op=ALU.mult)
                if r == 4:
                    wait(pool, f_r, 2 * F + 2)
                    pool.tensor_tensor(out=fgt[:, 1, :], in0=fgt[:, 1, :], in1=rcp[:, 1, :],
                                       op=ALU.mult).then_inc(f_p, 1)
                    wait(pool, f_p, 3 * F + 1)
                    pool.tensor_tensor(out=flat(cnd[:, :, :]), in0=flat(cnd[:, :, :]), in1=flat(rcp[:, :, :]),
                                       op=ALU.mult).then_inc(f_p, 1)
                if r == 5:
                    wait(pool, f_P, F + 1)
                    for h in range(DH):
                        v = rcp[:, h, :].rearrange("p (b t) -> p b t", t=L)
                        h0 = h0s[:, h, bass.ds(FB * F, FB)] if not isinstance(F, int) else h0s[:, h, FB * F:FB * F + FB]
                        last = pool.tensor_tensor(out=v, in0=v, in1=h0.unsqueeze(2).broadcast_to([P, FB, L]),
                                                  op=ALU.mult)
                    last.then_inc(f_w, 1)
                    wait(pool, f_w, 2 * F + 1)
                    pool.tensor_tensor(out=rcp[:, :, :], in0=xsl(F * FT, FT), in1=rcp[:, :, :],
                                       op=ALU.add).then_inc(f_w, 1)

            h0s = condT
            pool.wait_ge(s_dv, D_AT[("cond", 0)])
            for F in range(2):
                for r in range(6):
                    front_pool(r, F)
            with pool.Fori(0, NT // 2 - 1) as i:
                for f in range(4):
                    for r in range(6):
                        front_pool(r, 2 + 4 * i + f)
            for f in range(2):
                for r in range(6):
                    front_pool(r, NF - 2 + f)

            def rec_pool(r, J, u):
                z4 = z4s[:, u]
                if r == 0:
                    wait(pool, r_zh, J + 1)
                    wait(pool, r_z, J + 1)
                    wait(pool, r_zw, 1 + J)
                    pool.tensor_tensor(out=z4l[:, :, :, :].rearrange("p h t b -> p (h t b)"),
                                       in0=z4[:, :, :, :].rearrange("p h t b -> p (h t b)"),
                                       in1=z4h[:, :, :, :].bitcast(f32).rearrange("p h t b -> p (h t b)"),
                                       op=ALU.subtract).then_inc(r_zl, 1)
                if 1 <= r <= 4:
                    t = r - 1
                    wait(pool, r_h, 4 * J + t + 1)
                    wait(pool, r_v, 1 + 4 * J + t)
                    pool.tensor_tensor(out=hl[:, :, :], in0=hid[:, :, :], in1=leak(), op=ALU.mult).then_inc(r_hl, 1)
                    if t > 0:
                        out_row(J, t - 1, z4)
                if r == 5:
                    wait(pool, r_h, 4 * J + NQ + 1)
                    out_row(J, NQ - 1, z4)

            def leak():
                return cols_leak.unsqueeze(2).broadcast_to([P, DH, B])

            def out_row(J, t, z4):
                q = 2 * (t % 2) + t // 2
                if isinstance(J, int):
                    dst = oh[:, :, NQ * (J - KEPT) + q, :]
                else:
                    dst = o4[:, :, q, :]
                    if t == 0:
                        wait(pool, r_tr, 1 + J)
                pool.tensor_tensor(out=dst, in0=z4[:, :, t, :], in1=hid[:, :, :], op=ALU.add)\
                    .then_inc(r_o, 1)

            def tail_row(s):
                t = s % NQ
                pool.tensor_tensor(out=ot[:, :, s - t + 2 * (t % 2) + t // 2, :], in0=tail_z(s // NQ)[:, :, t, :],
                                   in1=hid[:, :, :], op=ALU.add).then_inc(r_o, 1)

            cols_leak = sc[:, 6:8]
            with pool.Fori(0, KEPT // 2) as i:
                for u in range(2):
                    for r in range(6):
                        rec_pool(r, 2 * i + u, u)
            rec_pool(0, KEPT, KEPT % 2)
            for J in range(KEPT, L // NQ - NTAIL):
                for r in (1, 2, 3, 0, 4, 5):
                    j = J + (r == 0)
                    if j < L // NQ - NTAIL:
                        rec_pool(r, j, j % 2)

            for b in range(NTAIL):
                for t in range(NQ):
                    s = S_TAIL + NQ * b + t
                    pool.wait_ge(r_h, s + 1)
                    pool.wait_ge(r_v, 1 + s)
                    pool.tensor_tensor(out=hl[:, :, :], in0=hid[:, :, :], in1=leak(), op=ALU.mult).then_inc(r_hl, 1)
                    if b or t:
                        tail_row(NQ * b + t - 1)
            pool.wait_ge(r_h, L + 1)
            tail_row(NTAIL * NQ - 1)

        @block.scalar
        def _(act):
            act.sem_inc(l_a1, 4)
            act.sem_inc(m_act, CH)
            act.sem_inc(m_hi, CH)
            act.sem_inc(r_st, 1)
            act.dma_start(condN[:, :], cond).then_inc(s_in["cond"], 16)
            act.dma_start(wrN[:, :], W_router).then_inc(s_in["wr"], 16)
            vecs = [(0, bp[0:N], 1), (1, bp[N:2 * N], 1), (2, bs, 1), (3, A_log, 1), (4, dt_log, 1)]
            for r, v, _ in vecs:
                act.dma_start(rows[r:r + 1, :].rearrange("o (q n) -> o q n", q=2),
                              v.rearrange("(o n) -> o n", o=1).unsqueeze(1).broadcast_to([1, 2, N]))\
                   .then_inc(s_in["rows"], 16)
            for r, v in ((5, conv_b), (7, bo), (9, b_f), (11, b_i), (13, b_h), (15, b3), (17, alpha)):
                act.dma_start(rows[r:r + 2, :], v.rearrange("(h p) -> h p", h=2)).then_inc(s_in["rows"], 16)
            def evacuate(job):
                kind, j = job
                if kind == "conv":
                    if finisher(job) == "A":
                        act.wait_ge(s_cv, j + 1)
                        act.activation(convS[:, 8 * j:8 * j + 8, :].rearrange("p c b -> p (c b)"),
                                       PS[:, j % 4, :], ACT.Copy).then_inc(s_av, 1)
                    return
                n = BANKED.index(job)
                bank = bank_of(n)
                if kind in ("x", "ct") and finisher(job) == "A":
                    act.wait_ge(s_tp, n + 1)
                    act.activation(transposed_dst(job), transposed_src(job, bank), ACT.Copy).then_inc(s_av, 1)
                if kind == "w" and signals(job)[0]:
                    act.wait_ge(s_tp, n + 1)
                    for dst, src in weight_parts(j, bank, 0):
                        last = act.activation(dst, src, ACT.Copy)
                    last.then_inc(s_av, 1)

            for job in ORDER[:ORDER.index(("conv", 0))]:
                evacuate(job)
            act.wait_ge(s_par, 1)
            act.activation(sc[:, 0:2], sc[:, 0:2], ACT.Exp, scale=-1.0).then_inc(s_pa, 1)
            act.wait_ge(s_pa, 1)
            act.activation(sc[:, 0:2], sc[:, 0:2], ACT.Ln, bias=1.0).then_inc(s_pa, 1)
            for job in ORDER[ORDER.index(("conv", 0)):N_EARLY]:
                evacuate(job)

            def l0_act(t, p, between):
                wait(act, l_pj, 2 * t + 1)
                wait(act, l_d, 5 * t + 5)
                act.activation(pb[:, p, :], PS[:, p, 0:FT], ACT.Identity, bias=sc[:, 2:3]).then_inc(l_a1, 1)
                act.activation(ct[:, p, :], PS[:, p, FT:2 * FT], ACT.Tanh, bias=sc[:, 3:4]).then_inc(l_a1, 1)
                evacuate(between)
                wait(act, l_d, 5 * t + 10 + 1)
                act.activation(ab[:, :], ab[:, :], ACT.Exp, scale=-1.0).then_inc(l_ln, 1)
                wait(act, l_ln, 2 * t + 1)
                act.activation(ab[:, :], ab[:, :], ACT.Ln, bias=1.0).then_inc(l_ln, 1)

            def front_act(r, F):
                if r == 0:
                    wait(act, l_x, front_ready(F))
                    wait(act, f_mm, 3 * F)
                    act.activation(x1h[:, :, :], xsl(F * FT, FT), ACT.Copy).then_inc(f_hi, 1)
                if r in (1, 2, 3):
                    q = r - 1
                    wait(act, f_mm, 3 * F + q + 1)
                    if q == 0:
                        wait(act, f_P, F)
                    if q == 1:
                        wait(act, f_p, 3 * F)
                    if q == 2:
                        wait(act, f_C, F)
                    buf = (fgt, inp, cnd)[q]
                    for m in range(DH):
                        last = act.activation(buf[:, m, :], PS[:, FL, m * FT:(m + 1) * FT], ACT.Identity,
                                              bias=cols[:, 9 + 2 * q + m:10 + 2 * q + m])
                    last.then_inc(f_ev, 1)
                    if q == 1:
                        wait(act, f_ev, 3 * F + 2)
                        both = gates[:, :, :, :].rearrange("p q h n -> p (q h n)")
                        act.activation(both, both, ACT.Sigmoid).then_inc(f_sg, 1)

            def split_act(T, kind):
                wait(act, f_x2, 2 * T + 2 if kind == "A" else NF)
                wait(act, m_l1, GRP + GRP * T)
                wait(act, m_rt, 1 + T)
                src, dst = tile_x(T, kind), tile_buf(xh, kind)
                act.activation(dst, src, ACT.Copy).then_inc(m_xh, 1)

            def moe_act(c, T, nxt, half=None):
                w = width(half)
                if c > 0:
                    hi(c - 1, T, w)
                wait(act, m_l1, GRP + GRP * T + (2 * c + 1 if c < SHC else c + SHC + 1))
                wait(act, m_mul, CH * T + CH + c - 1)
                bank = ROT[2 * c % 4] if c < SHC else ROT[(c - SHC) % 3]
                act.activation(act_g[:, c % 2, 0:w], PS[:, bank, 0:w], ACT.Silu if c < SHC else ACT.Gelu)\
                   .then_inc(m_act, 1)
                if c == ROUTER_AT and half != 1:
                    wait(act, m_lg, T + 1)
                    act.activation(rt[:, 1, :], rt[:, 0, :], ACT.Sigmoid).then_inc(m_sig, 1)
                if c == CH - 1:
                    if nxt:
                        split_act(T + 1, nxt)
                    hi(c, T, w)

            def hi(c, T, w):
                wait(act, m_mul, CH * T + CH + c + 1)
                wait(act, m_w2, CH * T + CH + c - LAG + 1)
                act.activation(hh[:, c % LAG, 0:w], hbuf[:, c % 2, 0:w], ACT.Copy).then_inc(m_hi, 1)

            def rec_act(r, J, u, tiles):
                z4 = z4s[:, u]
                if r == 0:
                    wait(act, m_o, tiles)
                    wait(act, r_o, NQ * (J + 1))
                    wait(act, r_zw, 1 + J)
                    src = xv[:, :, :, 4 * J:4 * J + 4] if isinstance(J, int) else xv[:, :, :, bass.ds(4 * J, 4)]
                    src = src.rearrange("p h b t -> p h t b")
                    for h in range(DH):
                        last = act.activation(z4[:, h, :, :], src[:, h, :, :], ACT.Copy)
                    last.then_inc(r_z, 1)
                    wait(act, r_z, J + 1)
                    act.activation(z4h[:, :, :, :].rearrange("p h t b -> p (h t b)"),
                                   z4[:, :, :, :].rearrange("p h t b -> p (h t b)"), ACT.Copy).then_inc(r_zh, 1)
                if 1 <= r <= 4:
                    t = r - 1
                    wait(act, r_mm, 4 * J + t + 1)
                    for m in range(DH):
                        last = act.activation(th[:, m, :], PS[:, FL, m * FT + t * B:m * FT + (t + 1) * B], ACT.Tanh,
                                              bias=sc[:, 8 + m:9 + m], scale=0.5)
                    last.then_inc(r_th, 1)
                if r == 5:
                    wait(act, r_tr, 1 + J + 1)
                    wait(act, r_out, 32 + 32 * J)
                    act.activation(ost[:, :, :].rearrange("p t d -> p (t d)"), PS[:, FL, :], ACT.Copy)\
                       .then_inc(r_st, 1)

            def tail_rows(b):
                act.wait_ge(t_tr, b + 1)
                if b >= 2:
                    act.wait_ge(t_out[b % 2], 32 * (b // 2))
                act.activation(ostt[:, b % 2, :, :].rearrange("p t d -> p (t d)"), PS[:, TR[b % 2], :], ACT.Copy)\
                   .then_inc(t_st, 1)

            def rec_act2(r, J):
                if 1 <= r <= 4:
                    t = r - 1
                    wait(act, r_v, 1 + 4 * J + t + 1)
                    wait(act, r_hl, 4 * J + t + 1)
                    wait(act, r_o, 2 * NQ + 4 * J + t)
                    act.activation(hid[:, :, :], uz[:, :, :], ACT.Tanh).then_inc(r_h, 1)

            act.wait_ge(s_par, 5)
            for t in range(NT):
                jobs, slots = beside_l0(t), l0_slots(t)
                l0_act(t, t % 2, jobs[0])
                for c in slots[:2]:
                    front_act(c % 6, c // 6)
                for job in jobs[1:]:
                    evacuate(job)
                for c in slots[2:]:
                    front_act(c % 6, c // 6)
            act.wait_ge(l_d, 10 + 5 * NT)
            split_act(0, "A")
            with act.Fori(0, NT // 2 - 1) as i:
                for c in range(CH):
                    moe_act(c, i, "A")
                    for r, f in fronts_at(c):
                        front_act(r, 2 + 4 * i + f)
            for c in range(CH):
                moe_act(c, NT // 2 - 1, "B")
                for r, f in fronts_at(c, 2):
                    front_act(r, NF - 2 + f)
            for c in range(CH):
                moe_act(c, NT // 2, "B")

            def rec_tile(k, nxt, half=None):
                for c in range(CH):
                    moe_act(c, NT // 2 + 1 + k + (half or 0), nxt, half)
                    for r, J, u in rec_at(c, k, half):
                        done = NT // 2 + 1 + k
                        if half is not None and J >= 4 * (k + 1):
                            done += 1
                        rec_act(r, J, u, 2 * done + 2)
                        rec_act2(r, J)

            with act.Fori(0, NT // 2 - 2) as k:
                rec_tile(k, "B")
            for half in range(2):
                rec_tile(NT // 2 - 2, None, half)

            def tail_split(b):
                for h in range(DH):
                    last = act.activation(zth[:, h, NQ * b:NQ * (b + 1), :], tail_z(b)[:, h, :, :], ACT.Copy)
                last.then_inc(t_zh, 1)

            act.wait_ge(m_o, 2 + 2 * NP)
            tail_split(0)
            for b in range(NTAIL):
                for t in range(NQ):
                    s = NQ * b + t
                    for m in range(DH):
                        act.wait_ge(t_mm, DH * s + m + 1)
                        act.activation(th[:, m, :], PS[:, ROT[2 * (b % 2) + m], t * B:(t + 1) * B], ACT.Tanh,
                                       bias=sc[:, 8 + m:9 + m], scale=0.5).then_inc(t_th, 1)
                    act.wait_ge(r_v, 1 + S_TAIL + s + 1)
                    act.wait_ge(r_hl, S_TAIL + s + 1)
                    act.wait_ge(r_o, 2 * NQ + S_TAIL + s)
                    act.activation(hid[:, :, :], uz[:, :, :], ACT.Tanh).then_inc(r_h, 1)
                    if t == 0 and b + 1 < NTAIL:
                        tail_split(b + 1)
                    if s in ROWS_AT:
                        tail_rows(ROWS_AT[s])
            tail_rows(N_OUT - 1)

        @block.vector
        def _(dve):
            dve.sem_inc(l_d, 10)
            dve.sem_inc(l_x, 4)
            dve.sem_inc(m_mul, CH)
            dve.sem_inc(m_lo, CH)
            dve.sem_inc(m_o, 2)
            dve.sem_inc(r_v, 1)

            def evacuate(job):
                kind, j = job
                if kind == "conv":
                    if finisher(job) == "D":
                        dve.wait_ge(s_cv, j + 1)
                        dve.tensor_copy(convS[:, 8 * j:8 * j + 8, :].rearrange("p c b -> p (c b)"),
                                        PS[:, j % 4, :]).then_inc(s_dv, 1)
                    return
                if finisher(job) != "D":
                    return
                n = BANKED.index(job)
                bank = bank_of(n)
                dve.wait_ge(s_tp, n + 1)
                b = PS[:, bank, :]
                if kind in ("x", "ct"):
                    dve.tensor_copy(transposed_dst(job), transposed_src(job, bank)).then_inc(s_dv, 1)
                elif kind == "rows":
                    dve.tensor_copy(cols[:, :], b[:, 0:19]).then_inc(s_dv, 1)
                elif kind == "cond":
                    dve.tensor_copy(condT[:, :, :], b[:, 0:2 * B].rearrange("p (h b) -> p h b", h=2)).then_inc(s_dv, 1)
                elif kind == "rtr":
                    v = b[:, 0:4 * NE].rearrange("p (k e) -> p k e", k=4)
                    dve.tensor_copy(wr2[:, :, 0, :], v[:, 0:2, :]).then_inc(s_par, 1)
                    dve.tensor_copy(wrt[:, :, :], v[:, 2:4, :])
                    dve.wait_ge(s_par, 2)
                    dve.tensor_tensor(out=wr2[:, :, 1, :], in0=v[:, 0:2, :], in1=wr2[:, :, 0, :].bitcast(f32),
                                      op=ALU.subtract).then_inc(s_dv, 1)
                elif kind == "cl":
                    dve.tensor_copy(cl[:, 0, :], PS[0:B, bank, 0:NE]).then_inc(s_cl, 1)
                    dve.wait_ge(s_cl, 1)
                    dve.tensor_tensor(out=cl[:, 1, :], in0=PS[0:B, bank, 0:NE], in1=cl[:, 0, :].bitcast(f32),
                                      op=ALU.subtract).then_inc(s_dv, 1)
                elif kind == "te":
                    v = b[:, 0:8 * NE * (NT // 2 + 1)].rearrange("p (g s e) -> p g e s", s=2, e=NE)
                    nA = 4 * (NT // 2)
                    dve.tensor_reduce(out=teA[:, :, :].rearrange("p a (g e) -> p (a g) e", e=NE), in_=v[:, 0:nA],
                                      op=ALU.add, axis=AX.X)
                    dve.tensor_reduce(out=teB[:, :].rearrange("p (g e) -> p g e", e=NE), in_=v[:, nA:nA + 4],
                                      op=ALU.add, axis=AX.X).then_inc(s_dv, 1)
                elif kind == "bpe":
                    dve.tensor_tensor(out=sc[:, 2:4], in0=b[:, 0:2], in1=cols[:, 0:2], op=ALU.add).then_inc(s_dv, 1)
                elif kind == "w":
                    if STAGES[j[0]][0] == "l3h":
                        dve.tensor_copy(whT[:, :, :], b.rearrange("p (k n) -> p k n", k=2)).then_inc(s_dv, 1)
                        return
                    dve.wait_ge(s_av, A_AT[job])
                    for (hi_, src), (lo_, _) in zip(weight_parts(j, bank, 0), weight_parts(j, bank, 1)):
                        last = dve.tensor_tensor(out=lo_, in0=src, in1=hi_.bitcast(f32), op=ALU.subtract)
                    last.then_inc(s_dv, 1)

            for h in range(DH):
                dve.memset(Tz[h * L + L // 2:(h + 1) * L, L // 2:L, :], 0.0).then_inc(s_tz, 1)
            for job in ORDER[:ORDER.index(("rows", 0)) + 1]:
                evacuate(job)
            dve.wait_ge(s_dv, D_AT[("rows", 0)])
            dve.scalar_tensor_tensor(out=sc[:, 0:2], in0=cols[:, 3:5], scalar=-1.0, in1=cols[:, 3:5],
                                     op0=ALU.mult, op1=ALU.max).then_inc(s_par, 1)
            for job in ORDER[ORDER.index(("rows", 0)) + 1:ORDER.index(("conv", 0))]:
                evacuate(job)
            dve.tensor_scalar(sc[:, 6:8], cols[:, 17:19], -1.0, 1.0, ALU.mult, ALU.add)
            dve.tensor_scalar(sc[:, 8:10], cols[:, 15:17], 0.5, None, ALU.mult)
            dve.wait_ge(s_pa, 2)
            dve.scalar_tensor_tensor(out=sc[:, 4:6], in0=cols[:, 3:5], scalar=0.0, in1=sc[:, 0:2],
                                     op0=ALU.max, op1=ALU.add).then_inc(s_par, 1)
            dve.wait_ge(s_par, 3)
            dve.scalar_tensor_tensor(out=sc[:, 10:11], in0=sc[:, 4:5], scalar=-1.0, in1=sc[:, 5:6],
                                     op0=ALU.mult, op1=ALU.mult).then_inc(s_par, 1)
            dve.wait_ge(s_par, 4)
            dve.tensor_scalar(sc[:, 10:11], sc[:, 10:11], 1.0, None, ALU.add).then_inc(s_par, 1)
            dve.wait_ge(s_par, 5)
            dve.wait_ge(s_cst, NCST)
            dve.tensor_scalar(dec[:, :], carry[:, 0:FT], sc[:, 10:11], None, ALU.mult).then_inc(s_par, 1)
            for job in ORDER[ORDER.index(("conv", 0)):N_EARLY]:
                evacuate(job)

            def l0_x(t):
                for m in range(DH):
                    wait(dve, l_wo, 4 + 2 * t + m + 1)
                    xs = xT[:, m, t * TILE:(t + 1) * TILE]
                    dve.scalar_tensor_tensor(out=xs, in0=PS[:, LO[m], :], scalar=cols[:, 7 + m:8 + m],
                                             in1=xs, op0=ALU.add, op1=ALU.add).then_inc(l_x, 1)

            def l0_dve(t, p, between):
                wait(dve, l_a1, 4 + 2 * t + 1)
                dve.scalar_tensor_tensor(out=ab[:, :], in0=pb[:, p, :], scalar=-1.0, in1=pb[:, p, :],
                                         op0=ALU.mult, op1=ALU.max).then_inc(l_d, 1)
                evacuate(between)
                if t:
                    l0_x(t - 1)
                wait(dve, l_ln, 2 * t + 2)
                dve.scalar_tensor_tensor(out=bu[:, :], in0=pb[:, p, :], scalar=0.0, in1=ab[:, :],
                                         op0=ALU.max, op1=ALU.add).then_inc(l_d, 1)
                wait(dve, l_d, 10 + 5 * t + 2)
                wait(dve, l_pj, 2 * t + 2)
                dve.scalar_tensor_tensor(out=bu[:, :], in0=PS[:, 2 + p, 0:FT], scalar=cols[:, 2:3],
                                         in1=bu[:, :], op0=ALU.add, op1=ALU.mult).then_inc(l_d, 1)
                wait(dve, l_d, 10 + 5 * t + 3)
                wait(dve, l_wo, 2 * t + 2)
                dve.tensor_tensor_scan(out=ys[:, p, :], data0=dec[:, :], data1=bu[:, :], initial=0.0,
                                       op0=ALU.mult, op1=ALU.add).then_inc(l_d, 1)
                wait(dve, l_d, 10 + 5 * t + 4)
                wait(dve, l_a1, 4 + 2 * t + 2)
                dve.scalar_tensor_tensor(out=ys[:, p, :], in0=ys[:, p, :], scalar=sc[:, 5:6], in1=ct[:, p, :],
                                         op0=ALU.mult, op1=ALU.mult).then_inc(l_d, 1)

            dve.wait_ge(s_in["rb"], 16)
            dve.wait_ge(s_par, 6)

            def front_dve(r, F):
                if r == 0:
                    wait(dve, f_hi, F + 1)
                    wait(dve, f_mm, 3 * F)
                    dve.tensor_tensor(out=x1l[:, :, :], in0=xsl(F * FT, FT), in1=x1h[:, :, :].bitcast(f32),
                                      op=ALU.subtract).then_inc(f_lo, 1)
                if r == 3:
                    wait(dve, f_sg, F + 1)
                    dve.scalar_tensor_tensor(out=flat(gsum[:, :, :]), in0=flat(fgt[:, :, :]), scalar=EPS,
                                             in1=flat(inp[:, :, :]), op0=ALU.add, op1=ALU.add).then_inc(f_s, 1)
                    wait(dve, f_s, F + 1)
                    wait(dve, f_w, 2 * F)
                    dve.reciprocal(rcp[:, 0, :], gsum[:, 0, :]).then_inc(f_r, 1)
                if r == 4:
                    dve.reciprocal(rcp[:, 1, :], gsum[:, 1, :]).then_inc(f_r, 1)
                if r == 5:
                    wait(dve, f_p, 3 * F + 2)
                    dve.tensor_scalar(flat(fgt[:, :, :]), flat(fgt[:, :, :]), EPS, 1.0, ALU.add, ALU.min)\
                       .then_inc(f_fn, 1)
                    wait(dve, f_fn, F + 1)
                    dve.tensor_tensor_scan(out=flat(gsum[:, :, :])[:, ::-1], data0=starts[:, :],
                                           data1=flat(fgt[:, :, :])[:, ::-1], initial=0.0,
                                           op0=ALU.max, op1=ALU.mult).then_inc(f_S, 1)
                    wait(dve, f_p, 3 * F + 3)
                    dve.tensor_tensor_scan(out=flat(rcp[:, :, :]), data0=starts[:, :], data1=flat(fgt[:, :, :]),
                                           initial=0.0, op0=ALU.max, op1=ALU.mult).then_inc(f_P, 1)
                if r == 6:
                    wait(dve, f_S, F + 1)
                    dve.tensor_tensor(out=flat(cnd[:, :, :]), in0=flat(cnd[:, :, :]), in1=flat(gsum[:, :, :]),
                                      op=ALU.mult).then_inc(f_qs, 1)
                    wait(dve, f_qs, F + 1)
                    dve.tensor_tensor_scan(out=flat(gsum[:, :, :]), data0=carry[:, :], data1=flat(cnd[:, :, :]),
                                           initial=0.0, op0=ALU.mult, op1=ALU.add).then_inc(f_C, 1)
                    wait(dve, f_C, F + 1)
                    wait(dve, f_w, 2 * F + 2)
                    dve.tensor_tensor(out=xsl(F * FT, FT), in0=rcp[:, :, :], in1=gsum[:, :, :],
                                      op=ALU.add).then_inc(f_x2, 1)

            K_RD = 14

            def router_logits(T, kind):
                lg = rt[:, 0, :]
                v3 = lambda a: a.rearrange("p (g e) -> p g e", g=4)
                wait(dve, m_rt, 1 + T + 1)
                te = teB[:, :] if kind == "B" else (teA[:, T, :] if isinstance(T, int) else
                                                    teA[:, bass.ds(T, 1), :].rearrange("p a b -> p (a b)"))
                xr = PS[:, G, 0:8 * NE].rearrange("p (g s e) -> p g s e", g=4, s=2)
                dve.tensor_tensor(out=v3(lg), in0=xr[:, :, 0, :], in1=v3(te), op=ALU.add).then_inc(m_la, 1)
                wait(dve, m_la, T + 1)
                dve.tensor_tensor(out=v3(lg), in0=xr[:, :, 1, :], in1=v3(lg), op=ALU.add).then_inc(m_lg, 1)

            def router_dve(T, third):
                base = K_RD * T
                k = [(0, 5, 9)[third]]

                def step(ins):
                    k[0] += 1
                    ins.then_inc(m_rd, 1)

                def prev():
                    wait(dve, m_rd, base + k[0])

                s, selv, rank, sm, mk = (rt[:, q, :] for q in range(1, 6))
                den, rc, hc, one = (r4[:, q, :] for q in range(4))
                v3 = lambda a: a.rearrange("p (g e) -> p g e", g=4)
                if third == 0:
                    wait(dve, m_sig, T + 1)
                    step(dve.tensor_tensor(out=selv, in0=s, in1=rb[:, :, :].rearrange("p g e -> p (g e)"), op=ALU.add))
                    prev()
                    for g in range(4):
                        row = v3(selv)[:, g, :]
                        sj = row.unsqueeze(1).broadcast_to([P, NE, NE])
                        se = row.unsqueeze(2).broadcast_to([P, NE, NE])
                        pg = [pair[:, q, g, :].rearrange("p (e j) -> p e j", e=NE) for q in range(2)]
                        dve.tensor_tensor(out=pg[0], in0=sj, in1=se, op=ALU.is_gt)
                        last = dve.tensor_tensor(out=pg[1], in0=sj, in1=se, op=ALU.is_equal)
                    step(last)
                    prev()
                    lmb = lm[:, :, :].rearrange("p e j -> p (e j)").unsqueeze(1).broadcast_to([P, 4, NE * NE])
                    step(dve.tensor_tensor(out=pair[:, 1, :, :], in0=pair[:, 1, :, :], in1=lmb, op=ALU.mult))
                    prev()
                    step(dve.tensor_tensor(out=pair[:, 0, :, :], in0=pair[:, 0, :, :], in1=pair[:, 1, :, :], op=ALU.add))
                    prev()
                    step(dve.tensor_reduce(out=rank, in_=pair[:, 0, :, :].rearrange("p g (e j) -> p (g e) j", j=NE),
                                           op=ALU.add, axis=AX.X))
                if third == 1:
                    prev()
                    dve.tensor_scalar(mk, rank, 1.5, None, ALU.is_lt)
                    step(dve.scalar_tensor_tensor(out=sm, in0=rank, scalar=1.5, in1=s, op0=ALU.is_lt, op1=ALU.mult))
                    prev()
                    step(dve.tensor_reduce(out=den, in_=v3(sm), op=ALU.add, axis=AX.X))
                    prev()
                    dve.tensor_scalar(one, den, 1e-9, None, ALU.is_gt)
                    step(dve.tensor_scalar(rc, den, 1e-9, None, ALU.add))
                    prev()
                    dve.tensor_scalar(hc, one, -0.5, 0.5, ALU.mult, ALU.add)
                    step(dve.reciprocal(rc, rc))
                if third == 2:
                    prev()
                    step(dve.tensor_tensor(out=rc, in0=rc, in1=one, op=ALU.mult))
                    prev()
                    dve.tensor_tensor(out=v3(mk), in0=v3(mk), in1=hc.unsqueeze(2).broadcast_to([P, 4, NE]), op=ALU.mult)
                    step(dve.tensor_tensor(out=v3(sm), in0=v3(sm), in1=rc.unsqueeze(2).broadcast_to([P, 4, NE]), op=ALU.mult))
                    prev()
                    step(dve.tensor_tensor(out=sm, in0=sm, in1=mk, op=ALU.add))
                    prev()
                    step(dve.tensor_copy(gg[:, :, 0:NE], v3(sm)))
                    prev()
                    step(dve.tensor_tensor(out=gg[:, :, NE:2 * NE], in0=v3(sm), in1=gg[:, :, 0:NE].bitcast(f32),
                                           op=ALU.subtract))
                assert k[0] == (5, 9, K_RD)[third]

            def lo(c, T, w):
                wait(dve, m_hi, CH * T + CH + c + 1)
                wait(dve, m_w2, CH * T + CH + c - LAG + 1)
                dve.tensor_tensor(out=hlo[:, c % LAG, 0:w], in0=hbuf[:, c % 2, 0:w],
                                  in1=hh[:, c % LAG, 0:w].bitcast(f32),
                                  op=ALU.subtract).then_inc(m_lo, 1)

            def split_dve(T, kind):
                wait(dve, m_xh, T + 1)
                src, dst = tile_x(T, kind), tile_buf(xl, kind)
                for h in range(DH):
                    last = dve.tensor_tensor(out=dst[:, h], in0=src[:, h],
                                             in1=tile_buf(xh, kind)[:, h].bitcast(f32), op=ALU.subtract)
                last.then_inc(m_xl, 1)

            def moe_dve(c, T, kind, nxt, between=None, half=None):
                w = width(half)
                if c == SHC - 1 and half != 1:
                    wait(dve, m_gtr, T + 1)
                    dve.tensor_copy(gT[:, :], PS[0:2 * NE, G, :]).then_inc(m_gsb, 1)
                if c > 0:
                    lo(c - 1, T, w)
                wait(dve, m_act, CH * T + CH + c + 1)
                if c < SHC:
                    wait(dve, m_l1, GRP + GRP * T + 2 * c + 2)
                    dve.scalar_tensor_tensor(out=hbuf[:, c % 2, 0:w], in0=act_g[:, c % 2, 0:w], scalar=1.0 / NSH,
                                             in1=PS[:, ROT[(2 * c + 1) % 4], 0:w], op0=ALU.mult, op1=ALU.mult)\
                       .then_inc(m_mul, 1)
                else:
                    wait(dve, m_bc, NE * T + (c - SHC) // 2 + 1)
                    dve.tensor_tensor(out=hbuf[:, c % 2, 0:w], in0=act_g[:, c % 2, 0:w],
                                      in1=PS[:, GATE[(c - SHC) // 2 % 2], 0:w],
                                      op=ALU.mult).then_inc(m_mul, 1)
                if between and c < CH - 1:
                    between()
                if c == ROUTER_AT - 1 and half != 1:
                    router_logits(T, kind)
                if ROUTER_AT + 1 <= c <= ROUTER_AT + 3 and half != 1:
                    router_dve(T, c - ROUTER_AT - 1)
                if c == CH - 1:
                    lo(c, T, w)
                    if nxt:
                        split_dve(T + 1, nxt)
                    if between:
                        between()
                    wait(dve, m_w2, CH * T + CH + CH)
                    for m in range(DH):
                        xs = tile_x(min(T, NT - 1) if isinstance(T, int) else T, kind)[:, m]
                        o = PS[:, O[m], 0:w]
                        if half is not None:
                            xs = xv[:, m, HALF:B, L - TH + half * TH // 2:L - TH + (half + 1) * TH // 2]
                            o = o.rearrange("p (b t) -> p b t", t=TH // 2)
                        elif kind == "B":
                            o = o.rearrange("p (b t) -> p b t", t=TH)
                        dve.scalar_tensor_tensor(out=xs, in0=o, scalar=0.25, in1=xs,
                                                 op0=ALU.mult, op1=ALU.add).then_inc(m_o, 1)

            def rec_dve(r, J, u):
                z4 = z4s[:, u]
                if 1 <= r <= 4:
                    t = r - 1
                    wait(dve, r_th, 4 * J + t + 1)
                    dve.scalar_tensor_tensor(out=uz[:, :, :], in0=th[:, :, :], scalar=1.0, in1=z4[:, :, t, :],
                                             op0=ALU.add, op1=ALU.mult).then_inc(r_u, 1)
                    wait(dve, r_u, 4 * J + t + 1)
                    wait(dve, r_hl, 4 * J + t + 1)
                    dve.scalar_tensor_tensor(out=uz[:, :, :], in0=uz[:, :, :], scalar=0.5, in1=hl[:, :, :],
                                             op0=ALU.mult, op1=ALU.add).then_inc(r_v, 1)

            def front_slot(c, F0):
                front_dve(c % 6, F0 + c // 6)
                if c == 6:
                    front_dve(6, F0)
                if c == 11:
                    front_dve(6, F0 + 1)

            def fronts(c, F0, n=4):
                for r, f in fronts_at(c, n)[::-1]:
                    if (r, c) == (5, CH - 2):
                        continue
                    if (r, c) == (6, CH - 1):
                        front_dve(5, F0 + f)
                    front_dve(r, F0 + f)

            for t in range(NT):
                jobs, slots = beside_l0(t), l0_slots(t)
                l0_dve(t, t % 2, jobs[0])
                for c in slots[:2]:
                    front_slot(c, 0)
                for job in jobs[1:]:
                    evacuate(job)
                for c in slots[2:]:
                    front_slot(c, 0)
            l0_x(NT - 1)
            split_dve(0, "A")
            dve.tensor_tensor(out=esel[:, :, :], in0=ident[0:2 * NE, 0:NE].unsqueeze(2).broadcast_to([2 * NE, NE, P]),
                              in1=ident[0:2 * NE, NE:2 * NE].unsqueeze(2).broadcast_to([2 * NE, NE, P]),
                              op=ALU.add).then_inc(m_es, 1)
            with dve.Fori(0, NT // 2 - 1) as i:
                for c in range(CH):
                    moe_dve(c, i, "A", "A", lambda: fronts(c, 2 + 4 * i))
            for c in range(CH):
                moe_dve(c, NT // 2 - 1, "A", "B", lambda: fronts(c, NF - 2, 2))
            for c in range(CH):
                if c == 1:
                    dve.tensor_copy(hid[:, :, :], condT[:, :, :]).then_inc(r_h, 1)
                moe_dve(c, NT // 2, "B", "B")

            def rec_tile(k, nxt, half=None):
                def recurrence(c):
                    for r, J, u in rec_at(c, k, half):
                        rec_dve(r, J, u)

                for c in range(CH):
                    moe_dve(c, NT // 2 + 1 + k + (half or 0), "B", nxt, lambda: recurrence(c), half)

            with dve.Fori(0, NT // 2 - 2) as k:
                rec_tile(k, "B")
            for half in range(2):
                rec_tile(NT // 2 - 2, None, half)

            def tail_split(b):
                dve.wait_ge(t_zh, b + 1)
                q = slice(NQ * b, NQ * (b + 1))
                for h in range(DH):
                    last = dve.tensor_tensor(out=ztl[:, h, q, :], in0=tail_z(b)[:, h, :, :],
                                             in1=zth[:, h, q, :].bitcast(f32), op=ALU.subtract)
                last.then_inc(t_zl, 1)

            tail_split(0)
            for b in range(NTAIL):
                for t in range(NQ):
                    s = NQ * b + t
                    for m in range(DH):
                        dve.wait_ge(t_th, DH * s + m + 1)
                        dve.scalar_tensor_tensor(out=uz[:, m, :], in0=th[:, m, :], scalar=1.0,
                                                 in1=tail_z(b)[:, m, t, :], op0=ALU.add, op1=ALU.mult)\
                           .then_inc(t_u, 1)
                    dve.wait_ge(t_u, DH * (s + 1))
                    dve.wait_ge(r_hl, S_TAIL + s + 1)
                    dve.scalar_tensor_tensor(out=uz[:, :, :], in0=uz[:, :, :], scalar=0.5, in1=hl[:, :, :],
                                             op0=ALU.mult, op1=ALU.add).then_inc(r_v, 1)
                    if t == 0 and b + 1 < NTAIL:
                        tail_split(b + 1)

        @block.tensor
        def _(pe):
            pe.sem_inc(l_wo, 4)
            pe.sem_inc(m_w2, CH)
            pe.sem_inc(m_l1, GRP)
            pe.sem_inc(m_rt, 1)
            pe.sem_inc(r_zw, 1)
            pe.sem_inc(r_tr, 1)

            def free_bank(job):
                kind, j = job
                if kind == "conv":
                    same = [("conv", j - 4)] if j >= 4 else []
                else:
                    n = BANKED.index(job)
                    same = [BANKED[n - 4]] if n >= 4 else []
                    if job in late:
                        i = late.index(job)
                        same = [late[i - 2 if i <= 12 else i - 1]] if i >= 2 else []
                for old in same:
                    if finisher(old) == "A":
                        pe.wait_ge(s_av, A_AT[old])
                    else:
                        pe.wait_ge(s_dv, D_AT[old])

            def split3(o, wh, wl, bh, bl, first, last, **kw):
                pe.matmul(o, wh, bh, start=first, stop=False, **kw)
                pe.matmul(o, wh, bl, start=False, stop=False, **kw)
                return pe.matmul(o, wl, bh, start=False, stop=last, **kw)

            waited = set()

            def once(s, name, v):
                if name not in waited:
                    waited.add(name)
                    pe.wait_ge(s, v)

            def setup_pe(job):
                kind, j = job
                free_bank(job)
                if kind == "conv":
                    once(s_in["t"], "t", 64)
                    once(s_tz, "tz", DH)
                    for c in range(8):
                        ch = 8 * j + c
                        for h in range(DH):
                            q = slice(h * L, (h + 1) * L)
                            last = pe.matmul(PS[q, j % 4, c * B:(c + 1) * B], Tz[q, :, ch], Xs[q, :, ch],
                                             start=True, stop=True)
                    last.then_inc(s_cv, 1)
                    return
                n = BANKED.index(job)
                b = PS[:, bank_of(n), :]
                if kind == "rows":
                    once(s_in["rows"], "rows", 16 * 12)
                    last = pe.transpose(b[:, 0:19], rows[:, :], ident[0:19, 0:19])
                elif kind == "cond":
                    once(s_in["cond"], "cond", 16)
                    for h in range(DH):
                        last = pe.transpose(b[:, h * B:(h + 1) * B], condN[:, h * P:(h + 1) * P], ident[0:B, 0:B])
                elif kind == "rtr":
                    once(s_in["wr"], "wr", 16)
                    for k in range(4):
                        last = pe.transpose(b[:, k * NE:(k + 1) * NE], wrN[:, k * P:(k + 1) * P], ident[0:NE, 0:NE])
                elif kind == "cl":
                    pe.wait_ge(s_dv, D_AT[("rtr", 0)])
                    for k in range(DH):
                        last = pe.matmul(PS[0:B, bank_of(n), 0:NE], condT[:, k, :], wrt[:, k, :],
                                         start=k == 0, stop=k == DH - 1)
                elif kind == "te":
                    pe.wait_ge(s_dv, D_AT[("cl", 0)])
                    pe.wait_ge(s_cst, NCST)
                    for g in range(4 * (NT // 2 + 1)):
                        last = pe.matmul(b[:, 2 * g * NE:2 * (g + 1) * NE], sel[:, g * P:(g + 1) * P],
                                         cl[:, :, :].rearrange("b s e -> b (s e)"), start=True, stop=True)
                elif kind == "bpe":
                    once(s_in["l0"], "l0", 16 * 5)
                    for q in range(2):
                        for th_ in range(2):
                            for k in range(DH):
                                last = pe.matmul(b[:, q:q + 1], wq[:, k, q, (1 - th_) * N:(1 - th_) * N + P],
                                                 cols[:, 5 + k:6 + k], start=th_ == 0 and k == 0,
                                                 stop=th_ == 1 and k == DH - 1)
                elif kind in ("x", "ct"):
                    if kind == "x":
                        once(s_cst, "ident", IDENT)
                        once(s_inx[j // 4], f"x{j // 4}", 32)
                    else:
                        once(s_av, "cvA", A_AT[("conv", 14)])
                        once(s_dv, "cvD", D_AT[("conv", 15)])
                    for i in range(4):
                        bt = 4 * j + i
                        src = Xs[:, bt, :] if kind == "x" else convS[:, :, bt]
                        last = pe.transpose(b[:, i * P:(i + 1) * P], src, ident[:, :])
                elif kind == "w":
                    k, half = j
                    if half == 0:
                        cnt = 16 * sum(len(STAGES[q][2]) for q in range(k % 2, k + 1, 2))
                        pe.wait_ge(s_stg[k % 2], cnt)
                    v = stage_view(k)
                    for i, (r, kc) in enumerate(stage_blocks(k, half)):
                        last = pe.transpose(b[:, i * P:(i + 1) * P], v[:, r, kc * P:(kc + 1) * P], ident[:, :])
                last.then_inc(s_tp, 1)

            for job in ORDER[:N_EARLY]:
                setup_pe(job)

            def l0_proj(t, p):
                def rhs(q, k, th_):
                    o = th_ * FT
                    return convT[:, t, k, o:o + FT] if q < 2 else xT[:, k, t * TILE + o:t * TILE + o + FT]

                wait(pe, l_a1, 2 * t + 2)
                for q in range(3):
                    if q == 2:
                        wait(pe, l_d, 5 * t + 3)
                    o = PS[:, p + 2 * (q // 2), (q % 2) * FT:(q % 2) * FT + FT]
                    n = 0
                    for k in range(DH):
                        for th_ in range(2):
                            n += 1
                            last = pe.matmul(o, wq[:, k, q, (1 - th_) * N:(1 - th_) * N + P],
                                             rhs(q, k, th_), start=n == 1, stop=n == 4)
                    if q:
                        last.then_inc(l_pj, 1)

            def l0_out(t, p):
                wait(pe, l_d, 10 + 5 * t + 5)
                wait(pe, l_x, 4 + 2 * t)
                for m in range(DH):
                    for th_ in range(2):
                        last = pe.matmul(PS[:, LO[m], th_ * FT:(th_ + 1) * FT],
                                         wo2[:, th_, m * P:(m + 1) * P], ys[:, p, :], start=True, stop=True)
                    last.then_inc(l_wo, 1)

            def front_pe(r, F):
                if r in (1, 2, 3):
                    q = r - 1
                    if q == 0:
                        wait(pe, f_hi, F + 1)
                        wait(pe, f_lo, F + 1)
                    wait(pe, f_ev, 3 * F + q)
                    for m in range(DH):
                        w = slice(q * D + m * P, q * D + (m + 1) * P)
                        for k in range(DH):
                            last = split3(PS[:, FL, m * FT:(m + 1) * FT], w1h[:, k, w], w1l[:, k, w],
                                          x1h[:, k, :], x1l[:, k, :], k == 0, k == DH - 1)
                    last.then_inc(f_mm, 1)

            def router_pe(T):
                wait(pe, m_mul, CH * T + CH - 2)
                for g in range(4):
                    o = 2 * NE * g
                    q = slice(g * P, (g + 1) * P)
                    for k in range(DH):
                        pe.matmul(PS[:, G, o:o + 2 * NE], xh[:, k, q], wr2[:, k, :, :].rearrange("p s e -> p (s e)"),
                                  start=k == 0, stop=False, skip_group_check=True)
                        last = pe.matmul(PS[:, G, o:o + NE], xl[:, k, q], wr2[:, k, 0, :], start=False,
                                         stop=k == DH - 1, skip_group_check=True)
                last.then_inc(m_rt, 1)

            def layer1(bank, wh, wl, w, half):
                for k in range(DH):
                    last = split3(PS[:, bank, 0:width(half)], wh[:, k, w], wl[:, k, w], part(xh[:, k, :], half),
                                  part(xl[:, k, :], half), k == 0, k == DH - 1)
                last.then_inc(m_l1, 1)

            def w2(c, T, n):
                wait(pe, m_lo, CH * T + CH + c + 1)
                if c == 0:
                    wait(pe, m_o, 2 * T + 2)
                for m in range(DH):
                    w = slice(m * P, (m + 1) * P)
                    last = split3(PS[:, O[m], 0:n], w2h[:, c, w], w2l[:, c, w], hh[:, c % LAG, 0:n], hlo[:, c % LAG, 0:n],
                                  c == 0, c == CH - 1, skip_group_check=True)
                last.then_inc(m_w2, 1)

            def moe_pe(c, T, half=None):
                n = width(half)
                if c == 0 and half != 1:
                    wait(pe, m_xh, T + 1)
                    wait(pe, m_xl, T + 1)
                if c < SHC:
                    wait(pe, m_act, CH * T + CH + max(c - 1, 0))
                    layer1(ROT[(2 * c) % 4], w13h, w13l, slice(c * P, (c + 1) * P), half)
                    if c:
                        wait(pe, m_mul, CH * T + CH + c - 1)
                    layer1(ROT[(2 * c + 1) % 4], w13h, w13l, slice((SHC + c) * P, (SHC + c + 1) * P), half)
                else:
                    g = c - SHC
                    if g == 1:
                        wait(pe, m_mul, CH * T + CH + SHC - 1)
                    else:
                        wait(pe, m_act, CH * T + CH + (SHC - 1, 0, SHC)[g] if g < 3 else CH * T + CH + c - 2)
                    layer1(ROT[g % 3], rw1h, rw1l, slice(g * P, (g + 1) * P), half)
                if c == 0 and half != 1:
                    router_pe(T)
                if c == SHC - 1 and half != 1:
                    wait(pe, m_rd, 14 * T + 14)
                    for g in range(4):
                        last = pe.transpose(PS[0:2 * NE, G, g * P:(g + 1) * P], gg[:, g, :].bitcast(f32), ident[:, :])
                    last.then_inc(m_gtr, 1)
                if c >= LAG:
                    w2(c - LAG, T, n)
                if c >= SHC and (c - SHC) % 2 == 0:
                    e = (c - SHC) // 2
                    if e == 0 and half != 1:
                        wait(pe, m_es, 1)
                        wait(pe, m_gsb, T + 1)
                    wait(pe, m_mul, CH * T + CH + c - 2)
                    pe.matmul(PS[:, GATE[e % 2], 0:n], esel[:, e, :], part(gT[:, :], half), start=True, stop=True).then_inc(m_bc, 1)
                if c == CH - 1:
                    for q in range(CH - LAG, CH):
                        w2(q, T, n)

            def rec_pe(r, J):
                if r == 0:
                    wait(pe, r_zl, J + 1)
                    wait(pe, r_zh, J + 1)
                    if isinstance(J, int) and J > KEPT:
                        wait(pe, r_h, 4 * J + 1)
                    else:
                        wait(pe, r_st, 1 + J)
                    for m in range(DH):
                        w = slice(m * P, (m + 1) * P)
                        for k in range(DH):
                            z_h = z4h[:, k, :, :].rearrange("p t b -> p (t b)")
                            z_l = z4l[:, k, :, :].rearrange("p t b -> p (t b)")
                            last = split3(PS[:, FL, m * FT:(m + 1) * FT], wzh[:, k, w], wzl[:, k, w], z_h, z_l,
                                          m == 0 and k == 0, False, skip_group_check=True)
                    last.then_inc(r_zw, 1)
                if 1 <= r <= 4:
                    t = r - 1
                    wait(pe, r_h, 4 * J + t + 1)
                    for m in range(DH):
                        for k in range(DH):
                            last = pe.matmul(PS[:, FL, m * FT + t * B:m * FT + (t + 1) * B],
                                             whT[:, k, m * P:(m + 1) * P], hid[:, k, :], start=False,
                                             stop=t == NQ - 1, skip_group_check=True)
                    last.then_inc(r_mm, 1)
                if r == 5:
                    wait(pe, r_o, 2 * NQ + 4 * J + 4)
                    for j in range(2):
                        for m in range(DH):
                            src = o4[:, m, 2 * j:2 * j + 2, :].rearrange("p t b -> p (t b)")
                            last = pe.transpose(PS[:, FL, j * D + m * P:j * D + (m + 1) * P], src, ident[:, :])
                    last.then_inc(r_tr, 1)

            pe.wait_ge(s_av, A_AT[LAST_EARLY])
            pe.wait_ge(s_dv, D_AT[LAST_EARLY])
            for t in range(NT):
                l0_proj(t, t % 2)
                jobs = beside_l0(t)
                setup_pe(jobs[0])
                slots = l0_slots(t)
                if t == 4:
                    pe.wait_ge(s_dv, D_AT[late[11]])
                for c in slots[:1]:
                    front_pe(c % 6, c // 6)
                if t:
                    l0_out(t - 1, 1 - t % 2)
                for c in slots[1:2]:
                    front_pe(c % 6, c // 6)
                for job in jobs[1:]:
                    setup_pe(job)
                for c in slots[2:]:
                    front_pe(c % 6, c // 6)
            l0_out(NT - 1, (NT - 1) % 2)
            pe.wait_ge(s_av, A_AT[ORDER[-1]])
            pe.wait_ge(s_dv, D_AT[ORDER[-1]])
            pe.wait_ge(l_x, 4 + 2 * NT)
            with pe.Fori(0, NT // 2 - 1) as i:
                for c in range(CH):
                    moe_pe(c, i)
                    for r, f in fronts_at(c):
                        front_pe(r, 2 + 4 * i + f)
            for c in range(CH):
                moe_pe(c, NT // 2 - 1)
                for r, f in fronts_at(c, 2):
                    front_pe(r, NF - 2 + f)
            for c in range(CH):
                moe_pe(c, NT // 2)

            def rec_tile(k, half=None):
                for c in range(CH):
                    moe_pe(c, NT // 2 + 1 + k + (half or 0), half)
                    for r, J, _ in rec_at(c, k, half):
                        if r == 1:
                            rec_pe(0, J)
                        if r:
                            rec_pe(r, J)

            with pe.Fori(0, NT // 2 - 2) as k:
                rec_tile(k)
            for half in range(2):
                rec_tile(NT // 2 - 2, half)

            def tail_z_product(b):
                pe.wait_ge(t_zl, b + 1)
                q = slice(NQ * b, NQ * (b + 1))
                for m in range(DH):
                    w = slice(m * P, (m + 1) * P)
                    for k in range(DH):
                        z_h = zth[:, k, q, :].rearrange("p t b -> p (t b)")
                        z_l = ztl[:, k, q, :].rearrange("p t b -> p (t b)")
                        split3(PS[:, ROT[2 * (b % 2) + m], 0:FT], wzh[:, k, w], wzl[:, k, w], z_h, z_l,
                               k == 0, False, skip_group_check=True)

            def tail_transposes(b):
                pe.wait_ge(r_o, 2 * NQ + NQ * (KEPT + b + 1))
                if b >= 2:
                    pe.wait_ge(t_st, b - 1)
                for j in range(2):
                    for m in range(DH):
                        rows_, n = (oh, b) if b < N_OUT - NTAIL else (ot, b - (N_OUT - NTAIL))
                        src = rows_[:, m, NQ * n + 2 * j:NQ * n + 2 * j + 2, :].rearrange("p t b -> p (t b)")
                        last = pe.transpose(PS[:, TR[b % 2], j * D + m * P:j * D + (m + 1) * P], src, ident[:, :])
                last.then_inc(t_tr, 1)

            tail_z_product(0)
            for b in range(NTAIL):
                for t in range(NQ):
                    pe.wait_ge(r_h, S_TAIL + NQ * b + t + 1)
                    for m in range(DH):
                        for k in range(DH):
                            last = pe.matmul(PS[:, ROT[2 * (b % 2) + m], t * B:(t + 1) * B],
                                             whT[:, k, m * P:(m + 1) * P], hid[:, k, :], start=False,
                                             stop=t == NQ - 1, skip_group_check=True)
                        last.then_inc(t_mm, 1)
                    if NQ * b + t in ROWS_AT:
                        tail_transposes(ROWS_AT[NQ * b + t])
                    if t == 2 and b + 1 < NTAIL:
                        tail_z_product(b + 1)
            tail_transposes(N_OUT - 1)


_INS = ['x', 'cond_1024', 'L0_cond_conv_b', 'L0_cond_Wp', 'L0_cond_bp', 'L0_cond_Ws', 'L0_cond_bs', 'L0_cond_A_log',
        'L0_cond_dt_log', 'L0_cond_Wo', 'L0_cond_bo', 'L1_cond_W_f', 'L1_cond_b_f', 'L1_cond_W_i', 'L1_cond_b_i',
        'L1_cond_W_h', 'L1_cond_b_h', 'L2_cond_W_router', 'L2_cond_router_bias', 'L2_cond_s_w1', 'L2_cond_s_w3',
        'L2_cond_s_w2', 'L2_cond_r_w1', 'L2_cond_r_w2', 'L3_cond_W', 'L3_cond_b', 'L3_cond_alpha']


def kernel(**inputs):
    import numpy as _np
    import concourse.bacc as _bacc
    from concourse import mybir as _mybir
    from concourse.bass_utils import run_bass_kernel_spmd as _run

    nc = _bacc.Bacc("TRN2", target_bir_lowering=False, num_devices=1, dynamic_dma_scratch_size=1024)
    arrays, args = {}, []
    for name in _INS:
        a = _np.ascontiguousarray(inputs[name])
        arrays[f"in_{name}_dram"] = a
        args.append(nc.dram_tensor(f"in_{name}_dram", a.shape, _mybir.dt.from_np(a.dtype), kind="ExternalInput").ap())
    args.append(nc.dram_tensor("out_0_dram", (B, L, D), _mybir.dt.float32, kind="ExternalOutput").ap())
    layered_blocks_kernel(nc, *args)
    r = _run(nc, [arrays], core_ids=[0])
    return r.results[0]["out_0_dram"]
```

```python
import concourse.bass as bass
from concourse import mybir
from contextlib import ExitStack

B, L, D, N = 64, 64, 256, 64
TOK = B * L
P = 128
DH = D // P
HALF = B // 2
TILE = 512
NT = TOK // TILE
TB = TILE // L
NE = 8
HS, HR = 512, 256
NSH = 2
SHC = NSH * HS // P
RC = NE * HR // P
CH = SHC + RC
GRP = 2 * SHC + RC
FT = 256
FB = FT // L
NF = TOK // FT
LAG = 3
EPS = 1e-8
NQ = 4
TH = TILE // (B // 2)
NP = NT + 1
KEPT = (NT // 2 - 2) * TH // NQ
NTAIL = TH // 2 // NQ


def layered_blocks_kernel(nc, x, cond, conv_b, Wp, bp, Ws, bs, A_log, dt_log, Wo, bo,
                          W_f, b_f, W_i, b_i, W_h, b_h, W_router, router_bias,
                          s_w1, s_w3, s_w2, r_w1, r_w2, W3, b3, alpha, out):
    f32, f32r, bf16 = mybir.dt.float32, mybir.dt.float32r, mybir.dt.bfloat16
    ALU, ACT, AX = mybir.AluOpType, mybir.ActivationFunctionType, mybir.AxisListType

    padded = nc.dram_tensor("cond_padded", (2 * L, D), f32, kind="Internal").ap()

    ctx = ExitStack()
    with ctx:
        def sb(name, shape, dt=f32, where=ctx):
            return where.enter_context(nc.sbuf_tensor(name, shape, dt))

        def sem(name):
            return ctx.enter_context(nc.semaphore(name))

        xT = sb("xT", [P, DH, TOK])
        with ExitStack() as o:
            Xs = sb("Xs", [P, B, P], where=o)
        with ExitStack() as o:
            convT = sb("convT", [P, NT, DH, TILE], where=o)
            dec = sb("dec", [P, FT], where=o)
            wrt = sb("wrt", [P, DH, NE], where=o)
            cl = sb("cl", [B, 2, NE], f32r, o)
        u_ctx = ExitStack()
        with u_ctx as o:
            with ExitStack() as o1:
                x1h = sb("x1h", [P, DH, FT], f32r, o1)
                x1l = sb("x1l", [P, DH, FT], f32r, o1)
                gates = sb("gates", [P, 2, DH, FT], f32, o1)
                fgt = gates[:, 0]
                inp = gates[:, 1]
                cnd = sb("cnd", [P, DH, FT], f32, o1)
                gsum = sb("gsum", [P, DH, FT], f32, o1)
                rcp = sb("rcp", [P, DH, FT], f32, o1)
            with ExitStack() as o2:
                z4s = sb("z4", [P, 2, DH, NQ, B], f32, o2)
                z4h = sb("z4h", [P, DH, NQ, B], f32r, o2)
                z4l = sb("z4l", [P, DH, NQ, B], f32r, o2)
                o4 = sb("o4", [P, DH, NQ, B], f32, o2)
                ost = sb("ost", [P, 2, D], f32, o2)
                th = sb("th", [P, DH, B], f32, o2)
                uz = sb("uz", [P, DH, B], f32, o2)
                hl = sb("hl", [P, DH, B], f32, o2)
                hid = sb("hid", [P, DH, B], f32, o2)
            keep = sb("u_l1_place", [P, 7 * DH * FT], f32, o)
            act_g = sb("act_g", [P, 2, TILE], f32, o)
            hbuf = sb("hbuf", [P, 2, TILE], f32, o)
            hh = sb("hh", [P, LAG, TILE], f32r, o)
            hlo = sb("hlo", [P, LAG, TILE], f32r, o)
        place = sb("u_place", [P, max(B * P, 7 * DH * FT + 4 * TILE + 2 * LAG * TILE)])
        with ExitStack() as o:
            Tz = sb("Tz", [P, L, P], f32, o)
            convS = sb("convS", [P, P, B], f32, o)
        with ExitStack() as o:
            o.enter_context(nc.sbuf_tensor("tz_place", [P, L * P], f32))
            sel = sb("sel", [B, (NT // 2 + 1) * TILE], f32r, o)
            rows = sb("rows", [19, P], f32, o)
            condN = sb("condN", [B, D], f32, o)
            wrN = sb("wrN", [NE, 2 * D], f32, o)
            zrow = sb("zrow", [L, D], f32, o)
        with ExitStack() as o:
            zth = sb("zth", [P, DH, NTAIL * NQ, B], f32r, o)
            ztl = sb("ztl", [P, DH, NTAIL * NQ, B], f32r, o)
            ot = sb("ot", [P, DH, NTAIL * NQ, B], f32, o)
            ostt = sb("ostt", [P, 2, 2, D], f32, o)
        w13h = sb("w13h", [P, DH, 2 * NSH * HS], f32r)
        w13l = sb("w13l", [P, DH, 2 * NSH * HS], f32r)
        rw1h = sb("rw1h", [P, DH, NE * HR], f32r)
        rw1l = sb("rw1l", [P, DH, NE * HR], f32r)
        w2h = sb("w2h", [P, SHC + RC, D], f32r)
        w2l = sb("w2l", [P, SHC + RC, D], f32r)
        with ExitStack() as o:
            stage = sb("stage", [P, 2, 4 * D], f32, o)
        with ExitStack() as o:
            rt = sb("rt", [P, 6, 4 * NE], f32, o)
            pair = sb("pair", [P, 2, 4, NE * NE], f32, o)
            r4 = sb("r4", [P, 4, 4], f32, o)
            gg = sb("gg", [P, 4, 2 * NE], f32r, o)
            gT = sb("gT", [2 * NE, TILE], f32r, o)
        stage_place = sb("stage_place", [P, 8 * D])
        with ExitStack() as o:
            pb = sb("pb", [P, 2, FT], f32, o)
            ct = sb("ct", [P, 2, FT], f32, o)
            ys = sb("ys", [P, 2, FT], f32, o)
            ab = sb("ab", [P, FT], f32, o)
            bu = sb("bu", [P, FT], f32, o)
        xh = sb("xh", [P, DH, TILE], f32r)
        xl = sb("xl", [P, DH, TILE], f32r)
        with ExitStack() as o:
            oh = sb("oh", [P, DH, (L // NQ - NTAIL - KEPT) * NQ, B], f32, o)
        w1h = sb("w1h", [P, DH, 3 * D], f32r)
        w1l = sb("w1l", [P, DH, 3 * D], f32r)
        wzh = sb("wzh", [P, DH, D], f32r)
        wzl = sb("wzl", [P, DH, D], f32r)
        whT = sb("whT", [P, DH, D])
        with ExitStack() as o:
            esel = sb("esel", [2 * NE, NE, P], f32r, o)
        wq = sb("wq", [P, DH, 3, 3 * N])
        wo2 = sb("wo2", [P, 2, D])
        starts = sb("starts", [P, DH * FT], bf16)
        carry = sb("carry", [P, DH * FT], bf16)
        ident = sb("ident", [P, P])
        cols = sb("cols", [P, 19])
        sc = sb("sc", [P, 12])
        condT = sb("condT", [P, DH, B])
        wr2 = sb("wr2", [P, DH, 2, NE], f32r)
        teA = sb("teA", [P, NT // 2, 4 * NE])
        teB = sb("teB", [P, 4 * NE])
        rb = sb("rb", [P, 4, NE])
        lm = sb("lm", [P, NE, NE])
        PS = ctx.enter_context(nc.psum_tensor("PS", [P, 8, 512], f32))
        del keep, place, stage_place

        LO = [4, 5]
        O = [0, 1]
        ROT = [2, 3, 4, 5]
        G = 6
        FL = 7
        GATE = [G, ROT[3]]

        xv = xT[:, :, :].rearrange("p h (b t) -> p h b t", t=L)

        def weight_stages():
            r = lambda w: w.rearrange("(r p) n -> p r n", p=P)
            st = []
            for e in range(NE // 2):
                st.append(("rw2", e, [r(r_w2[2 * e + i]) for i in range(2)]))
            for e in range(NSH):
                st.append(("w2", e, [r(s_w2[e])]))
            st.append(("l1a", 0, [r(W_f), r(W_i)]))
            st.append(("l1b", 0, [r(W_h), r(W3[:, D:2 * D])]))
            st.append(("l3h", 0, [r(W3[:, 0:D])]))
            for w, nm in ((s_w1, "w1"), (s_w3, "w3")):
                for e in range(NSH):
                    st.append((nm, e, [r(w[e])]))
            for e in range(NE // 2):
                st.append(("rw1", e, [r(r_w1[2 * e + i]) for i in range(2)]))
            return st

        STAGES = weight_stages()
        NSTG = len(STAGES)

        def stage_dst(k, half):
            nm, e, _ = STAGES[k]
            if nm == "rw2":
                c = SHC + 2 * (2 * e + half)
                return w2h[:, c:c + 2, :], w2l[:, c:c + 2, :], 2
            if nm == "w2":
                c = 4 * e + 2 * half
                return w2h[:, c:c + 2, :], w2l[:, c:c + 2, :], 2
            if nm == "l1a":
                return w1h[:, half, 0:512], w1l[:, half, 0:512], 1
            if nm == "w1":
                return w13h[:, half, e * HS:(e + 1) * HS], w13l[:, half, e * HS:(e + 1) * HS], 1
            if nm == "w3":
                q = NSH * HS + e * HS
                return w13h[:, half, q:q + HS], w13l[:, half, q:q + HS], 1
            return rw1h[:, half, e * 512:(e + 1) * 512], rw1l[:, half, e * 512:(e + 1) * 512], 1

        def stage_blocks(k, half):
            nm = STAGES[k][0]
            if nm == "rw2":
                return [(2 * half + r, kc) for kc in range(2) for r in range(2)]
            if nm == "w2":
                return [(r, 2 * half + kc) for kc in range(2) for r in range(2)]
            if nm == "l3h":
                return [(r, kc) for kc in range(2) for r in range(2)]
            return [(r, half) for r in range(4)]

        def stage_view(k):
            nm = STAGES[k][0]
            if nm == "w2":
                return stage[:, k % 2, :].rearrange("p (r n) -> p r n", r=2)
            return stage[:, k % 2, :].rearrange("p (r n) -> p r n", r=4)

        ORDER = [("x", j) for j in range(16)]
        ORDER += [("rows", 0), ("cond", 0), ("rtr", 0), ("cl", 0), ("te", 0)]
        early = [("w", (k, h)) for k in range(9) for h in range(1 if STAGES[k][0] == "l3h" else 2)]
        late = [("w", (k, h)) for k in range(9, NSTG) for h in range(2)]
        for g in range(16):
            ORDER.append(("conv", g))
            if g >= 4:
                ORDER += early[:1]
                early = early[1:]
        ORDER += early
        ORDER += [("ct", g) for g in range(16)] + [("bpe", 0)]
        N_EARLY = len(ORDER)
        ORDER += late
        BANKED = [j for j in ORDER if j[0] != "conv"]

        def bank_of(n):
            if BANKED[n] in late:
                i = late.index(BANKED[n])
                return FL if i < 12 and i % 2 else G
            return 4 + n % 4

        def finisher(job):
            kind, j = job
            if kind in ("x", "ct", "conv") and j % 2 == 0 and not (kind == "x" and j < 8):
                return "A"
            return "D"

        def signals(job):
            kind, j = job
            if kind == "w":
                return (0, 1) if STAGES[j[0]][0] == "l3h" else (1, 1)
            return (1, 0) if finisher(job) == "A" else (0, 1)

        A_AT, D_AT = {}, {}
        a = d = 0
        for job in ORDER:
            a += signals(job)[0]
            d += signals(job)[1]
            A_AT[job], D_AT[job] = a, d
        LAST_EARLY = ORDER[N_EARLY - 1]

        s_in = {n: sem("s_in_" + n) for n in ("t", "pad", "rows", "cond", "wr", "l0", "rb")}
        s_inx = [sem(f"s_in_x{q}") for q in range(4)]
        s_stg = [sem(f"s_stg{i}") for i in range(2)]
        s_tz = sem("s_tz")
        s_cl = sem("s_cl")
        s_cst = sem("s_cst")
        s_zero = sem("s_zero")
        s_tp = sem("s_tp")
        s_cv = sem("s_cv")
        s_av = sem("s_av")
        s_dv = sem("s_dv")
        s_par = sem("s_par")
        s_pa = sem("s_pa")
        proj_done = sem("proj_done")
        l0_product = sem("l0_product")
        bc_ready = sem("bc_ready")
        log_exp = sem("log_exp")
        l0_chain = sem("l0_chain")
        x_after_l0 = sem("x_after_l0")
        x1_rounded = sem("x1_rounded")
        x1_rest = sem("x1_rest")
        gate_products = sem("gate_products")
        gate_inputs = sem("gate_inputs")
        gates_ready = sem("gates_ready")
        gate_sum = sem("gate_sum")
        sum_reciprocal = sem("sum_reciprocal")
        normalised = sem("normalised")
        forget_clamped = sem("forget_clamped")
        suffix_ready = sem("suffix_ready")
        prefix_ready = sem("prefix_ready")
        h0_added = sem("h0_added")
        info_scaled = sem("info_scaled")
        info_summed = sem("info_summed")
        x_after_l1 = sem("x_after_l1")
        x_rounded = sem("x_rounded")
        x_rest = sem("x_rest")
        router_product = sem("router_product")
        logit_part = sem("logit_part")
        logits_ready = sem("logits_ready")
        scores_ready = sem("scores_ready")
        router_step = sem("router_step")
        gates_turned = sem("gates_turned")
        gates_kept = sem("gates_kept")
        selectors_ready = sem("selectors_ready")
        gates_spread = sem("gates_spread")
        layer1_done = sem("layer1_done")
        act_ready = sem("act_ready")
        hidden_gated = sem("hidden_gated")
        hidden_rounded = sem("hidden_rounded")
        hidden_rest = sem("hidden_rest")
        layer2_done = sem("layer2_done")
        x_after_l2 = sem("x_after_l2")
        z_copied = sem("z_copied")
        z_rounded = sem("z_rounded")
        z_rest = sem("z_rest")
        z_product = sem("z_product")
        step_product = sem("step_product")
        step_tanh = sem("step_tanh")
        step_gated = sem("step_gated")
        step_sum = sem("step_sum")
        state_ready = sem("state_ready")
        state_leaked = sem("state_leaked")
        row_added = sem("row_added")
        rows_turned = sem("rows_turned")
        rows_staged = sem("rows_staged")
        rows_stored = sem("rows_stored")
        last_z_rounded = sem("last_z_rounded")
        last_z_rest = sem("last_z_rest")
        last_product = sem("last_product")
        last_tanh = sem("last_tanh")
        last_gated = sem("last_gated")
        last_turned = sem("last_turned")
        last_staged = sem("last_staged")
        last_stored = [sem(f"last_stored{i}") for i in range(2)]

        block = ctx.enter_context(nc.Block())

        def wait(eng, s, v):
            if isinstance(v, int) and v <= 0:
                return
            eng.wait_ge(s, v)

        def flat(ap):
            return ap.rearrange("p h n -> p (h n)")

        NCST = 13
        IDENT = 2
        ZEROED = 5

        def xsl(t0, n):
            return xT[:, :, t0:t0 + n] if isinstance(t0, int) else xT[:, :, bass.ds(t0, n)]

        ROUTER_AT = 2

        FRONT_AT = [0, 5, 11, 17]
        SPLIT_AT = [0, 4, 10, 16]

        def fronts_at(c, n=4):
            split = [(0, f) for f in range(n) if c == SPLIT_AT[f]]
            return [(c - FRONT_AT[f], f) for f in range(n) if 1 <= c - FRONT_AT[f] <= 6] + split

        def beside_l0(t):
            return late[3 * t:3 * t + 3] if t < 4 else late[8 + t:9 + t]

        def l0_slots(t):
            return {3: [0], 4: [1, 2, 3, 4], 5: [5, 6], 6: [7, 8, 9, 10], 7: [11]}.get(t, [])

        S_TAIL = L - NTAIL * NQ
        TR = [G, FL]
        ROWS_AT = {0: 0, 1: 1, 3: 2, 4: 3, 5: 4, 6: 5, 7: 6}
        N_OUT = L // NQ - KEPT

        def steps(J):
            t0 = NQ * J
            src = xv[:, :, :, t0:t0 + NQ] if isinstance(J, int) else xv[:, :, :, bass.ds(t0, NQ)]
            return src.rearrange("p h b t -> p h t b")

        def tail_z(b):
            return steps(S_TAIL // NQ + b)

        def tail_row(eng, s):
            t = s % NQ
            eng.tensor_tensor(out=ot[:, :, s - t + 2 * (t % 2) + t // 2, :], in0=tail_z(s // NQ)[:, :, t, :],
                              in1=hid[:, :, :], op=ALU.add).then_inc(row_added, 1)

        def front_ready(F):
            if isinstance(F, int):
                return 4 + 2 * (F // 2) + 2
            return 4 + 2 * NT

        def width(half):
            return TILE if half is None else FT

        def part(row, half):
            if half is None:
                return row
            return row.rearrange("p (b t) -> p b t", t=TH)[:, :, half * TH // 2:(half + 1) * TH // 2]

        def rec_at(c, k, half):
            if half is None:
                return [(c % 6, 4 * k + c // 6, c // 6 % 2)]
            J = 4 * k + 3 * half + c // 8
            at = {1: [(1, J)], 3: [(2, J)], 5: [(3, J), (0, J + 1)], 7: [(4, J)]}.get(c % 8, [])
            if c == 0 and half == 0:
                at = [(0, J)]
            return [(r, j, j % 2) for r, j in at if j < L // NQ - NTAIL]

        def tile_x(T, kind):
            if kind == "A":
                return xsl(T * TILE, TILE)
            if isinstance(T, int):
                k = TH * (T - NT // 2)
                return xv[:, :, HALF:B, k:k + TH]
            return xv[:, :, HALF:B, bass.ds(TH * (T - NT // 2), TH)]

        def tile_buf(buf, kind):
            v = buf[:, :, :]
            return v if kind == "A" else v.rearrange("p h (b t) -> p h b t", t=TH)

        def transposed_src(job, bank):
            return PS[:, bank, :].rearrange("p (b h s) -> p h b s", b=4, h=2)

        def transposed_dst(job):
            kind, j = job
            if kind == "x":
                return xv[:, :, 4 * j:4 * j + 4, :]
            v = convT[:, j // 2].rearrange("p h (b t) -> p h b t", t=L)
            j = j % 2
            return v[:, :, 4 * j:4 * j + 4, ::-1]

        def weight_parts(kh, bank, part):
            k, half = kh
            nm = STAGES[k][0]
            src = PS[:, bank, :]
            if nm == "l1b":
                return [((w1h, w1l)[part][:, half, 2 * D:3 * D], src[:, 0:D]),
                        ((wzh, wzl)[part][:, half, :], src[:, D:2 * D])]
            dst = stage_dst(k, half)
            if dst[2] == 2:
                src = src.rearrange("p (c n) -> p c n", c=2)
            return [(dst[part], src)]

        @block.sync
        def _(sp):
            sp.sem_inc(rows_stored, 32)
            def load_x(q):
                for h in range(DH):
                    sp.dma_start(Xs[h * L:(h + 1) * L, q * 16:(q + 1) * 16, :],
                                 x[q * 16:(q + 1) * 16, :, h * P:(h + 1) * P].rearrange("b s d -> s b d"))\
                      .then_inc(s_inx[q], 16)

            load_x(0)
            sp.dma_start(padded[0:L, :], cond).then_inc(s_in["pad"], 16)
            sp.wait_ge(s_zero, 1)
            sp.dma_start(padded[L:2 * L, :], zrow[:, :]).then_inc(s_in["pad"], 16)
            for q in range(1, 4):
                load_x(q)
            sp.wait_ge(s_in["pad"], 32)
            for h in range(DH):
                for s0, n in ((0, L), (L // 2, L // 2)):
                    src = bass.AP(padded.tensor, s0 * D + h * P, [[D, L // 2], [D, n], [1, P]])
                    sp.dma_start(Tz[h * L + s0:h * L + s0 + L // 2, 0:n, :], src).then_inc(s_in["t"], 16)
            sp.wait_ge(s_cst, ZEROED)
            for k in range(NSTG):
                if k == 2:
                    for q, src in enumerate((Wp[:, 0:N], Wp[:, N:2 * N], Ws)):
                        sp.dma_start(wq[:, :, q, N:2 * N], src.rearrange("(k p) n -> p k n", p=P))\
                          .then_inc(s_in["l0"], 16)
                    for q in range(2):
                        sp.dma_start(wo2[q * N:(q + 1) * N, q, :], Wo).then_inc(s_in["l0"], 16)
                    sp.dma_start(rb[:, :, :], bass.AP(router_bias.tensor, 0, [[0, P], [0, 4], [1, NE]]))\
                      .then_inc(s_in["rb"], 16)
                nm, _, srcs = STAGES[k]
                if k >= 2:
                    sp.wait_ge(s_tp, max(n + 1 for n, j in enumerate(BANKED)
                                         if j[0] == "w" and j[1][0] == k - 2))
                view = stage_view(k)
                r0 = 0
                for s in srcs:
                    sp.dma_start(view[:, r0:r0 + s.shape[1], :], s).then_inc(s_stg[k % 2], 16)
                    r0 += s.shape[1]

            def store(J):
                wait(sp, rows_staged, 1 + J + 1)
                for tp in range(2):
                    if isinstance(J, int):
                        dst = out[:, 4 * J + 2 * tp:4 * J + 2 * tp + 2, :]
                    else:
                        dst = out[:, bass.ds(4 * J + 2 * tp, 2), :]
                    sp.dma_start(dst.rearrange("b t d -> b (t d)"),
                                 ost[tp * B:(tp + 1) * B, :, :].rearrange("p t d -> p (t d)")).then_inc(rows_stored, 16)

            with sp.Fori(0, KEPT) as J:
                store(J)
            for b in range(N_OUT):
                sp.wait_ge(last_staged, b + 1)
                for tp in range(2):
                    t = NQ * (KEPT + b) + 2 * tp
                    sp.dma_start(out[:, t:t + 2, :].rearrange("b t d -> b (t d)"),
                                 ostt[tp * B:(tp + 1) * B, b % 2, :, :].rearrange("p t d -> p (t d)"))\
                      .then_inc(last_stored[b % 2], 16)
            sp.wait_ge(rows_stored, 32 + 32 * KEPT)
            for q in range(2):
                sp.wait_ge(last_stored[q], 32 * (N_OUT // 2))

        @block.gpsimd
        def _(pool):
            n = [0]
            pool.sem_inc(row_added, 2 * NQ)

            def made(ins):
                n[0] += 1
                ins.then_inc(s_cst, 1)
                return n[0]

            def after(k):
                pool.wait_ge(s_cst, k)

            pool.memset(zrow[:, :], 0.0).then_inc(s_zero, 1)
            made(pool.memset(ident[:, :], 0.0))
            after(1)
            made(pool.affine_select(out=ident[:, :], in_=ident[:, :], compare_op=ALU.not_equal, fill=1.0,
                                    base=0, pattern=[[-1, P]], channel_multiplier=1))
            made(pool.memset(sel[:, :].bitcast(f32), 1.0))
            made(pool.memset(wq[:, :, :, :], 0.0))
            made(pool.memset(wo2[:, :, :], 0.0))
            made(pool.memset(lm[:, :, :], 1.0))
            made(pool.memset(starts[:, :], 0.0))
            made(pool.memset(carry[:, :], 1.0))
            after(8)
            sv = starts[:, :].rearrange("p (s t) -> p s t", t=L)
            made(pool.affine_select(out=sv, in_=sv, compare_op=ALU.not_equal, fill=1.0,
                                    base=0, pattern=[[0, DH * FB], [1, L]], channel_multiplier=0))
            cv = carry[:, :].rearrange("p (s t) -> p s t", t=L)
            made(pool.affine_select(out=cv, in_=cv, compare_op=ALU.not_equal, fill=0.0,
                                    base=0, pattern=[[0, DH * FB], [1, L]], channel_multiplier=0))
            made(pool.affine_select(out=lm[:, :, :], in_=lm[:, :, :], compare_op=ALU.is_ge, fill=0.0,
                                    base=-1, pattern=[[1, NE], [-1, NE]], channel_multiplier=0))
            after(11)
            nA = NT // 2 * TB
            sA = sel[:, 0:NT // 2 * TILE].rearrange("p (b t) -> p b t", t=L)
            sB = sel[:, NT // 2 * TILE:].rearrange("p (b t) -> p b t", t=16)
            made(pool.affine_select(out=sA, in_=sA.bitcast(f32), compare_op=ALU.is_equal, fill=0.0,
                                    base=0, pattern=[[-1, nA], [0, L]], channel_multiplier=1))
            made(pool.affine_select(out=sB, in_=sB.bitcast(f32), compare_op=ALU.is_equal, fill=0.0,
                                    base=-HALF, pattern=[[-1, HALF], [0, 16]], channel_multiplier=1))
            assert n[0] == NCST

            def front_pool(r, F):
                if r == 3:
                    wait(pool, gate_inputs, 3 * F + 3)
                    wait(pool, gates_ready, F + 1)
                    pool.tensor_tensor(out=flat(cnd[:, :, :]), in0=flat(cnd[:, :, :]), in1=flat(inp[:, :, :]),
                                       op=ALU.mult).then_inc(normalised, 1)
                    wait(pool, sum_reciprocal, 2 * F + 1)
                    pool.tensor_tensor(out=fgt[:, 0, :], in0=fgt[:, 0, :], in1=rcp[:, 0, :], op=ALU.mult)
                if r == 4:
                    wait(pool, sum_reciprocal, 2 * F + 2)
                    pool.tensor_tensor(out=fgt[:, 1, :], in0=fgt[:, 1, :], in1=rcp[:, 1, :],
                                       op=ALU.mult).then_inc(normalised, 1)
                    wait(pool, normalised, 3 * F + 1)
                    pool.tensor_tensor(out=flat(cnd[:, :, :]), in0=flat(cnd[:, :, :]), in1=flat(rcp[:, :, :]),
                                       op=ALU.mult).then_inc(normalised, 1)
                if r == 5:
                    wait(pool, prefix_ready, F + 1)
                    for h in range(DH):
                        v = rcp[:, h, :].rearrange("p (b t) -> p b t", t=L)
                        b0 = FB * F
                        h0 = condT[:, h, b0:b0 + FB] if isinstance(F, int) else condT[:, h, bass.ds(b0, FB)]
                        last = pool.tensor_tensor(out=v, in0=v, in1=h0.unsqueeze(2).broadcast_to([P, FB, L]),
                                                  op=ALU.mult)
                    last.then_inc(h0_added, 1)
                    wait(pool, h0_added, 2 * F + 1)
                    pool.tensor_tensor(out=rcp[:, :, :], in0=xsl(F * FT, FT), in1=rcp[:, :, :],
                                       op=ALU.add).then_inc(h0_added, 1)

            pool.wait_ge(s_dv, D_AT[("cond", 0)])
            for F in range(2):
                for r in range(6):
                    front_pool(r, F)
            with pool.Fori(0, NT // 2 - 1) as i:
                for f in range(4):
                    for r in range(6):
                        front_pool(r, 2 + 4 * i + f)
            for f in range(2):
                for r in range(6):
                    front_pool(r, NF - 2 + f)

            def rec_pool(r, J, u):
                z4 = z4s[:, u]
                if r == 0:
                    wait(pool, z_rounded, J + 1)
                    wait(pool, z_copied, J + 1)
                    wait(pool, z_product, 1 + J)
                    pool.tensor_tensor(out=z4l[:, :, :, :].rearrange("p h t b -> p (h t b)"),
                                       in0=z4[:, :, :, :].rearrange("p h t b -> p (h t b)"),
                                       in1=z4h[:, :, :, :].bitcast(f32).rearrange("p h t b -> p (h t b)"),
                                       op=ALU.subtract).then_inc(z_rest, 1)
                if 1 <= r <= 4:
                    t = r - 1
                    wait(pool, state_ready, 4 * J + t + 1)
                    wait(pool, step_sum, 1 + 4 * J + t)
                    pool.tensor_tensor(out=hl[:, :, :], in0=hid[:, :, :], in1=leak(),
                                       op=ALU.mult).then_inc(state_leaked, 1)
                    if t > 0:
                        out_row(J, t - 1, z4)
                if r == 5:
                    wait(pool, state_ready, 4 * J + NQ + 1)
                    out_row(J, NQ - 1, z4)

            def leak():
                return sc[:, 6:8].unsqueeze(2).broadcast_to([P, DH, B])

            def out_row(J, t, z4):
                q = 2 * (t % 2) + t // 2
                if isinstance(J, int):
                    dst = oh[:, :, NQ * (J - KEPT) + q, :]
                else:
                    dst = o4[:, :, q, :]
                    if t == 0:
                        wait(pool, rows_turned, 1 + J)
                pool.tensor_tensor(out=dst, in0=z4[:, :, t, :], in1=hid[:, :, :], op=ALU.add)\
                    .then_inc(row_added, 1)

            with pool.Fori(0, KEPT // 2) as i:
                for u in range(2):
                    for r in range(6):
                        rec_pool(r, 2 * i + u, u)
            rec_pool(0, KEPT, KEPT % 2)
            for J in range(KEPT, L // NQ - NTAIL):
                for r in (1, 2, 3, 0, 4, 5):
                    j = J + (r == 0)
                    if j < L // NQ - NTAIL:
                        rec_pool(r, j, j % 2)

            for b in range(NTAIL):
                for t in range(NQ):
                    s = S_TAIL + NQ * b + t
                    pool.wait_ge(state_ready, s + 1)
                    pool.wait_ge(step_sum, 1 + s)
                    pool.tensor_tensor(out=hl[:, :, :], in0=hid[:, :, :], in1=leak(),
                                       op=ALU.mult).then_inc(state_leaked, 1)
                    if b or t:
                        tail_row(pool, NQ * b + t - 1)

        @block.scalar
        def _(act):
            act.sem_inc(bc_ready, 4)
            act.sem_inc(act_ready, CH)
            act.sem_inc(hidden_rounded, CH)
            act.sem_inc(rows_staged, 1)
            act.dma_start(condN[:, :], cond).then_inc(s_in["cond"], 16)
            act.dma_start(wrN[:, :], W_router).then_inc(s_in["wr"], 16)
            vecs = [(0, bp[0:N], 1), (1, bp[N:2 * N], 1), (2, bs, 1), (3, A_log, 1), (4, dt_log, 1)]
            for r, v, _ in vecs:
                act.dma_start(rows[r:r + 1, :].rearrange("o (q n) -> o q n", q=2),
                              v.rearrange("(o n) -> o n", o=1).unsqueeze(1).broadcast_to([1, 2, N]))\
                   .then_inc(s_in["rows"], 16)
            for r, v in ((5, conv_b), (7, bo), (9, b_f), (11, b_i), (13, b_h), (15, b3), (17, alpha)):
                act.dma_start(rows[r:r + 2, :], v.rearrange("(h p) -> h p", h=2)).then_inc(s_in["rows"], 16)

            def evacuate(job):
                kind, j = job
                if kind == "conv":
                    if finisher(job) == "A":
                        act.wait_ge(s_cv, j + 1)
                        act.activation(convS[:, 8 * j:8 * j + 8, :].rearrange("p c b -> p (c b)"),
                                       PS[:, j % 4, :], ACT.Copy).then_inc(s_av, 1)
                    return
                n = BANKED.index(job)
                bank = bank_of(n)
                if kind in ("x", "ct") and finisher(job) == "A":
                    act.wait_ge(s_tp, n + 1)
                    act.activation(transposed_dst(job), transposed_src(job, bank), ACT.Copy).then_inc(s_av, 1)
                if kind == "w" and signals(job)[0]:
                    act.wait_ge(s_tp, n + 1)
                    for dst, src in weight_parts(j, bank, 0):
                        last = act.activation(dst, src, ACT.Copy)
                    last.then_inc(s_av, 1)

            for job in ORDER[:ORDER.index(("conv", 0))]:
                evacuate(job)
            act.wait_ge(s_par, 1)
            act.activation(sc[:, 0:2], sc[:, 0:2], ACT.Exp, scale=-1.0).then_inc(s_pa, 1)
            act.wait_ge(s_pa, 1)
            act.activation(sc[:, 0:2], sc[:, 0:2], ACT.Ln, bias=1.0).then_inc(s_pa, 1)
            for job in ORDER[ORDER.index(("conv", 0)):N_EARLY]:
                evacuate(job)

            def l0_act(t, p, between):
                wait(act, proj_done, 2 * t + 1)
                wait(act, l0_chain, 5 * t + 5)
                act.activation(pb[:, p, :], PS[:, p, 0:FT], ACT.Identity, bias=sc[:, 2:3]).then_inc(bc_ready, 1)
                act.activation(ct[:, p, :], PS[:, p, FT:2 * FT], ACT.Tanh, bias=sc[:, 3:4]).then_inc(bc_ready, 1)
                evacuate(between)
                wait(act, l0_chain, 5 * t + 10 + 1)
                act.activation(ab[:, :], ab[:, :], ACT.Exp, scale=-1.0).then_inc(log_exp, 1)
                wait(act, log_exp, 2 * t + 1)
                act.activation(ab[:, :], ab[:, :], ACT.Ln, bias=1.0).then_inc(log_exp, 1)

            def front_act(r, F):
                if r == 0:
                    wait(act, x_after_l0, front_ready(F))
                    wait(act, gate_products, 3 * F)
                    act.activation(x1h[:, :, :], xsl(F * FT, FT), ACT.Copy).then_inc(x1_rounded, 1)
                if r in (1, 2, 3):
                    q = r - 1
                    wait(act, gate_products, 3 * F + q + 1)
                    if q == 0:
                        wait(act, prefix_ready, F)
                    if q == 1:
                        wait(act, normalised, 3 * F)
                    if q == 2:
                        wait(act, info_summed, F)
                    buf = (fgt, inp, cnd)[q]
                    for m in range(DH):
                        last = act.activation(buf[:, m, :], PS[:, FL, m * FT:(m + 1) * FT], ACT.Identity,
                                              bias=cols[:, 9 + 2 * q + m:10 + 2 * q + m])
                    last.then_inc(gate_inputs, 1)
                    if q == 1:
                        wait(act, gate_inputs, 3 * F + 2)
                        both = gates[:, :, :, :].rearrange("p q h n -> p (q h n)")
                        act.activation(both, both, ACT.Sigmoid).then_inc(gates_ready, 1)

            def split_act(T, kind):
                wait(act, x_after_l1, 2 * T + 2 if kind == "A" else NF)
                wait(act, layer1_done, GRP + GRP * T)
                wait(act, router_product, 1 + T)
                src, dst = tile_x(T, kind), tile_buf(xh, kind)
                act.activation(dst, src, ACT.Copy).then_inc(x_rounded, 1)

            def moe_act(c, T, nxt, half=None):
                w = width(half)
                if c > 0:
                    hi(c - 1, T, w)
                wait(act, layer1_done, GRP + GRP * T + (2 * c + 1 if c < SHC else c + SHC + 1))
                wait(act, hidden_gated, CH * T + CH + c - 1)
                bank = ROT[2 * c % 4] if c < SHC else ROT[(c - SHC) % 3]
                act.activation(act_g[:, c % 2, 0:w], PS[:, bank, 0:w], ACT.Silu if c < SHC else ACT.Gelu)\
                   .then_inc(act_ready, 1)
                if c == ROUTER_AT and half != 1:
                    wait(act, logits_ready, T + 1)
                    act.activation(rt[:, 1, :], rt[:, 0, :], ACT.Sigmoid).then_inc(scores_ready, 1)
                if c == CH - 1:
                    if nxt:
                        split_act(T + 1, nxt)
                    hi(c, T, w)

            def hi(c, T, w):
                wait(act, hidden_gated, CH * T + CH + c + 1)
                wait(act, layer2_done, CH * T + CH + c - LAG + 1)
                act.activation(hh[:, c % LAG, 0:w], hbuf[:, c % 2, 0:w], ACT.Copy).then_inc(hidden_rounded, 1)

            def rec_act(r, J, u, tiles):
                z4 = z4s[:, u]
                if r == 0:
                    wait(act, x_after_l2, tiles)
                    wait(act, row_added, NQ * (J + 1))
                    wait(act, z_product, 1 + J)
                    src = steps(J)
                    for h in range(DH):
                        last = act.activation(z4[:, h, :, :], src[:, h, :, :], ACT.Copy)
                    last.then_inc(z_copied, 1)
                    wait(act, z_copied, J + 1)
                    act.activation(z4h[:, :, :, :].rearrange("p h t b -> p (h t b)"),
                                   z4[:, :, :, :].rearrange("p h t b -> p (h t b)"), ACT.Copy).then_inc(z_rounded, 1)
                if 1 <= r <= 4:
                    t = r - 1
                    wait(act, step_product, 4 * J + t + 1)
                    for m in range(DH):
                        last = act.activation(th[:, m, :], PS[:, FL, m * FT + t * B:m * FT + (t + 1) * B], ACT.Tanh,
                                              bias=sc[:, 8 + m:9 + m], scale=0.5)
                    last.then_inc(step_tanh, 1)
                if r == 5:
                    wait(act, rows_turned, 1 + J + 1)
                    wait(act, rows_stored, 32 + 32 * J)
                    act.activation(ost[:, :, :].rearrange("p t d -> p (t d)"), PS[:, FL, :], ACT.Copy)\
                       .then_inc(rows_staged, 1)

            def tail_rows(b):
                act.wait_ge(last_turned, b + 1)
                if b >= 2:
                    act.wait_ge(last_stored[b % 2], 32 * (b // 2))
                act.activation(ostt[:, b % 2, :, :].rearrange("p t d -> p (t d)"), PS[:, TR[b % 2], :], ACT.Copy)\
                   .then_inc(last_staged, 1)

            def rec_act2(r, J):
                if 1 <= r <= 4:
                    t = r - 1
                    wait(act, step_sum, 1 + 4 * J + t + 1)
                    wait(act, state_leaked, 4 * J + t + 1)
                    wait(act, row_added, 2 * NQ + 4 * J + t)
                    act.activation(hid[:, :, :], uz[:, :, :], ACT.Tanh).then_inc(state_ready, 1)

            act.wait_ge(s_par, 5)
            for t in range(NT):
                jobs, slots = beside_l0(t), l0_slots(t)
                l0_act(t, t % 2, jobs[0])
                for c in slots[:2]:
                    front_act(c % 6, c // 6)
                for job in jobs[1:]:
                    evacuate(job)
                for c in slots[2:]:
                    front_act(c % 6, c // 6)
            act.wait_ge(l0_chain, 10 + 5 * NT)
            split_act(0, "A")
            with act.Fori(0, NT // 2 - 1) as i:
                for c in range(CH):
                    moe_act(c, i, "A")
                    for r, f in fronts_at(c):
                        front_act(r, 2 + 4 * i + f)
            for c in range(CH):
                moe_act(c, NT // 2 - 1, "B")
                for r, f in fronts_at(c, 2):
                    front_act(r, NF - 2 + f)
            for c in range(CH):
                moe_act(c, NT // 2, "B")

            def rec_tile(k, nxt, half=None):
                for c in range(CH):
                    moe_act(c, NT // 2 + 1 + k + (half or 0), nxt, half)
                    for r, J, u in rec_at(c, k, half):
                        done = NT // 2 + 1 + k
                        if half is not None and J >= 4 * (k + 1):
                            done += 1
                        rec_act(r, J, u, 2 * done + 2)
                        rec_act2(r, J)

            with act.Fori(0, NT // 2 - 2) as k:
                rec_tile(k, "B")
            for half in range(2):
                rec_tile(NT // 2 - 2, None, half)

            def tail_split(b):
                for h in range(DH):
                    last = act.activation(zth[:, h, NQ * b:NQ * (b + 1), :], tail_z(b)[:, h, :, :], ACT.Copy)
                last.then_inc(last_z_rounded, 1)

            act.wait_ge(x_after_l2, 2 + 2 * NP)
            tail_split(0)
            for b in range(NTAIL):
                for t in range(NQ):
                    s = NQ * b + t
                    for m in range(DH):
                        act.wait_ge(last_product, DH * s + m + 1)
                        act.activation(th[:, m, :], PS[:, ROT[2 * (b % 2) + m], t * B:(t + 1) * B], ACT.Tanh,
                                       bias=sc[:, 8 + m:9 + m], scale=0.5).then_inc(last_tanh, 1)
                    act.wait_ge(step_sum, 1 + S_TAIL + s + 1)
                    act.wait_ge(state_leaked, S_TAIL + s + 1)
                    act.wait_ge(row_added, 2 * NQ + S_TAIL + s)
                    act.activation(hid[:, :, :], uz[:, :, :], ACT.Tanh).then_inc(state_ready, 1)
                    if t == 0 and b + 1 < NTAIL:
                        tail_split(b + 1)
                    if s in ROWS_AT:
                        tail_rows(ROWS_AT[s])
            tail_rows(N_OUT - 1)

        @block.vector
        def _(dve):
            dve.sem_inc(l0_chain, 10)
            dve.sem_inc(x_after_l0, 4)
            dve.sem_inc(hidden_gated, CH)
            dve.sem_inc(hidden_rest, CH)
            dve.sem_inc(x_after_l2, 2)
            dve.sem_inc(step_sum, 1)

            def evacuate(job):
                kind, j = job
                if kind == "conv":
                    if finisher(job) == "D":
                        dve.wait_ge(s_cv, j + 1)
                        dve.tensor_copy(convS[:, 8 * j:8 * j + 8, :].rearrange("p c b -> p (c b)"),
                                        PS[:, j % 4, :]).then_inc(s_dv, 1)
                    return
                if finisher(job) != "D":
                    return
                n = BANKED.index(job)
                bank = bank_of(n)
                dve.wait_ge(s_tp, n + 1)
                b = PS[:, bank, :]
                if kind in ("x", "ct"):
                    dve.tensor_copy(transposed_dst(job), transposed_src(job, bank)).then_inc(s_dv, 1)
                elif kind == "rows":
                    dve.tensor_copy(cols[:, :], b[:, 0:19]).then_inc(s_dv, 1)
                elif kind == "cond":
                    dve.tensor_copy(condT[:, :, :], b[:, 0:2 * B].rearrange("p (h b) -> p h b", h=2)).then_inc(s_dv, 1)
                elif kind == "rtr":
                    v = b[:, 0:4 * NE].rearrange("p (k e) -> p k e", k=4)
                    dve.tensor_copy(wr2[:, :, 0, :], v[:, 0:2, :]).then_inc(s_par, 1)
                    dve.tensor_copy(wrt[:, :, :], v[:, 2:4, :])
                    dve.wait_ge(s_par, 2)
                    dve.tensor_tensor(out=wr2[:, :, 1, :], in0=v[:, 0:2, :], in1=wr2[:, :, 0, :].bitcast(f32),
                                      op=ALU.subtract).then_inc(s_dv, 1)
                elif kind == "cl":
                    dve.tensor_copy(cl[:, 0, :], PS[0:B, bank, 0:NE]).then_inc(s_cl, 1)
                    dve.wait_ge(s_cl, 1)
                    dve.tensor_tensor(out=cl[:, 1, :], in0=PS[0:B, bank, 0:NE], in1=cl[:, 0, :].bitcast(f32),
                                      op=ALU.subtract).then_inc(s_dv, 1)
                elif kind == "te":
                    v = b[:, 0:8 * NE * (NT // 2 + 1)].rearrange("p (g s e) -> p g e s", s=2, e=NE)
                    nA = 4 * (NT // 2)
                    dve.tensor_reduce(out=teA[:, :, :].rearrange("p a (g e) -> p (a g) e", e=NE), in_=v[:, 0:nA],
                                      op=ALU.add, axis=AX.X)
                    dve.tensor_reduce(out=teB[:, :].rearrange("p (g e) -> p g e", e=NE), in_=v[:, nA:nA + 4],
                                      op=ALU.add, axis=AX.X).then_inc(s_dv, 1)
                elif kind == "bpe":
                    dve.tensor_tensor(out=sc[:, 2:4], in0=b[:, 0:2], in1=cols[:, 0:2], op=ALU.add).then_inc(s_dv, 1)
                elif kind == "w":
                    if STAGES[j[0]][0] == "l3h":
                        dve.tensor_copy(whT[:, :, :], b.rearrange("p (k n) -> p k n", k=2)).then_inc(s_dv, 1)
                        return
                    dve.wait_ge(s_av, A_AT[job])
                    for (hi_, src), (lo_, _) in zip(weight_parts(j, bank, 0), weight_parts(j, bank, 1)):
                        last = dve.tensor_tensor(out=lo_, in0=src, in1=hi_.bitcast(f32), op=ALU.subtract)
                    last.then_inc(s_dv, 1)

            for h in range(DH):
                dve.memset(Tz[h * L + L // 2:(h + 1) * L, L // 2:L, :], 0.0).then_inc(s_tz, 1)
            for job in ORDER[:ORDER.index(("rows", 0)) + 1]:
                evacuate(job)
            dve.wait_ge(s_dv, D_AT[("rows", 0)])
            dve.scalar_tensor_tensor(out=sc[:, 0:2], in0=cols[:, 3:5], scalar=-1.0, in1=cols[:, 3:5],
                                     op0=ALU.mult, op1=ALU.max).then_inc(s_par, 1)
            for job in ORDER[ORDER.index(("rows", 0)) + 1:ORDER.index(("conv", 0))]:
                evacuate(job)
            dve.tensor_scalar(sc[:, 6:8], cols[:, 17:19], -1.0, 1.0, ALU.mult, ALU.add)
            dve.tensor_scalar(sc[:, 8:10], cols[:, 15:17], 0.5, None, ALU.mult)
            dve.wait_ge(s_pa, 2)
            dve.scalar_tensor_tensor(out=sc[:, 4:6], in0=cols[:, 3:5], scalar=0.0, in1=sc[:, 0:2],
                                     op0=ALU.max, op1=ALU.add).then_inc(s_par, 1)
            dve.wait_ge(s_par, 3)
            dve.scalar_tensor_tensor(out=sc[:, 10:11], in0=sc[:, 4:5], scalar=-1.0, in1=sc[:, 5:6],
                                     op0=ALU.mult, op1=ALU.mult).then_inc(s_par, 1)
            dve.wait_ge(s_par, 4)
            dve.tensor_scalar(sc[:, 10:11], sc[:, 10:11], 1.0, None, ALU.add).then_inc(s_par, 1)
            dve.wait_ge(s_par, 5)
            dve.wait_ge(s_cst, NCST)
            dve.tensor_scalar(dec[:, :], carry[:, 0:FT], sc[:, 10:11], None, ALU.mult).then_inc(s_par, 1)
            for job in ORDER[ORDER.index(("conv", 0)):N_EARLY]:
                evacuate(job)

            def l0_x(t):
                for m in range(DH):
                    wait(dve, l0_product, 4 + 2 * t + m + 1)
                    xs = xT[:, m, t * TILE:(t + 1) * TILE]
                    dve.scalar_tensor_tensor(out=xs, in0=PS[:, LO[m], :], scalar=cols[:, 7 + m:8 + m],
                                             in1=xs, op0=ALU.add, op1=ALU.add).then_inc(x_after_l0, 1)

            def l0_dve(t, p, between):
                wait(dve, bc_ready, 4 + 2 * t + 1)
                dve.scalar_tensor_tensor(out=ab[:, :], in0=pb[:, p, :], scalar=-1.0, in1=pb[:, p, :],
                                         op0=ALU.mult, op1=ALU.max).then_inc(l0_chain, 1)
                evacuate(between)
                if t:
                    l0_x(t - 1)
                wait(dve, log_exp, 2 * t + 2)
                dve.scalar_tensor_tensor(out=bu[:, :], in0=pb[:, p, :], scalar=0.0, in1=ab[:, :],
                                         op0=ALU.max, op1=ALU.add).then_inc(l0_chain, 1)
                wait(dve, l0_chain, 10 + 5 * t + 2)
                wait(dve, proj_done, 2 * t + 2)
                dve.scalar_tensor_tensor(out=bu[:, :], in0=PS[:, 2 + p, 0:FT], scalar=cols[:, 2:3],
                                         in1=bu[:, :], op0=ALU.add, op1=ALU.mult).then_inc(l0_chain, 1)
                wait(dve, l0_chain, 10 + 5 * t + 3)
                wait(dve, l0_product, 2 * t + 2)
                dve.tensor_tensor_scan(out=ys[:, p, :], data0=dec[:, :], data1=bu[:, :], initial=0.0,
                                       op0=ALU.mult, op1=ALU.add).then_inc(l0_chain, 1)
                wait(dve, l0_chain, 10 + 5 * t + 4)
                wait(dve, bc_ready, 4 + 2 * t + 2)
                dve.scalar_tensor_tensor(out=ys[:, p, :], in0=ys[:, p, :], scalar=sc[:, 5:6], in1=ct[:, p, :],
                                         op0=ALU.mult, op1=ALU.mult).then_inc(l0_chain, 1)

            dve.wait_ge(s_in["rb"], 16)
            dve.wait_ge(s_par, 6)

            def front_dve(r, F):
                if r == 0:
                    wait(dve, x1_rounded, F + 1)
                    wait(dve, gate_products, 3 * F)
                    dve.tensor_tensor(out=x1l[:, :, :], in0=xsl(F * FT, FT), in1=x1h[:, :, :].bitcast(f32),
                                      op=ALU.subtract).then_inc(x1_rest, 1)
                if r == 3:
                    wait(dve, gates_ready, F + 1)
                    dve.scalar_tensor_tensor(out=flat(gsum[:, :, :]), in0=flat(fgt[:, :, :]), scalar=EPS,
                                             in1=flat(inp[:, :, :]), op0=ALU.add, op1=ALU.add).then_inc(gate_sum, 1)
                    wait(dve, gate_sum, F + 1)
                    wait(dve, h0_added, 2 * F)
                    dve.reciprocal(rcp[:, 0, :], gsum[:, 0, :]).then_inc(sum_reciprocal, 1)
                if r == 4:
                    dve.reciprocal(rcp[:, 1, :], gsum[:, 1, :]).then_inc(sum_reciprocal, 1)
                if r == 5:
                    wait(dve, normalised, 3 * F + 2)
                    dve.tensor_scalar(flat(fgt[:, :, :]), flat(fgt[:, :, :]), EPS, 1.0, ALU.add, ALU.min)\
                       .then_inc(forget_clamped, 1)
                    wait(dve, forget_clamped, F + 1)
                    dve.tensor_tensor_scan(out=flat(gsum[:, :, :])[:, ::-1], data0=starts[:, :],
                                           data1=flat(fgt[:, :, :])[:, ::-1], initial=0.0,
                                           op0=ALU.max, op1=ALU.mult).then_inc(suffix_ready, 1)
                    wait(dve, normalised, 3 * F + 3)
                    dve.tensor_tensor_scan(out=flat(rcp[:, :, :]), data0=starts[:, :], data1=flat(fgt[:, :, :]),
                                           initial=0.0, op0=ALU.max, op1=ALU.mult).then_inc(prefix_ready, 1)
                if r == 6:
                    wait(dve, suffix_ready, F + 1)
                    dve.tensor_tensor(out=flat(cnd[:, :, :]), in0=flat(cnd[:, :, :]), in1=flat(gsum[:, :, :]),
                                      op=ALU.mult).then_inc(info_scaled, 1)
                    wait(dve, info_scaled, F + 1)
                    dve.tensor_tensor_scan(out=flat(gsum[:, :, :]), data0=carry[:, :], data1=flat(cnd[:, :, :]),
                                           initial=0.0, op0=ALU.mult, op1=ALU.add).then_inc(info_summed, 1)
                    wait(dve, info_summed, F + 1)
                    wait(dve, h0_added, 2 * F + 2)
                    dve.tensor_tensor(out=xsl(F * FT, FT), in0=rcp[:, :, :], in1=gsum[:, :, :],
                                      op=ALU.add).then_inc(x_after_l1, 1)

            K_RD = 14

            def router_logits(T, kind):
                lg = rt[:, 0, :]
                v3 = lambda a: a.rearrange("p (g e) -> p g e", g=4)
                wait(dve, router_product, 1 + T + 1)
                te = teB[:, :] if kind == "B" else (teA[:, T, :] if isinstance(T, int) else
                                                    teA[:, bass.ds(T, 1), :].rearrange("p a b -> p (a b)"))
                xr = PS[:, G, 0:8 * NE].rearrange("p (g s e) -> p g s e", g=4, s=2)
                dve.tensor_tensor(out=v3(lg), in0=xr[:, :, 0, :], in1=v3(te), op=ALU.add).then_inc(logit_part, 1)
                wait(dve, logit_part, T + 1)
                dve.tensor_tensor(out=v3(lg), in0=xr[:, :, 1, :], in1=v3(lg), op=ALU.add).then_inc(logits_ready, 1)

            def router_dve(T, third):
                base = K_RD * T
                k = [(0, 5, 9)[third]]

                def step(ins):
                    k[0] += 1
                    ins.then_inc(router_step, 1)

                def prev():
                    wait(dve, router_step, base + k[0])

                s, selv, rank, sm, mk = (rt[:, q, :] for q in range(1, 6))
                den, rc, hc, one = (r4[:, q, :] for q in range(4))
                v3 = lambda a: a.rearrange("p (g e) -> p g e", g=4)
                if third == 0:
                    wait(dve, scores_ready, T + 1)
                    step(dve.tensor_tensor(out=selv, in0=s, in1=rb[:, :, :].rearrange("p g e -> p (g e)"), op=ALU.add))
                    prev()
                    for g in range(4):
                        row = v3(selv)[:, g, :]
                        sj = row.unsqueeze(1).broadcast_to([P, NE, NE])
                        se = row.unsqueeze(2).broadcast_to([P, NE, NE])
                        pg = [pair[:, q, g, :].rearrange("p (e j) -> p e j", e=NE) for q in range(2)]
                        dve.tensor_tensor(out=pg[0], in0=sj, in1=se, op=ALU.is_gt)
                        last = dve.tensor_tensor(out=pg[1], in0=sj, in1=se, op=ALU.is_equal)
                    step(last)
                    prev()
                    lmb = lm[:, :, :].rearrange("p e j -> p (e j)").unsqueeze(1).broadcast_to([P, 4, NE * NE])
                    step(dve.tensor_tensor(out=pair[:, 1, :, :], in0=pair[:, 1, :, :], in1=lmb, op=ALU.mult))
                    prev()
                    step(dve.tensor_tensor(out=pair[:, 0, :, :], in0=pair[:, 0, :, :], in1=pair[:, 1, :, :],
                                           op=ALU.add))
                    prev()
                    step(dve.tensor_reduce(out=rank, in_=pair[:, 0, :, :].rearrange("p g (e j) -> p (g e) j", j=NE),
                                           op=ALU.add, axis=AX.X))
                if third == 1:
                    prev()
                    dve.tensor_scalar(mk, rank, 1.5, None, ALU.is_lt)
                    step(dve.scalar_tensor_tensor(out=sm, in0=rank, scalar=1.5, in1=s, op0=ALU.is_lt, op1=ALU.mult))
                    prev()
                    step(dve.tensor_reduce(out=den, in_=v3(sm), op=ALU.add, axis=AX.X))
                    prev()
                    dve.tensor_scalar(one, den, 1e-9, None, ALU.is_gt)
                    step(dve.tensor_scalar(rc, den, 1e-9, None, ALU.add))
                    prev()
                    dve.tensor_scalar(hc, one, -0.5, 0.5, ALU.mult, ALU.add)
                    step(dve.reciprocal(rc, rc))
                if third == 2:
                    prev()
                    step(dve.tensor_tensor(out=rc, in0=rc, in1=one, op=ALU.mult))
                    prev()
                    dve.tensor_tensor(out=v3(mk), in0=v3(mk), in1=hc.unsqueeze(2).broadcast_to([P, 4, NE]), op=ALU.mult)
                    step(dve.tensor_tensor(out=v3(sm), in0=v3(sm), in1=rc.unsqueeze(2).broadcast_to([P, 4, NE]),
                                           op=ALU.mult))
                    prev()
                    step(dve.tensor_tensor(out=sm, in0=sm, in1=mk, op=ALU.add))
                    prev()
                    step(dve.tensor_copy(gg[:, :, 0:NE], v3(sm)))
                    prev()
                    step(dve.tensor_tensor(out=gg[:, :, NE:2 * NE], in0=v3(sm), in1=gg[:, :, 0:NE].bitcast(f32),
                                           op=ALU.subtract))
                assert k[0] == (5, 9, K_RD)[third]

            def lo(c, T, w):
                wait(dve, hidden_rounded, CH * T + CH + c + 1)
                wait(dve, layer2_done, CH * T + CH + c - LAG + 1)
                dve.tensor_tensor(out=hlo[:, c % LAG, 0:w], in0=hbuf[:, c % 2, 0:w],
                                  in1=hh[:, c % LAG, 0:w].bitcast(f32),
                                  op=ALU.subtract).then_inc(hidden_rest, 1)

            def split_dve(T, kind):
                wait(dve, x_rounded, T + 1)
                src, dst = tile_x(T, kind), tile_buf(xl, kind)
                for h in range(DH):
                    last = dve.tensor_tensor(out=dst[:, h], in0=src[:, h],
                                             in1=tile_buf(xh, kind)[:, h].bitcast(f32), op=ALU.subtract)
                last.then_inc(x_rest, 1)

            def moe_dve(c, T, kind, nxt, between=None, half=None):
                w = width(half)
                if c == SHC - 1 and half != 1:
                    wait(dve, gates_turned, T + 1)
                    dve.tensor_copy(gT[:, :], PS[0:2 * NE, G, :]).then_inc(gates_kept, 1)
                if c > 0:
                    lo(c - 1, T, w)
                wait(dve, act_ready, CH * T + CH + c + 1)
                if c < SHC:
                    wait(dve, layer1_done, GRP + GRP * T + 2 * c + 2)
                    dve.scalar_tensor_tensor(out=hbuf[:, c % 2, 0:w], in0=act_g[:, c % 2, 0:w], scalar=1.0 / NSH,
                                             in1=PS[:, ROT[(2 * c + 1) % 4], 0:w], op0=ALU.mult, op1=ALU.mult)\
                       .then_inc(hidden_gated, 1)
                else:
                    wait(dve, gates_spread, NE * T + (c - SHC) // 2 + 1)
                    dve.tensor_tensor(out=hbuf[:, c % 2, 0:w], in0=act_g[:, c % 2, 0:w],
                                      in1=PS[:, GATE[(c - SHC) // 2 % 2], 0:w],
                                      op=ALU.mult).then_inc(hidden_gated, 1)
                if between and c < CH - 1:
                    between()
                if c == ROUTER_AT - 1 and half != 1:
                    router_logits(T, kind)
                if ROUTER_AT + 1 <= c <= ROUTER_AT + 3 and half != 1:
                    router_dve(T, c - ROUTER_AT - 1)
                if c == CH - 1:
                    lo(c, T, w)
                    if nxt:
                        split_dve(T + 1, nxt)
                    if between:
                        between()
                    wait(dve, layer2_done, CH * T + CH + CH)
                    for m in range(DH):
                        o = PS[:, O[m], 0:w]
                        if half is None:
                            xs = tile_x(T, kind)[:, m]
                        else:
                            xs = xv[:, m, HALF:B, L - TH + half * TH // 2:L - TH + (half + 1) * TH // 2]
                        if kind == "B":
                            o = o.rearrange("p (b t) -> p b t", t=TH if half is None else TH // 2)
                        dve.scalar_tensor_tensor(out=xs, in0=o, scalar=0.25, in1=xs,
                                                 op0=ALU.mult, op1=ALU.add).then_inc(x_after_l2, 1)

            def rec_dve(r, J, u):
                z4 = z4s[:, u]
                if 1 <= r <= 4:
                    t = r - 1
                    wait(dve, step_tanh, 4 * J + t + 1)
                    dve.scalar_tensor_tensor(out=uz[:, :, :], in0=th[:, :, :], scalar=1.0, in1=z4[:, :, t, :],
                                             op0=ALU.add, op1=ALU.mult).then_inc(step_gated, 1)
                    wait(dve, step_gated, 4 * J + t + 1)
                    wait(dve, state_leaked, 4 * J + t + 1)
                    dve.scalar_tensor_tensor(out=uz[:, :, :], in0=uz[:, :, :], scalar=0.5, in1=hl[:, :, :],
                                             op0=ALU.mult, op1=ALU.add).then_inc(step_sum, 1)

            def front_slot(c, F0):
                front_dve(c % 6, F0 + c // 6)
                if c == 6:
                    front_dve(6, F0)
                if c == 11:
                    front_dve(6, F0 + 1)

            def fronts(c, F0, n=4):
                for r, f in fronts_at(c, n)[::-1]:
                    if (r, c) == (5, CH - 2):
                        continue
                    if (r, c) == (6, CH - 1):
                        front_dve(5, F0 + f)
                    front_dve(r, F0 + f)

            for t in range(NT):
                jobs, slots = beside_l0(t), l0_slots(t)
                l0_dve(t, t % 2, jobs[0])
                for c in slots[:2]:
                    front_slot(c, 0)
                for job in jobs[1:]:
                    evacuate(job)
                for c in slots[2:]:
                    front_slot(c, 0)
            l0_x(NT - 1)
            split_dve(0, "A")
            dve.tensor_tensor(out=esel[:, :, :], in0=ident[0:2 * NE, 0:NE].unsqueeze(2).broadcast_to([2 * NE, NE, P]),
                              in1=ident[0:2 * NE, NE:2 * NE].unsqueeze(2).broadcast_to([2 * NE, NE, P]),
                              op=ALU.add).then_inc(selectors_ready, 1)
            with dve.Fori(0, NT // 2 - 1) as i:
                for c in range(CH):
                    moe_dve(c, i, "A", "A", lambda: fronts(c, 2 + 4 * i))
            for c in range(CH):
                moe_dve(c, NT // 2 - 1, "A", "B", lambda: fronts(c, NF - 2, 2))
            for c in range(CH):
                if c == 1:
                    dve.tensor_copy(hid[:, :, :], condT[:, :, :]).then_inc(state_ready, 1)
                moe_dve(c, NT // 2, "B", "B")

            def rec_tile(k, nxt, half=None):
                def recurrence(c):
                    for r, J, u in rec_at(c, k, half):
                        rec_dve(r, J, u)

                for c in range(CH):
                    moe_dve(c, NT // 2 + 1 + k + (half or 0), "B", nxt, lambda: recurrence(c), half)

            with dve.Fori(0, NT // 2 - 2) as k:
                rec_tile(k, "B")
            for half in range(2):
                rec_tile(NT // 2 - 2, None, half)

            def tail_split(b):
                dve.wait_ge(last_z_rounded, b + 1)
                q = slice(NQ * b, NQ * (b + 1))
                for h in range(DH):
                    last = dve.tensor_tensor(out=ztl[:, h, q, :], in0=tail_z(b)[:, h, :, :],
                                             in1=zth[:, h, q, :].bitcast(f32), op=ALU.subtract)
                last.then_inc(last_z_rest, 1)

            tail_split(0)
            for b in range(NTAIL):
                for t in range(NQ):
                    s = NQ * b + t
                    for m in range(DH):
                        dve.wait_ge(last_tanh, DH * s + m + 1)
                        dve.scalar_tensor_tensor(out=uz[:, m, :], in0=th[:, m, :], scalar=1.0,
                                                 in1=tail_z(b)[:, m, t, :], op0=ALU.add, op1=ALU.mult)\
                           .then_inc(last_gated, 1)
                    dve.wait_ge(last_gated, DH * (s + 1))
                    dve.wait_ge(state_leaked, S_TAIL + s + 1)
                    dve.scalar_tensor_tensor(out=uz[:, :, :], in0=uz[:, :, :], scalar=0.5, in1=hl[:, :, :],
                                             op0=ALU.mult, op1=ALU.add).then_inc(step_sum, 1)
                    if t == 0 and b + 1 < NTAIL:
                        tail_split(b + 1)
            dve.wait_ge(state_ready, L + 1)
            tail_row(dve, NTAIL * NQ - 1)

        @block.tensor
        def _(pe):
            pe.sem_inc(l0_product, 4)
            pe.sem_inc(layer2_done, CH)
            pe.sem_inc(layer1_done, GRP)
            pe.sem_inc(router_product, 1)
            pe.sem_inc(z_product, 1)
            pe.sem_inc(rows_turned, 1)

            def free_bank(job):
                kind, j = job
                if kind == "conv":
                    same = [("conv", j - 4)] if j >= 4 else []
                else:
                    n = BANKED.index(job)
                    same = [BANKED[n - 4]] if n >= 4 else []
                    if job in late:
                        i = late.index(job)
                        same = [late[i - 2 if i <= 12 else i - 1]] if i >= 2 else []
                for old in same:
                    if finisher(old) == "A":
                        pe.wait_ge(s_av, A_AT[old])
                    else:
                        pe.wait_ge(s_dv, D_AT[old])

            def split3(o, wh, wl, bh, bl, first, last, **kw):
                pe.matmul(o, wh, bh, start=first, stop=False, **kw)
                pe.matmul(o, wh, bl, start=False, stop=False, **kw)
                return pe.matmul(o, wl, bh, start=False, stop=last, **kw)

            waited = set()

            def once(s, name, v):
                if name not in waited:
                    waited.add(name)
                    pe.wait_ge(s, v)

            def setup_pe(job):
                kind, j = job
                free_bank(job)
                if kind == "conv":
                    once(s_in["t"], "t", 64)
                    once(s_tz, "tz", DH)
                    for c in range(8):
                        ch = 8 * j + c
                        for h in range(DH):
                            q = slice(h * L, (h + 1) * L)
                            last = pe.matmul(PS[q, j % 4, c * B:(c + 1) * B], Tz[q, :, ch], Xs[q, :, ch],
                                             start=True, stop=True)
                    last.then_inc(s_cv, 1)
                    return
                n = BANKED.index(job)
                b = PS[:, bank_of(n), :]
                if kind == "rows":
                    once(s_in["rows"], "rows", 16 * 12)
                    last = pe.transpose(b[:, 0:19], rows[:, :], ident[0:19, 0:19])
                elif kind == "cond":
                    once(s_in["cond"], "cond", 16)
                    for h in range(DH):
                        last = pe.transpose(b[:, h * B:(h + 1) * B], condN[:, h * P:(h + 1) * P], ident[0:B, 0:B])
                elif kind == "rtr":
                    once(s_in["wr"], "wr", 16)
                    for k in range(4):
                        last = pe.transpose(b[:, k * NE:(k + 1) * NE], wrN[:, k * P:(k + 1) * P], ident[0:NE, 0:NE])
                elif kind == "cl":
                    pe.wait_ge(s_dv, D_AT[("rtr", 0)])
                    for k in range(DH):
                        last = pe.matmul(PS[0:B, bank_of(n), 0:NE], condT[:, k, :], wrt[:, k, :],
                                         start=k == 0, stop=k == DH - 1)
                elif kind == "te":
                    pe.wait_ge(s_dv, D_AT[("cl", 0)])
                    pe.wait_ge(s_cst, NCST)
                    for g in range(4 * (NT // 2 + 1)):
                        last = pe.matmul(b[:, 2 * g * NE:2 * (g + 1) * NE], sel[:, g * P:(g + 1) * P],
                                         cl[:, :, :].rearrange("b s e -> b (s e)"), start=True, stop=True)
                elif kind == "bpe":
                    once(s_in["l0"], "l0", 16 * 5)
                    for q in range(2):
                        for th_ in range(2):
                            for k in range(DH):
                                last = pe.matmul(b[:, q:q + 1], wq[:, k, q, (1 - th_) * N:(1 - th_) * N + P],
                                                 cols[:, 5 + k:6 + k], start=th_ == 0 and k == 0,
                                                 stop=th_ == 1 and k == DH - 1)
                elif kind in ("x", "ct"):
                    if kind == "x":
                        once(s_cst, "ident", IDENT)
                        once(s_inx[j // 4], f"x{j // 4}", 32)
                    else:
                        once(s_av, "cvA", A_AT[("conv", 14)])
                        once(s_dv, "cvD", D_AT[("conv", 15)])
                    for i in range(4):
                        bt = 4 * j + i
                        src = Xs[:, bt, :] if kind == "x" else convS[:, :, bt]
                        last = pe.transpose(b[:, i * P:(i + 1) * P], src, ident[:, :])
                elif kind == "w":
                    k, half = j
                    if half == 0:
                        cnt = 16 * sum(len(STAGES[q][2]) for q in range(k % 2, k + 1, 2))
                        pe.wait_ge(s_stg[k % 2], cnt)
                    v = stage_view(k)
                    for i, (r, kc) in enumerate(stage_blocks(k, half)):
                        last = pe.transpose(b[:, i * P:(i + 1) * P], v[:, r, kc * P:(kc + 1) * P], ident[:, :])
                last.then_inc(s_tp, 1)

            for job in ORDER[:N_EARLY]:
                setup_pe(job)

            def l0_proj(t, p):
                def rhs(q, k, th_):
                    o = th_ * FT
                    return convT[:, t, k, o:o + FT] if q < 2 else xT[:, k, t * TILE + o:t * TILE + o + FT]

                wait(pe, bc_ready, 2 * t + 2)
                for q in range(3):
                    if q == 2:
                        wait(pe, l0_chain, 5 * t + 3)
                    o = PS[:, p + 2 * (q // 2), (q % 2) * FT:(q % 2) * FT + FT]
                    n = 0
                    for k in range(DH):
                        for th_ in range(2):
                            n += 1
                            last = pe.matmul(o, wq[:, k, q, (1 - th_) * N:(1 - th_) * N + P],
                                             rhs(q, k, th_), start=n == 1, stop=n == 4)
                    if q:
                        last.then_inc(proj_done, 1)

            def l0_out(t, p):
                wait(pe, l0_chain, 10 + 5 * t + 5)
                wait(pe, x_after_l0, 4 + 2 * t)
                for m in range(DH):
                    for th_ in range(2):
                        last = pe.matmul(PS[:, LO[m], th_ * FT:(th_ + 1) * FT],
                                         wo2[:, th_, m * P:(m + 1) * P], ys[:, p, :], start=True, stop=True)
                    last.then_inc(l0_product, 1)

            def front_pe(r, F):
                if r in (1, 2, 3):
                    q = r - 1
                    if q == 0:
                        wait(pe, x1_rounded, F + 1)
                        wait(pe, x1_rest, F + 1)
                    wait(pe, gate_inputs, 3 * F + q)
                    for m in range(DH):
                        w = slice(q * D + m * P, q * D + (m + 1) * P)
                        for k in range(DH):
                            last = split3(PS[:, FL, m * FT:(m + 1) * FT], w1h[:, k, w], w1l[:, k, w],
                                          x1h[:, k, :], x1l[:, k, :], k == 0, k == DH - 1)
                    last.then_inc(gate_products, 1)

            def router_pe(T):
                wait(pe, hidden_gated, CH * T + CH - 2)
                for g in range(4):
                    o = 2 * NE * g
                    q = slice(g * P, (g + 1) * P)
                    for k in range(DH):
                        pe.matmul(PS[:, G, o:o + 2 * NE], xh[:, k, q], wr2[:, k, :, :].rearrange("p s e -> p (s e)"),
                                  start=k == 0, stop=False, skip_group_check=True)
                        last = pe.matmul(PS[:, G, o:o + NE], xl[:, k, q], wr2[:, k, 0, :], start=False,
                                         stop=k == DH - 1, skip_group_check=True)
                last.then_inc(router_product, 1)

            def layer1(bank, wh, wl, w, half):
                for k in range(DH):
                    last = split3(PS[:, bank, 0:width(half)], wh[:, k, w], wl[:, k, w], part(xh[:, k, :], half),
                                  part(xl[:, k, :], half), k == 0, k == DH - 1)
                last.then_inc(layer1_done, 1)

            def w2(c, T, n):
                wait(pe, hidden_rest, CH * T + CH + c + 1)
                if c == 0:
                    wait(pe, x_after_l2, 2 * T + 2)
                for m in range(DH):
                    w = slice(m * P, (m + 1) * P)
                    last = split3(PS[:, O[m], 0:n], w2h[:, c, w], w2l[:, c, w], hh[:, c % LAG, 0:n],
                                  hlo[:, c % LAG, 0:n],
                                  c == 0, c == CH - 1, skip_group_check=True)
                last.then_inc(layer2_done, 1)

            def moe_pe(c, T, half=None):
                n = width(half)
                if c == 0 and half != 1:
                    wait(pe, x_rounded, T + 1)
                    wait(pe, x_rest, T + 1)
                if c < SHC:
                    wait(pe, act_ready, CH * T + CH + max(c - 1, 0))
                    layer1(ROT[(2 * c) % 4], w13h, w13l, slice(c * P, (c + 1) * P), half)
                    if c:
                        wait(pe, hidden_gated, CH * T + CH + c - 1)
                    layer1(ROT[(2 * c + 1) % 4], w13h, w13l, slice((SHC + c) * P, (SHC + c + 1) * P), half)
                else:
                    g = c - SHC
                    if g == 1:
                        wait(pe, hidden_gated, CH * T + CH + SHC - 1)
                    else:
                        wait(pe, act_ready, CH * T + CH + (SHC - 1, 0, SHC)[g] if g < 3 else CH * T + CH + c - 2)
                    layer1(ROT[g % 3], rw1h, rw1l, slice(g * P, (g + 1) * P), half)
                if c == 0 and half != 1:
                    router_pe(T)
                if c == SHC - 1 and half != 1:
                    wait(pe, router_step, 14 * T + 14)
                    for g in range(4):
                        last = pe.transpose(PS[0:2 * NE, G, g * P:(g + 1) * P], gg[:, g, :].bitcast(f32), ident[:, :])
                    last.then_inc(gates_turned, 1)
                if c >= LAG:
                    w2(c - LAG, T, n)
                if c >= SHC and (c - SHC) % 2 == 0:
                    e = (c - SHC) // 2
                    if e == 0 and half != 1:
                        wait(pe, selectors_ready, 1)
                        wait(pe, gates_kept, T + 1)
                    wait(pe, hidden_gated, CH * T + CH + c - 2)
                    pe.matmul(PS[:, GATE[e % 2], 0:n], esel[:, e, :], part(gT[:, :], half), start=True,
                              stop=True).then_inc(gates_spread, 1)
                if c == CH - 1:
                    for q in range(CH - LAG, CH):
                        w2(q, T, n)

            def rec_pe(r, J):
                if r == 0:
                    wait(pe, z_rest, J + 1)
                    wait(pe, z_rounded, J + 1)
                    if isinstance(J, int) and J > KEPT:
                        wait(pe, state_ready, 4 * J + 1)
                    else:
                        wait(pe, rows_staged, 1 + J)
                    for m in range(DH):
                        w = slice(m * P, (m + 1) * P)
                        for k in range(DH):
                            z_h = z4h[:, k, :, :].rearrange("p t b -> p (t b)")
                            z_l = z4l[:, k, :, :].rearrange("p t b -> p (t b)")
                            last = split3(PS[:, FL, m * FT:(m + 1) * FT], wzh[:, k, w], wzl[:, k, w], z_h, z_l,
                                          m == 0 and k == 0, False, skip_group_check=True)
                    last.then_inc(z_product, 1)
                if 1 <= r <= 4:
                    t = r - 1
                    wait(pe, state_ready, 4 * J + t + 1)
                    for m in range(DH):
                        for k in range(DH):
                            last = pe.matmul(PS[:, FL, m * FT + t * B:m * FT + (t + 1) * B],
                                             whT[:, k, m * P:(m + 1) * P], hid[:, k, :], start=False,
                                             stop=t == NQ - 1, skip_group_check=True)
                    last.then_inc(step_product, 1)
                if r == 5:
                    wait(pe, row_added, 2 * NQ + 4 * J + 4)
                    for j in range(2):
                        for m in range(DH):
                            src = o4[:, m, 2 * j:2 * j + 2, :].rearrange("p t b -> p (t b)")
                            last = pe.transpose(PS[:, FL, j * D + m * P:j * D + (m + 1) * P], src, ident[:, :])
                    last.then_inc(rows_turned, 1)

            pe.wait_ge(s_av, A_AT[LAST_EARLY])
            pe.wait_ge(s_dv, D_AT[LAST_EARLY])
            for t in range(NT):
                l0_proj(t, t % 2)
                jobs = beside_l0(t)
                setup_pe(jobs[0])
                slots = l0_slots(t)
                if t == 4:
                    pe.wait_ge(s_dv, D_AT[late[11]])
                for c in slots[:1]:
                    front_pe(c % 6, c // 6)
                if t:
                    l0_out(t - 1, 1 - t % 2)
                for c in slots[1:2]:
                    front_pe(c % 6, c // 6)
                for job in jobs[1:]:
                    setup_pe(job)
                for c in slots[2:]:
                    front_pe(c % 6, c // 6)
            l0_out(NT - 1, (NT - 1) % 2)
            pe.wait_ge(s_av, A_AT[ORDER[-1]])
            pe.wait_ge(s_dv, D_AT[ORDER[-1]])
            pe.wait_ge(x_after_l0, 4 + 2 * NT)
            with pe.Fori(0, NT // 2 - 1) as i:
                for c in range(CH):
                    moe_pe(c, i)
                    for r, f in fronts_at(c):
                        front_pe(r, 2 + 4 * i + f)
            for c in range(CH):
                moe_pe(c, NT // 2 - 1)
                for r, f in fronts_at(c, 2):
                    front_pe(r, NF - 2 + f)
            for c in range(CH):
                moe_pe(c, NT // 2)

            def rec_tile(k, half=None):
                for c in range(CH):
                    moe_pe(c, NT // 2 + 1 + k + (half or 0), half)
                    for r, J, _ in rec_at(c, k, half):
                        if r == 1:
                            rec_pe(0, J)
                        if r:
                            rec_pe(r, J)

            with pe.Fori(0, NT // 2 - 2) as k:
                rec_tile(k)
            for half in range(2):
                rec_tile(NT // 2 - 2, half)

            def tail_z_product(b):
                pe.wait_ge(last_z_rest, b + 1)
                q = slice(NQ * b, NQ * (b + 1))
                for m in range(DH):
                    w = slice(m * P, (m + 1) * P)
                    for k in range(DH):
                        z_h = zth[:, k, q, :].rearrange("p t b -> p (t b)")
                        z_l = ztl[:, k, q, :].rearrange("p t b -> p (t b)")
                        split3(PS[:, ROT[2 * (b % 2) + m], 0:FT], wzh[:, k, w], wzl[:, k, w], z_h, z_l,
                               k == 0, False, skip_group_check=True)

            def tail_transposes(b):
                pe.wait_ge(row_added, 2 * NQ + NQ * (KEPT + b + 1))
                if b >= 2:
                    pe.wait_ge(last_staged, b - 1)
                for j in range(2):
                    for m in range(DH):
                        rows_, n = (oh, b) if b < N_OUT - NTAIL else (ot, b - (N_OUT - NTAIL))
                        src = rows_[:, m, NQ * n + 2 * j:NQ * n + 2 * j + 2, :].rearrange("p t b -> p (t b)")
                        last = pe.transpose(PS[:, TR[b % 2], j * D + m * P:j * D + (m + 1) * P], src, ident[:, :])
                last.then_inc(last_turned, 1)

            tail_z_product(0)
            for b in range(NTAIL):
                for t in range(NQ):
                    pe.wait_ge(state_ready, S_TAIL + NQ * b + t + 1)
                    for m in range(DH):
                        for k in range(DH):
                            last = pe.matmul(PS[:, ROT[2 * (b % 2) + m], t * B:(t + 1) * B],
                                             whT[:, k, m * P:(m + 1) * P], hid[:, k, :], start=False,
                                             stop=t == NQ - 1, skip_group_check=True)
                        last.then_inc(last_product, 1)
                    if NQ * b + t in ROWS_AT:
                        tail_transposes(ROWS_AT[NQ * b + t])
                    if t == 2 and b + 1 < NTAIL:
                        tail_z_product(b + 1)
            tail_transposes(N_OUT - 1)


_INS = ['x', 'cond_1024', 'L0_cond_conv_b', 'L0_cond_Wp', 'L0_cond_bp', 'L0_cond_Ws', 'L0_cond_bs', 'L0_cond_A_log',
        'L0_cond_dt_log', 'L0_cond_Wo', 'L0_cond_bo', 'L1_cond_W_f', 'L1_cond_b_f', 'L1_cond_W_i', 'L1_cond_b_i',
        'L1_cond_W_h', 'L1_cond_b_h', 'L2_cond_W_router', 'L2_cond_router_bias', 'L2_cond_s_w1', 'L2_cond_s_w3',
        'L2_cond_s_w2', 'L2_cond_r_w1', 'L2_cond_r_w2', 'L3_cond_W', 'L3_cond_b', 'L3_cond_alpha']


def kernel(**inputs):
    import numpy as _np
    import concourse.bacc as _bacc
    from concourse import mybir as _mybir
    from concourse.bass_utils import run_bass_kernel_spmd as _run

    nc = _bacc.Bacc("TRN2", target_bir_lowering=False, num_devices=1, dynamic_dma_scratch_size=1024)
    arrays, args = {}, []
    for name in _INS:
        a = _np.ascontiguousarray(inputs[name])
        arrays[f"in_{name}_dram"] = a
        args.append(nc.dram_tensor(f"in_{name}_dram", a.shape, _mybir.dt.from_np(a.dtype), kind="ExternalInput").ap())
    args.append(nc.dram_tensor("out_0_dram", (B, L, D), _mybir.dt.float32, kind="ExternalOutput").ap())
    layered_blocks_kernel(nc, *args)
    r = _run(nc, [arrays], core_ids=[0])
    return r.results[0]["out_0_dram"]
```
